# Optimizing a Trainium2 kernel written in Bass

```python
import numpy as np
import jax
import jax.numpy as jnp

def _softmax(x, axis=-1):
    return jax.nn.softmax(x, axis=axis)

def _gelu(x):
    return jax.nn.gelu(x, approximate=True)

def _silu(x):
    return jax.nn.silu(x)

def _sigmoid(x):
    return jax.nn.sigmoid(x)

def _layernorm(x, axis=-1, eps=1e-05):
    m = jnp.mean(x, axis=axis, keepdims=True)
    v = jnp.var(x, axis=axis, keepdims=True)
    return (x - m) / jnp.sqrt(v + eps)

def _scatter_add(tgt, idx, src, axis=0):
    return tgt.at[idx].add(src)

def _segment_sum(src, seg, n):
    return jax.ops.segment_sum(src, seg, n)
kernel_name = 'mk_gnn_ffn_d4_gnn_r8_32a928'

def setup_inputs(seed: int=0):
    np.random.seed(seed)
    _w = jnp.asarray

    def _rec_inputs():
        import jax
        import jax.numpy as jnp
        _gk = jax.random.key(seed)
        x = -0.001003 + 1 * jax.random.normal(jax.random.fold_in(_gk, 1), (256, 768), jnp.float32)
        src = jax.random.randint(jax.random.fold_in(_gk, 2), (4096,), 0, 256, jnp.int32)
        dst = jax.random.randint(jax.random.fold_in(_gk, 3), (4096,), 0, 256, jnp.int32)
        _o = jnp.argsort(dst, stable=True)
        src = src[_o]
        dst = dst[_o]
        edge_type_3 = jax.random.randint(jax.random.fold_in(_gk, 13), (4096,), 0, 3, jnp.int32)
        return (x, src, dst, edge_type_3)
    x, src, dst, edge_type_3 = _rec_inputs()

    def _L0_gnn_setup():
        import jax, jax.numpy as jnp
        import numpy as np
        NUM_RELATIONS = 3

        def _rgcn(x, W_rel, W_root, bias, src, dst, etype):
            n = x.shape[0]
            xr = jnp.einsum('ni,rio->rno', x, W_rel)
            msg = xr[etype, src]
            out = x @ W_root + bias
            for r in range(NUM_RELATIONS):
                m = etype == r
                s = jax.ops.segment_sum(jnp.where(m[:, None], msg, 0.0), dst, num_segments=n)
                c = jax.ops.segment_sum(m.astype(x.dtype), dst, num_segments=n)
                out = out + s / jnp.maximum(c, 1.0)[:, None]
            return out

        def _gate(h, q, Wg, bg, Wq, bq):
            B, L, F = q.shape
            N = h.shape[0] // B
            h3 = h.reshape(B, N, F)
            hg = jnp.einsum('bnf,gf->bng', h3, Wg[:, :F])
            qg = jnp.einsum('blf,gf->blg', q, Wg[:, F:]) + bg
            attn = jax.nn.sigmoid(hg[:, :, None, :] + qg[:, None, :, :])
            qi = jnp.einsum('bnlf,blf->bnf', attn, q)
            alpha = jax.nn.sigmoid(jnp.einsum('bnf,gf->bng', h3, Wq[:, :F]) + jnp.einsum('bnf,gf->bng', qi, Wq[:, F:]) + bq)
            hn = alpha * jnp.tanh(qi) + (1.0 - alpha) * h3
            return hn.reshape(B * N, F)
        key = jax.random.key(seed)
        ks = jax.random.split(key, 16)
        F = 768
        BN, E, B, L = (256, 8192, 8, 64)
        s = 0.02
        return {'x': jax.random.normal(ks[0], (BN, F), jnp.float32), 'edge_index': jax.random.randint(ks[1], (2, E), 0, BN), 'edge_type': jax.random.randint(ks[2], (E,), 0, NUM_RELATIONS), 'query_embs': jax.random.normal(ks[3], (B, L, F), jnp.float32), 'W_rel1': jax.random.normal(ks[4], (NUM_RELATIONS, F, F), jnp.float32) * s, 'W_root1': jax.random.normal(ks[5], (F, F), jnp.float32) * s, 'b1': jnp.zeros((F,), jnp.float32), 'W_rel2': jax.random.normal(ks[6], (NUM_RELATIONS, F, F), jnp.float32) * s, 'W_root2': jax.random.normal(ks[7], (F, F), jnp.float32) * s, 'b2': jnp.zeros((F,), jnp.float32), 'Wg': jax.random.normal(ks[8], (F, 2 * F), jnp.float32) * s, 'bg': jnp.zeros((F,), jnp.float32), 'Wq': jax.random.normal(ks[9], (F, 2 * F), jnp.float32) * s, 'bq': jnp.zeros((F,), jnp.float32)}
    _L0_gnn_all = _L0_gnn_setup()
    _L0_gnn_in = {k: v for k, v in _L0_gnn_all.items() if k in ('query_embs', 'W_rel1', 'W_root1', 'b1', 'W_rel2', 'W_root2', 'b2', 'Wg', 'bg', 'Wq', 'bq')}
    del _L0_gnn_all

    def _L0_ffn_setup():
        import jax, jax.numpy as jnp
        import numpy as np
        B, L, D, H, F = (4, 256, 768, 12, 384)
        ROUTE_FRAC = 0.15
        LN_EPS = 1e-05

        def _ln(x, g, b):
            m = jnp.mean(x, axis=-1, keepdims=True)
            v = jnp.mean((x - m) ** 2, axis=-1, keepdims=True)
            return (x - m) * jax.lax.rsqrt(v + LN_EPS) * g + b
        key = jax.random.key(seed)
        ks = jax.random.split(key, 20)
        s = 0.02
        return {'hidden_states': jax.random.normal(ks[0], (B, L, D), dtype=jnp.float32), 'g1': jnp.ones((D,), jnp.float32), 'b1': jnp.zeros((D,), jnp.float32), 'g2': jnp.ones((D,), jnp.float32), 'b2': jnp.zeros((D,), jnp.float32), 'Wr': jax.random.normal(ks[1], (D,), jnp.float32) * s, 'br': jnp.zeros((), jnp.float32), 'Wq': jax.random.normal(ks[2], (D, D), jnp.float32) * s, 'bq': jnp.zeros((D,), jnp.float32), 'Wk': jax.random.normal(ks[3], (D, D), jnp.float32) * s, 'bk': jnp.zeros((D,), jnp.float32), 'Wv': jax.random.normal(ks[4], (D, D), jnp.float32) * s, 'bv': jnp.zeros((D,), jnp.float32), 'Wo': jax.random.normal(ks[5], (D, D), jnp.float32) * s, 'bo': jnp.zeros((D,), jnp.float32), 'Wm': jax.random.normal(ks[6], (D, D), jnp.float32) * s, 'bm': jnp.zeros((D,), jnp.float32), 'W1': jax.random.normal(ks[7], (D, F), jnp.float32) * s, 'bf1': jnp.zeros((F,), jnp.float32), 'W2': jax.random.normal(ks[8], (F, D), jnp.float32) * s, 'bf2': jnp.zeros((D,), jnp.float32)}
    _L0_ffn_all = _L0_ffn_setup()
    _L0_ffn_in = {k: v for k, v in _L0_ffn_all.items() if k in ('g1', 'b1', 'g2', 'b2', 'Wr', 'br', 'Wq', 'bq', 'Wk', 'bk', 'Wv', 'bv', 'Wo', 'bo', 'Wm', 'bm', 'W1', 'bf1', 'W2', 'bf2')}
    del _L0_ffn_all

    def _L1_gnn_setup():
        import jax, jax.numpy as jnp
        import numpy as np
        N_NODES = 2500
        N_EDGES = 20000
        IN_DIM = 768
        HID = 256
        HEADS = 4
        OUT_DIM = 768
        LN_EPS = 1e-05

        def _add_self_loops(edge_index, n):
            loop = jnp.arange(n, dtype=edge_index.dtype)
            return jnp.concatenate([edge_index, jnp.stack([loop, loop])], axis=1)

        def gat_conv(x, edge_index, W, a_src, a_dst, bias, heads, out_ch, concat):
            n = x.shape[0]
            ei = _add_self_loops(edge_index, n)
            src, dst = (ei[0], ei[1])
            xl = (x @ W).reshape(n, heads, out_ch)
            alpha_src = jnp.einsum('nhc,hc->nh', xl, a_src)
            alpha_dst = jnp.einsum('nhc,hc->nh', xl, a_dst)
            e = jax.nn.leaky_relu(alpha_src[src] + alpha_dst[dst], 0.2)
            m = jax.ops.segment_max(e, dst, num_segments=n)
            e = jnp.exp(e - m[dst])
            s = jax.ops.segment_sum(e, dst, num_segments=n)
            alpha = e / (s[dst] + 1e-16)
            msg = xl[src] * alpha[:, :, None]
            out = jax.ops.segment_sum(msg, dst, num_segments=n)
            out = out.reshape(n, heads * out_ch) if concat else out.mean(axis=1)
            return out + bias

        def layer_norm(x, g, b):
            mu = jnp.mean(x, axis=-1, keepdims=True)
            var = jnp.var(x, axis=-1, keepdims=True)
            return (x - mu) * jax.lax.rsqrt(var + LN_EPS) * g + b
        key = jax.random.key(seed)
        ks = jax.random.split(key, 16)
        s = 0.02
        HC = HID * HEADS
        return {'x': jax.random.normal(ks[0], (N_NODES, IN_DIM), jnp.float32), 'edge_index': jax.random.randint(ks[1], (2, N_EDGES), 0, N_NODES, jnp.int64 if jax.config.jax_enable_x64 else jnp.int32), 'W1': jax.random.normal(ks[2], (IN_DIM, HC), jnp.float32) * s, 'a_src1': jax.random.normal(ks[3], (HEADS, HID), jnp.float32) * s, 'a_dst1': jax.random.normal(ks[4], (HEADS, HID), jnp.float32) * s, 'b1': jnp.zeros((HC,), jnp.float32), 'g1': jnp.ones((HC,), jnp.float32), 'be1': jnp.zeros((HC,), jnp.float32), 'Wr1': jax.random.normal(ks[5], (IN_DIM, HC), jnp.float32) * s, 'br1': jnp.zeros((HC,), jnp.float32), 'W2': jax.random.normal(ks[6], (HC, OUT_DIM), jnp.float32) * s, 'a_src2': jax.random.normal(ks[7], (1, OUT_DIM), jnp.float32) * s, 'a_dst2': jax.random.normal(ks[8], (1, OUT_DIM), jnp.float32) * s, 'b2': jnp.zeros((OUT_DIM,), jnp.float32), 'g2': jnp.ones((OUT_DIM,), jnp.float32), 'be2': jnp.zeros((OUT_DIM,), jnp.float32), 'Wr2': jax.random.normal(ks[9], (HC, OUT_DIM), jnp.float32) * s, 'br2': jnp.zeros((OUT_DIM,), jnp.float32)}
    _L1_gnn_all = _L1_gnn_setup()
    _L1_gnn_in = {k: v for k, v in _L1_gnn_all.items() if k in ('W1', 'a_src1', 'a_dst1', 'b1', 'g1', 'be1', 'Wr1', 'br1', 'W2', 'a_src2', 'a_dst2', 'b2', 'g2', 'be2', 'Wr2', 'br2')}
    del _L1_gnn_all

    def _L1_ffn_setup():
        import jax, jax.numpy as jnp
        import numpy as np
        B, S, H, F, E, TOP_K = (4, 256, 768, 384, 8, 2)
        key = jax.random.key(seed)
        ks = jax.random.split(key, 6)
        x = jax.random.normal(ks[0], (B, S, H), dtype=jnp.float32)
        Wr = jax.random.normal(ks[1], (E, H), dtype=jnp.float32) * 0.02
        Wi = jax.random.normal(ks[2], (E, F, H), dtype=jnp.float32) * 0.02
        bi = jnp.zeros((E, F), dtype=jnp.float32)
        Wo = jax.random.normal(ks[3], (E, H, F), dtype=jnp.float32) * 0.02
        bo = jnp.zeros((E, H), dtype=jnp.float32)
        return {'x': x, 'Wr': Wr, 'Wi': Wi, 'bi': bi, 'Wo': Wo, 'bo': bo}
    _L1_ffn_all = _L1_ffn_setup()
    _L1_ffn_in = {k: v for k, v in _L1_ffn_all.items() if k in ('Wr', 'Wi', 'bi', 'Wo', 'bo')}
    del _L1_ffn_all

    def _L2_gnn_setup():
        import jax, jax.numpy as jnp
        import numpy as np
        N_NODES = 1250
        NEG_SLOPE = 0.2
        EPS = 1e-16

        def gat_layer(x, W, att_src, att_dst, bias, src, dst, heads, out_ch, concat):
            n = x.shape[0]
            h = (x @ W.T).reshape(n, heads, out_ch)
            a_src = jnp.einsum('nhc,hc->nh', h, att_src)
            a_dst = jnp.einsum('nhc,hc->nh', h, att_dst)
            e = a_src[src] + a_dst[dst]
            e = jax.nn.leaky_relu(e, NEG_SLOPE)
            m = jax.ops.segment_max(e, dst, num_segments=n)
            ex = jnp.exp(e - m[dst])
            denom = jax.ops.segment_sum(ex, dst, num_segments=n)
            alpha = ex / (denom[dst] + EPS)
            msg = alpha[:, :, None] * h[src]
            out = jax.ops.segment_sum(msg, dst, num_segments=n)
            if concat:
                out = out.reshape(n, heads * out_ch)
            else:
                out = out.mean(axis=1)
            return out + bias
        key = jax.random.key(seed)
        ks = jax.random.split(key, 12)
        x = jax.random.normal(ks[0], (N_NODES, 768), dtype=jnp.float32)
        edge_index = jax.random.randint(ks[1], (2, 20000), 0, N_NODES, dtype=jnp.int64)
        s1 = 1.0 / np.sqrt(768.0)
        W1 = jax.random.normal(ks[2], (8 * 128, 768), dtype=jnp.float32) * s1
        att_src1 = jax.random.normal(ks[3], (8, 128), dtype=jnp.float32) * (1.0 / np.sqrt(128.0))
        att_dst1 = jax.random.normal(ks[4], (8, 128), dtype=jnp.float32) * (1.0 / np.sqrt(128.0))
        b1 = jnp.zeros((8 * 128,), dtype=jnp.float32)
        s2 = 1.0 / np.sqrt(1024.0)
        W2 = jax.random.normal(ks[5], (1 * 768, 1024), dtype=jnp.float32) * s2
        att_src2 = jax.random.normal(ks[6], (1, 768), dtype=jnp.float32) * (1.0 / np.sqrt(768.0))
        att_dst2 = jax.random.normal(ks[7], (1, 768), dtype=jnp.float32) * (1.0 / np.sqrt(768.0))
        b2 = jnp.zeros((768,), dtype=jnp.float32)
        return {'x': x, 'edge_index': edge_index, 'W1': W1, 'att_src1': att_src1, 'att_dst1': att_dst1, 'b1': b1, 'W2': W2, 'att_src2': att_src2, 'att_dst2': att_dst2, 'b2': b2}
    _L2_gnn_all = _L2_gnn_setup()
    _L2_gnn_in = {k: v for k, v in _L2_gnn_all.items() if k in ('W1', 'att_src1', 'att_dst1', 'b1', 'W2', 'att_src2', 'att_dst2', 'b2')}
    del _L2_gnn_all

    def _L2_ffn_setup():
        import jax, jax.numpy as jnp
        import numpy as np
        B, S, D = (2, 1024, 768)
        I = 384
        E = 8
        G = 4
        TOPK_GROUPS = 2
        K = 2
        ROUTE_SCALE = 1.0
        ALPHA, LIMIT = (1.702, 7.0)

        def swiglu(h):
            xg = jnp.minimum(h[..., ::2], LIMIT)
            xl = jnp.clip(h[..., 1::2], -LIMIT, LIMIT)
            return xg * jax.nn.sigmoid(ALPHA * xg) * (xl + 1.0)

        def gate(x, gate_w, gate_b):
            scores = jax.nn.softmax(jnp.einsum('td,ed->te', x, gate_w).astype(jnp.float32), axis=-1)
            original_scores = scores
            s = scores + gate_b
            T = x.shape[0]
            sg = s.reshape(T, G, E // G)
            group_scores = jnp.sum(jax.lax.top_k(sg, 2)[0], axis=-1)
            _, gidx = jax.lax.top_k(group_scores, TOPK_GROUPS)
            keep = jnp.any(jax.nn.one_hot(gidx, G, dtype=jnp.bool_), axis=1)
            sg = jnp.where(keep[:, :, None], sg, -jnp.inf)
            s = sg.reshape(T, E)
            _, idx = jax.lax.top_k(s, K)
            w = jnp.take_along_axis(original_scores, idx, axis=1) * ROUTE_SCALE
            return (w.astype(x.dtype), idx)

        def expert_ffn(x, W1, B1, W3, B3, W2, B2):
            h1 = jnp.einsum('td,edh->teh', x, W1) + B1
            h3 = jnp.einsum('td,edh->teh', x, W3) + B3
            g = swiglu(h1 * h3)
            return jnp.einsum('tei,eid->ted', g, W2) + B2

        def shared_ffn(x, Ws1, Bs1, Ws3, Bs3, Ws2, Bs2):
            h = (x @ Ws1 + Bs1) * (x @ Ws3 + Bs3)
            return swiglu(h) @ Ws2 + Bs2
        key = jax.random.key(seed)
        ks = jax.random.split(key, 16)
        sc = 0.02
        inp = {'x': jax.random.normal(ks[0], (B, S, D), jnp.float32), 'gate_w': jax.random.normal(ks[1], (E, D), jnp.float32) * sc, 'gate_b': jax.random.normal(ks[2], (E,), jnp.float32) * sc, 'W1': jax.random.normal(ks[3], (E, D, 2 * I), jnp.float32) * sc, 'B1': jax.random.normal(ks[4], (E, 2 * I), jnp.float32) * sc, 'W3': jax.random.normal(ks[5], (E, D, 2 * I), jnp.float32) * sc, 'B3': jax.random.normal(ks[6], (E, 2 * I), jnp.float32) * sc, 'W2': jax.random.normal(ks[7], (E, I, D), jnp.float32) * sc, 'B2': jax.random.normal(ks[8], (E, D), jnp.float32) * sc, 'Ws1': jax.random.normal(ks[9], (D, 2 * I), jnp.float32) * sc, 'Bs1': jax.random.normal(ks[10], (2 * I,), jnp.float32) * sc, 'Ws3': jax.random.normal(ks[11], (D, 2 * I), jnp.float32) * sc, 'Bs3': jax.random.normal(ks[12], (2 * I,), jnp.float32) * sc, 'Ws2': jax.random.normal(ks[13], (I, D), jnp.float32) * sc, 'Bs2': jax.random.normal(ks[14], (D,), jnp.float32) * sc}
        return inp
    _L2_ffn_all = _L2_ffn_setup()
    _L2_ffn_in = {k: v for k, v in _L2_ffn_all.items() if k in ('gate_w', 'gate_b', 'W1', 'B1', 'W3', 'B3', 'W2', 'B2', 'Ws1', 'Bs1', 'Ws3', 'Bs3', 'Ws2', 'Bs2')}
    del _L2_ffn_all

    def _L3_gnn_setup():
        import jax, jax.numpy as jnp
        import numpy as np
        N = 2500
        DEG = 16
        E = N * DEG
        H = 12
        DIN = 64
        DOUT = 64
        NEG_SLOPE = 0.2
        key = jax.random.key(seed)
        k_h, k_src, k_w, k_al, k_ar, k_wr = jax.random.split(key, 6)
        std = 1.414 * np.sqrt(2.0 / (DIN + DOUT))
        h = jax.random.normal(k_h, (N, H * DIN), dtype=jnp.float32)
        src = jax.random.randint(k_src, (E,), 0, N, dtype=jnp.int64)
        dst = jnp.repeat(jnp.arange(N, dtype=jnp.int64), DEG)
        W = jax.random.normal(k_w, (DOUT, DIN), dtype=jnp.float32) * std
        attn_l = jax.random.normal(k_al, (1, H, DOUT), dtype=jnp.float32) * std
        attn_r = jax.random.normal(k_ar, (1, H, DOUT), dtype=jnp.float32) * std
        W_res = jax.random.normal(k_wr, (DOUT, DIN), dtype=jnp.float32) * std
        return {'h': h, 'src': src, 'dst': dst, 'W': W, 'attn_l': attn_l, 'attn_r': attn_r, 'W_res': W_res}
    _L3_gnn_all = _L3_gnn_setup()
    _L3_gnn_in = {k: v for k, v in _L3_gnn_all.items() if k in ('W', 'attn_l', 'attn_r', 'W_res')}
    del _L3_gnn_all

    def _L3_ffn_setup():
        import jax, jax.numpy as jnp
        import numpy as np
        B_SZ, S, D = (8, 512, 768)
        H = 12
        N_EXP = 8
        RANK = 16
        ALPHA = 32
        TOP_K = 2
        key = jax.random.key(seed)
        ks = jax.random.split(key, 9)
        x = jax.random.normal(ks[0], (B_SZ, S, D), jnp.float32)
        W_qkv = jax.random.normal(ks[1], (3 * D, D), jnp.float32) * 0.02
        b_qkv = jnp.zeros((3 * D,), jnp.float32)
        W_gate = jax.random.normal(ks[2], (N_EXP, D), jnp.float32) * 0.02
        b_gate = jnp.zeros((N_EXP,), jnp.float32)
        A = jax.random.normal(ks[3], (N_EXP, RANK, D), jnp.float32) * 0.02
        B_lora = jax.random.normal(ks[4], (N_EXP, 3 * D, RANK), jnp.float32) * 0.02
        W_proj = jax.random.normal(ks[5], (D, D), jnp.float32) * 0.02
        b_proj = jnp.zeros((D,), jnp.float32)
        return {'x': x, 'W_qkv': W_qkv, 'b_qkv': b_qkv, 'W_gate': W_gate, 'b_gate': b_gate, 'A': A, 'B_lora': B_lora, 'W_proj': W_proj, 'b_proj': b_proj}
    _L3_ffn_all = _L3_ffn_setup()
    _L3_ffn_in = {k: v for k, v in _L3_ffn_all.items() if k in ('W_qkv', 'b_qkv', 'W_gate', 'b_gate', 'A', 'B_lora', 'W_proj', 'b_proj')}
    del _L3_ffn_all
    return {'x': x, 'src': src, 'dst': dst, 'edge_type_3': edge_type_3, 'L0_gnn_query_embs': _L0_gnn_in['query_embs'], 'L0_gnn_W_rel1': _L0_gnn_in['W_rel1'], 'L0_gnn_W_root1': _L0_gnn_in['W_root1'], 'L0_gnn_b1': _L0_gnn_in['b1'], 'L0_gnn_W_rel2': _L0_gnn_in['W_rel2'], 'L0_gnn_W_root2': _L0_gnn_in['W_root2'], 'L0_gnn_b2': _L0_gnn_in['b2'], 'L0_gnn_Wg': _L0_gnn_in['Wg'], 'L0_gnn_bg': _L0_gnn_in['bg'], 'L0_gnn_Wq': _L0_gnn_in['Wq'], 'L0_gnn_bq': _L0_gnn_in['bq'], 'L0_ffn_g1': _L0_ffn_in['g1'], 'L0_ffn_b1': _L0_ffn_in['b1'], 'L0_ffn_g2': _L0_ffn_in['g2'], 'L0_ffn_b2': _L0_ffn_in['b2'], 'L0_ffn_Wr': _L0_ffn_in['Wr'], 'L0_ffn_br': _L0_ffn_in['br'], 'L0_ffn_Wq': _L0_ffn_in['Wq'], 'L0_ffn_bq': _L0_ffn_in['bq'], 'L0_ffn_Wk': _L0_ffn_in['Wk'], 'L0_ffn_bk': _L0_ffn_in['bk'], 'L0_ffn_Wv': _L0_ffn_in['Wv'], 'L0_ffn_bv': _L0_ffn_in['bv'], 'L0_ffn_Wo': _L0_ffn_in['Wo'], 'L0_ffn_bo': _L0_ffn_in['bo'], 'L0_ffn_Wm': _L0_ffn_in['Wm'], 'L0_ffn_bm': _L0_ffn_in['bm'], 'L0_ffn_W1': _L0_ffn_in['W1'], 'L0_ffn_bf1': _L0_ffn_in['bf1'], 'L0_ffn_W2': _L0_ffn_in['W2'], 'L0_ffn_bf2': _L0_ffn_in['bf2'], 'L1_gnn_W1': _L1_gnn_in['W1'], 'L1_gnn_a_src1': _L1_gnn_in['a_src1'], 'L1_gnn_a_dst1': _L1_gnn_in['a_dst1'], 'L1_gnn_b1': _L1_gnn_in['b1'], 'L1_gnn_g1': _L1_gnn_in['g1'], 'L1_gnn_be1': _L1_gnn_in['be1'], 'L1_gnn_Wr1': _L1_gnn_in['Wr1'], 'L1_gnn_br1': _L1_gnn_in['br1'], 'L1_gnn_W2': _L1_gnn_in['W2'], 'L1_gnn_a_src2': _L1_gnn_in['a_src2'], 'L1_gnn_a_dst2': _L1_gnn_in['a_dst2'], 'L1_gnn_b2': _L1_gnn_in['b2'], 'L1_gnn_g2': _L1_gnn_in['g2'], 'L1_gnn_be2': _L1_gnn_in['be2'], 'L1_gnn_Wr2': _L1_gnn_in['Wr2'], 'L1_gnn_br2': _L1_gnn_in['br2'], 'L1_ffn_Wr': _L1_ffn_in['Wr'], 'L1_ffn_Wi': _L1_ffn_in['Wi'], 'L1_ffn_bi': _L1_ffn_in['bi'], 'L1_ffn_Wo': _L1_ffn_in['Wo'], 'L1_ffn_bo': _L1_ffn_in['bo'], 'L2_gnn_W1': _L2_gnn_in['W1'], 'L2_gnn_att_src1': _L2_gnn_in['att_src1'], 'L2_gnn_att_dst1': _L2_gnn_in['att_dst1'], 'L2_gnn_b1': _L2_gnn_in['b1'], 'L2_gnn_W2': _L2_gnn_in['W2'], 'L2_gnn_att_src2': _L2_gnn_in['att_src2'], 'L2_gnn_att_dst2': _L2_gnn_in['att_dst2'], 'L2_gnn_b2': _L2_gnn_in['b2'], 'L2_ffn_gate_w': _L2_ffn_in['gate_w'], 'L2_ffn_gate_b': _L2_ffn_in['gate_b'], 'L2_ffn_W1': _L2_ffn_in['W1'], 'L2_ffn_B1': _L2_ffn_in['B1'], 'L2_ffn_W3': _L2_ffn_in['W3'], 'L2_ffn_B3': _L2_ffn_in['B3'], 'L2_ffn_W2': _L2_ffn_in['W2'], 'L2_ffn_B2': _L2_ffn_in['B2'], 'L2_ffn_Ws1': _L2_ffn_in['Ws1'], 'L2_ffn_Bs1': _L2_ffn_in['Bs1'], 'L2_ffn_Ws3': _L2_ffn_in['Ws3'], 'L2_ffn_Bs3': _L2_ffn_in['Bs3'], 'L2_ffn_Ws2': _L2_ffn_in['Ws2'], 'L2_ffn_Bs2': _L2_ffn_in['Bs2'], 'L3_gnn_W': _L3_gnn_in['W'], 'L3_gnn_attn_l': _L3_gnn_in['attn_l'], 'L3_gnn_attn_r': _L3_gnn_in['attn_r'], 'L3_gnn_W_res': _L3_gnn_in['W_res'], 'L3_ffn_W_qkv': _L3_ffn_in['W_qkv'], 'L3_ffn_b_qkv': _L3_ffn_in['b_qkv'], 'L3_ffn_W_gate': _L3_ffn_in['W_gate'], 'L3_ffn_b_gate': _L3_ffn_in['b_gate'], 'L3_ffn_A': _L3_ffn_in['A'], 'L3_ffn_B_lora': _L3_ffn_in['B_lora'], 'L3_ffn_W_proj': _L3_ffn_in['W_proj'], 'L3_ffn_b_proj': _L3_ffn_in['b_proj']}

def reference(x, src, dst, edge_type_3, L0_gnn_query_embs, L0_gnn_W_rel1, L0_gnn_W_root1, L0_gnn_b1, L0_gnn_W_rel2, L0_gnn_W_root2, L0_gnn_b2, L0_gnn_Wg, L0_gnn_bg, L0_gnn_Wq, L0_gnn_bq, L0_ffn_g1, L0_ffn_b1, L0_ffn_g2, L0_ffn_b2, L0_ffn_Wr, L0_ffn_br, L0_ffn_Wq, L0_ffn_bq, L0_ffn_Wk, L0_ffn_bk, L0_ffn_Wv, L0_ffn_bv, L0_ffn_Wo, L0_ffn_bo, L0_ffn_Wm, L0_ffn_bm, L0_ffn_W1, L0_ffn_bf1, L0_ffn_W2, L0_ffn_bf2, L1_gnn_W1, L1_gnn_a_src1, L1_gnn_a_dst1, L1_gnn_b1, L1_gnn_g1, L1_gnn_be1, L1_gnn_Wr1, L1_gnn_br1, L1_gnn_W2, L1_gnn_a_src2, L1_gnn_a_dst2, L1_gnn_b2, L1_gnn_g2, L1_gnn_be2, L1_gnn_Wr2, L1_gnn_br2, L1_ffn_Wr, L1_ffn_Wi, L1_ffn_bi, L1_ffn_Wo, L1_ffn_bo, L2_gnn_W1, L2_gnn_att_src1, L2_gnn_att_dst1, L2_gnn_b1, L2_gnn_W2, L2_gnn_att_src2, L2_gnn_att_dst2, L2_gnn_b2, L2_ffn_gate_w, L2_ffn_gate_b, L2_ffn_W1, L2_ffn_B1, L2_ffn_W3, L2_ffn_B3, L2_ffn_W2, L2_ffn_B2, L2_ffn_Ws1, L2_ffn_Bs1, L2_ffn_Ws3, L2_ffn_Bs3, L2_ffn_Ws2, L2_ffn_Bs2, L3_gnn_W, L3_gnn_attn_l, L3_gnn_attn_r, L3_gnn_W_res, L3_ffn_W_qkv, L3_ffn_b_qkv, L3_ffn_W_gate, L3_ffn_b_gate, L3_ffn_A, L3_ffn_B_lora, L3_ffn_W_proj, L3_ffn_b_proj):
    import jax
    import jax.numpy as jnp

    def _L0_gnn_ref(x, edge_index, edge_type, query_embs, W_rel1, W_root1, b1, W_rel2, W_root2, b2, Wg, bg, Wq, bq):
        import jax, jax.numpy as jnp
        import numpy as np
        NUM_RELATIONS = 3

        def _rgcn(x, W_rel, W_root, bias, src, dst, etype):
            n = x.shape[0]
            xr = jnp.einsum('ni,rio->rno', x, W_rel)
            msg = xr[etype, src]
            out = x @ W_root + bias
            for r in range(NUM_RELATIONS):
                m = etype == r
                s = jax.ops.segment_sum(jnp.where(m[:, None], msg, 0.0), dst, num_segments=n)
                c = jax.ops.segment_sum(m.astype(x.dtype), dst, num_segments=n)
                out = out + s / jnp.maximum(c, 1.0)[:, None]
            return out

        def _gate(h, q, Wg, bg, Wq, bq):
            B, L, F = q.shape
            N = h.shape[0] // B
            h3 = h.reshape(B, N, F)
            hg = jnp.einsum('bnf,gf->bng', h3, Wg[:, :F])
            qg = jnp.einsum('blf,gf->blg', q, Wg[:, F:]) + bg
            attn = jax.nn.sigmoid(hg[:, :, None, :] + qg[:, None, :, :])
            qi = jnp.einsum('bnlf,blf->bnf', attn, q)
            alpha = jax.nn.sigmoid(jnp.einsum('bnf,gf->bng', h3, Wq[:, :F]) + jnp.einsum('bnf,gf->bng', qi, Wq[:, F:]) + bq)
            hn = alpha * jnp.tanh(qi) + (1.0 - alpha) * h3
            return hn.reshape(B * N, F)
        src, dst = (edge_index[0], edge_index[1])
        h = jax.nn.relu(_rgcn(x, W_rel1, W_root1, b1, src, dst, edge_type))
        h = _gate(h, query_embs, Wg, bg, Wq, bq)
        h = jax.nn.relu(_rgcn(h, W_rel2, W_root2, b2, src, dst, edge_type))
        h = _gate(h, query_embs, Wg, bg, Wq, bq)
        return h

    def _L0_ffn_ref(hidden_states, g1, b1, g2, b2, Wr, br, Wq, bq, Wk, bk, Wv, bv, Wo, bo, Wm, bm, W1, bf1, W2, bf2):
        import jax, jax.numpy as jnp
        import numpy as np
        B, L, D, H, F = (4, 256, 768, 12, 384)
        ROUTE_FRAC = 0.15
        LN_EPS = 1e-05

        def _ln(x, g, b):
            m = jnp.mean(x, axis=-1, keepdims=True)
            v = jnp.mean((x - m) ** 2, axis=-1, keepdims=True)
            return (x - m) * jax.lax.rsqrt(v + LN_EPS) * g + b
        b, l, d = hidden_states.shape
        dh = d // H
        normed = _ln(hidden_states, g1, b1)
        scores = jax.nn.sigmoid(jnp.einsum('bld,d->bl', normed, Wr) + br)
        k = max(1, int(round(ROUTE_FRAC * l)))
        _, idx = jax.lax.top_k(-scores, k)
        attn_mask = jnp.zeros((b, l), bool).at[jnp.arange(b)[:, None], idx].set(True)
        q = (normed @ Wq + bq).reshape(b, l, H, dh)
        kk = (normed @ Wk + bk).reshape(b, l, H, dh)
        v = (normed @ Wv + bv).reshape(b, l, H, dh)
        logits = jnp.einsum('blhd,bmhd->bhlm', q, kk) / jnp.sqrt(jnp.float32(dh))
        probs = jax.nn.softmax(logits, axis=-1)
        ctx = jnp.einsum('bhlm,bmhd->blhd', probs, v).reshape(b, l, d)
        attn_out = ctx @ Wo + bo
        w = scores / (jnp.sum(scores, axis=1, keepdims=True) + 1e-06)
        pooled = jnp.einsum('bl,bld->bd', w, normed)
        mix_out = (normed + scores[..., None] * pooled[:, None, :]) @ Wm + bm
        merged = jnp.where(attn_mask[..., None], attn_out, mix_out)
        h = hidden_states + merged
        n2 = _ln(h, g2, b2)
        ffn = jax.nn.gelu(n2 @ W1 + bf1, approximate=False) @ W2 + bf2
        return h + ffn

    def _L1_gnn_ref(x, edge_index, W1, a_src1, a_dst1, b1, g1, be1, Wr1, br1, W2, a_src2, a_dst2, b2, g2, be2, Wr2, br2):
        import jax, jax.numpy as jnp
        import numpy as np
        N_NODES = 2500
        N_EDGES = 20000
        IN_DIM = 768
        HID = 256
        HEADS = 4
        OUT_DIM = 768
        LN_EPS = 1e-05

        def _add_self_loops(edge_index, n):
            loop = jnp.arange(n, dtype=edge_index.dtype)
            return jnp.concatenate([edge_index, jnp.stack([loop, loop])], axis=1)

        def gat_conv(x, edge_index, W, a_src, a_dst, bias, heads, out_ch, concat):
            n = x.shape[0]
            ei = _add_self_loops(edge_index, n)
            src, dst = (ei[0], ei[1])
            xl = (x @ W).reshape(n, heads, out_ch)
            alpha_src = jnp.einsum('nhc,hc->nh', xl, a_src)
            alpha_dst = jnp.einsum('nhc,hc->nh', xl, a_dst)
            e = jax.nn.leaky_relu(alpha_src[src] + alpha_dst[dst], 0.2)
            m = jax.ops.segment_max(e, dst, num_segments=n)
            e = jnp.exp(e - m[dst])
            s = jax.ops.segment_sum(e, dst, num_segments=n)
            alpha = e / (s[dst] + 1e-16)
            msg = xl[src] * alpha[:, :, None]
            out = jax.ops.segment_sum(msg, dst, num_segments=n)
            out = out.reshape(n, heads * out_ch) if concat else out.mean(axis=1)
            return out + bias

        def layer_norm(x, g, b):
            mu = jnp.mean(x, axis=-1, keepdims=True)
            var = jnp.var(x, axis=-1, keepdims=True)
            return (x - mu) * jax.lax.rsqrt(var + LN_EPS) * g + b
        h0 = x
        h = gat_conv(x, edge_index, W1, a_src1, a_dst1, b1, HEADS, HID, True)
        h = layer_norm(h, g1, be1)
        h = jax.nn.relu(h)
        h = h + (h0 @ Wr1 + br1)
        h1 = h
        h = gat_conv(h, edge_index, W2, a_src2, a_dst2, b2, 1, OUT_DIM, False)
        h = layer_norm(h, g2, be2)
        h = h + (h1 @ Wr2 + br2)
        return h

    def _L1_ffn_ref(x, Wr, Wi, bi, Wo, bo):
        import jax, jax.numpy as jnp
        import numpy as np
        B, S, H, F, E, TOP_K = (4, 256, 768, 384, 8, 2)
        xf = x.reshape(-1, x.shape[-1])
        router_logits = jnp.einsum('th,eh->te', xf, Wr)
        topk_vals, topk_idx = jax.lax.top_k(router_logits, TOP_K)
        routing_weights = jax.nn.softmax(topk_vals, axis=-1)
        h = jnp.einsum('th,efh->etf', xf, Wi) + bi[:, None, :]
        h = jax.nn.gelu(h, approximate=False)
        expert_out = jnp.einsum('etf,ehf->eth', h, Wo) + bo[:, None, :]
        expert_out = jnp.transpose(expert_out, (1, 0, 2))
        gathered = jnp.take_along_axis(expert_out, topk_idx[:, :, None], axis=1)
        out = jnp.einsum('tk,tkh->th', routing_weights, gathered)
        return out.reshape(x.shape)

    def _L2_gnn_ref(x, edge_index, W1, att_src1, att_dst1, b1, W2, att_src2, att_dst2, b2):
        import jax, jax.numpy as jnp
        import numpy as np
        N_NODES = 1250
        NEG_SLOPE = 0.2
        EPS = 1e-16

        def gat_layer(x, W, att_src, att_dst, bias, src, dst, heads, out_ch, concat):
            n = x.shape[0]
            h = (x @ W.T).reshape(n, heads, out_ch)
            a_src = jnp.einsum('nhc,hc->nh', h, att_src)
            a_dst = jnp.einsum('nhc,hc->nh', h, att_dst)
            e = a_src[src] + a_dst[dst]
            e = jax.nn.leaky_relu(e, NEG_SLOPE)
            m = jax.ops.segment_max(e, dst, num_segments=n)
            ex = jnp.exp(e - m[dst])
            denom = jax.ops.segment_sum(ex, dst, num_segments=n)
            alpha = ex / (denom[dst] + EPS)
            msg = alpha[:, :, None] * h[src]
            out = jax.ops.segment_sum(msg, dst, num_segments=n)
            if concat:
                out = out.reshape(n, heads * out_ch)
            else:
                out = out.mean(axis=1)
            return out + bias
        src, dst = (edge_index[0], edge_index[1])
        h = gat_layer(x, W1, att_src1, att_dst1, b1, src, dst, heads=8, out_ch=128, concat=True)
        h = jax.nn.relu(h)
        out = gat_layer(h, W2, att_src2, att_dst2, b2, src, dst, heads=1, out_ch=768, concat=True)
        return out

    def _L2_ffn_ref(x, gate_w, gate_b, W1, B1, W3, B3, W2, B2, Ws1, Bs1, Ws3, Bs3, Ws2, Bs2):
        import jax, jax.numpy as jnp
        import numpy as np
        B, S, D = (2, 1024, 768)
        I = 384
        E = 8
        G = 4
        TOPK_GROUPS = 2
        K = 2
        ROUTE_SCALE = 1.0
        ALPHA, LIMIT = (1.702, 7.0)

        def swiglu(h):
            xg = jnp.minimum(h[..., ::2], LIMIT)
            xl = jnp.clip(h[..., 1::2], -LIMIT, LIMIT)
            return xg * jax.nn.sigmoid(ALPHA * xg) * (xl + 1.0)

        def gate(x, gate_w, gate_b):
            scores = jax.nn.softmax(jnp.einsum('td,ed->te', x, gate_w).astype(jnp.float32), axis=-1)
            original_scores = scores
            s = scores + gate_b
            T = x.shape[0]
            sg = s.reshape(T, G, E // G)
            group_scores = jnp.sum(jax.lax.top_k(sg, 2)[0], axis=-1)
            _, gidx = jax.lax.top_k(group_scores, TOPK_GROUPS)
            keep = jnp.any(jax.nn.one_hot(gidx, G, dtype=jnp.bool_), axis=1)
            sg = jnp.where(keep[:, :, None], sg, -jnp.inf)
            s = sg.reshape(T, E)
            _, idx = jax.lax.top_k(s, K)
            w = jnp.take_along_axis(original_scores, idx, axis=1) * ROUTE_SCALE
            return (w.astype(x.dtype), idx)

        def expert_ffn(x, W1, B1, W3, B3, W2, B2):
            h1 = jnp.einsum('td,edh->teh', x, W1) + B1
            h3 = jnp.einsum('td,edh->teh', x, W3) + B3
            g = swiglu(h1 * h3)
            return jnp.einsum('tei,eid->ted', g, W2) + B2

        def shared_ffn(x, Ws1, Bs1, Ws3, Bs3, Ws2, Bs2):
            h = (x @ Ws1 + Bs1) * (x @ Ws3 + Bs3)
            return swiglu(h) @ Ws2 + Bs2
        inp_shape = x.shape
        xt = x.reshape(-1, D)
        w, idx = gate(xt, gate_w, gate_b)
        combine = jnp.einsum('tk,tke->te', w, jax.nn.one_hot(idx, E, dtype=w.dtype))
        per_expert = expert_ffn(xt, W1, B1, W3, B3, W2, B2)
        routed = jnp.einsum('ted,te->td', per_expert, combine)
        out = routed + shared_ffn(xt, Ws1, Bs1, Ws3, Bs3, Ws2, Bs2)
        return out.reshape(inp_shape)

    def _L3_gnn_ref(h, src, dst, W, attn_l, attn_r, W_res):
        import jax, jax.numpy as jnp
        import numpy as np
        N = 2500
        DEG = 16
        E = N * DEG
        H = 12
        DIN = 64
        DOUT = 64
        NEG_SLOPE = 0.2
        n = h.shape[0]
        hv = h.reshape(n, H, DIN)
        ft = jnp.einsum('nhd,od->nho', hv, W)
        a1 = jnp.sum(ft * attn_l, axis=-1)
        a2 = jnp.sum(ft * attn_r, axis=-1)
        e = jax.nn.leaky_relu(a1[src] + a2[dst], negative_slope=NEG_SLOPE)
        m = jax.ops.segment_max(e, dst, num_segments=n)
        m = jnp.where(jnp.isfinite(m), m, 0.0)
        w = jnp.exp(e - m[dst])
        denom = jax.ops.segment_sum(w, dst, num_segments=n)
        alpha = w / jnp.maximum(denom[dst], 1e-16)
        msg = alpha[:, :, None] * ft[src]
        agg = jax.ops.segment_sum(msg, dst, num_segments=n)
        res = jnp.einsum('nhd,od->nho', hv, W_res)
        out = jax.nn.relu((agg + res).reshape(n, H * DOUT))
        return out

    def _L3_ffn_ref(x, W_qkv, b_qkv, W_gate, b_gate, A, B_lora, W_proj, b_proj):
        import jax, jax.numpy as jnp
        import numpy as np
        B_SZ, S, D = (8, 512, 768)
        H = 12
        N_EXP = 8
        RANK = 16
        ALPHA = 32
        TOP_K = 2
        b, s, d = x.shape
        n_exp, rank = (A.shape[0], A.shape[1])
        scaling = ALPHA / rank
        head_dim = d // H
        scale = head_dim ** (-0.5)
        t = b * s
        x_flat = x.reshape(t, d)
        qkv_base = x @ W_qkv.T + b_qkv
        logits = x_flat @ W_gate.T + b_gate
        router_probs = jax.nn.softmax(logits, axis=-1)
        top_k_weights, top_k_indices = jax.lax.top_k(router_probs, TOP_K)
        a_down = jnp.einsum('td,nrd->tnr', x_flat, A)
        expert_out = jnp.einsum('tnr,nor->tno', a_down, B_lora) * scaling
        dispatch = jnp.zeros((t, n_exp), x.dtype).at[jnp.arange(t)[:, None], top_k_indices].add(top_k_weights)
        sparse_out = jnp.einsum('tno,tn->to', expert_out, dispatch)
        qkv = qkv_base + sparse_out.reshape(b, s, 3 * d)
        qkv = qkv.reshape(b, s, 3, H, head_dim).transpose(2, 0, 3, 1, 4)
        q, k, v = (qkv[0], qkv[1], qkv[2])
        attn = jax.nn.softmax(jnp.einsum('bhqd,bhkd->bhqk', q, k) * scale, axis=-1)
        out = jnp.einsum('bhqk,bhkd->bhqd', attn, v)
        out = out.transpose(0, 2, 1, 3).reshape(b, s, d)
        return out @ W_proj.T + b_proj
    edge_index = jnp.stack([src, dst])
    x = x + _L0_gnn_ref(_layernorm(x, axis=-1), edge_index, edge_type_3, L0_gnn_query_embs, L0_gnn_W_rel1, L0_gnn_W_root1, L0_gnn_b1, L0_gnn_W_rel2, L0_gnn_W_root2, L0_gnn_b2, L0_gnn_Wg, L0_gnn_bg, L0_gnn_Wq, L0_gnn_bq)
    x = x + _L0_ffn_ref(_layernorm(x, axis=-1)[None], L0_ffn_g1, L0_ffn_b1, L0_ffn_g2, L0_ffn_b2, L0_ffn_Wr, L0_ffn_br, L0_ffn_Wq, L0_ffn_bq, L0_ffn_Wk, L0_ffn_bk, L0_ffn_Wv, L0_ffn_bv, L0_ffn_Wo, L0_ffn_bo, L0_ffn_Wm, L0_ffn_bm, L0_ffn_W1, L0_ffn_bf1, L0_ffn_W2, L0_ffn_bf2)[0]
    x = x + _L1_gnn_ref(_layernorm(x, axis=-1), edge_index, L1_gnn_W1, L1_gnn_a_src1, L1_gnn_a_dst1, L1_gnn_b1, L1_gnn_g1, L1_gnn_be1, L1_gnn_Wr1, L1_gnn_br1, L1_gnn_W2, L1_gnn_a_src2, L1_gnn_a_dst2, L1_gnn_b2, L1_gnn_g2, L1_gnn_be2, L1_gnn_Wr2, L1_gnn_br2)
    x = x + _L1_ffn_ref(_layernorm(x, axis=-1)[None], L1_ffn_Wr, L1_ffn_Wi, L1_ffn_bi, L1_ffn_Wo, L1_ffn_bo)[0]
    x = x + _L2_gnn_ref(_layernorm(x, axis=-1), edge_index, L2_gnn_W1, L2_gnn_att_src1, L2_gnn_att_dst1, L2_gnn_b1, L2_gnn_W2, L2_gnn_att_src2, L2_gnn_att_dst2, L2_gnn_b2)
    x = x + _L2_ffn_ref(_layernorm(x, axis=-1)[None], L2_ffn_gate_w, L2_ffn_gate_b, L2_ffn_W1, L2_ffn_B1, L2_ffn_W3, L2_ffn_B3, L2_ffn_W2, L2_ffn_B2, L2_ffn_Ws1, L2_ffn_Bs1, L2_ffn_Ws3, L2_ffn_Bs3, L2_ffn_Ws2, L2_ffn_Bs2)[0]
    x = x + _L3_gnn_ref(_layernorm(x, axis=-1), src, dst, L3_gnn_W, L3_gnn_attn_l, L3_gnn_attn_r, L3_gnn_W_res)
    x = x + _L3_ffn_ref(_layernorm(x, axis=-1)[None], L3_ffn_W_qkv, L3_ffn_b_qkv, L3_ffn_W_gate, L3_ffn_b_gate, L3_ffn_A, L3_ffn_B_lora, L3_ffn_W_proj, L3_ffn_b_proj)[0]
    return x

_drawn_inputs = setup_inputs


def setup_inputs(seed=0):
    import zlib

    import numpy as np

    out = dict(_drawn_inputs(seed))
    spreads = {'L0_gnn_b1': (0.0, 0.517),
     'L0_gnn_b2': (0.0, 0.1),
     'L0_gnn_bg': (0.0, 0.28),
     'L0_gnn_bq': (0.0, 0.505),
     'L0_ffn_g1': (1.0, 0.2),
     'L0_ffn_b1': (0.0, 0.1),
     'L0_ffn_g2': (1.0, 0.6),
     'L0_ffn_b2': (0.0, 0.8),
     'L0_ffn_bq': (0.0, 0.8),
     'L0_ffn_bk': (0.0, 2.0),
     'L0_ffn_bv': (0.0, 0.78),
     'L0_ffn_bo': (0.0, 0.443),
     'L0_ffn_bm': (0.0, 0.1),
     'L0_ffn_bf1': (0.0, 0.489),
     'L0_ffn_bf2': (0.0, 0.1),
     'L1_gnn_b1': (0.0, 0.1),
     'L1_gnn_g1': (1.0, 0.2),
     'L1_gnn_be1': (0.0, 0.1),
     'L1_gnn_br1': (0.0, 0.1),
     'L1_gnn_b2': (0.0, 0.1),
     'L1_gnn_g2': (1.0, 0.2),
     'L1_gnn_be2': (0.0, 0.1),
     'L1_gnn_br2': (0.0, 0.1),
     'L1_ffn_bi': (0.0, 0.8),
     'L1_ffn_bo': (0.0, 0.281),
     'L2_gnn_b1': (0.0, 0.338),
     'L2_gnn_b2': (0.0, 0.1),
     'L3_ffn_b_qkv': (0.0, 2.0),
     'L3_ffn_b_gate': (0.0, 0.8),
     'L3_ffn_b_proj': (0.0, 2.0)}
    factors = {'L0_ffn_Wq': 8.0,
     'L0_ffn_Wk': 8.0,
     'L0_ffn_Wv': 4.535,
     'L0_ffn_Wo': 3.452,
     'L1_gnn_a_dst1': 8.0,
     'L1_gnn_a_src2': 3.342,
     'L1_gnn_a_dst2': 8.0,
     'L2_gnn_att_src1': 3.133,
     'L2_gnn_att_dst1': 8.0,
     'L2_gnn_att_src2': 8.0,
     'L2_gnn_att_dst2': 8.0,
     'L2_ffn_gate_w': 7.027,
     'L2_ffn_gate_b': 8.0,
     'L2_ffn_W1': 6.105,
     'L2_ffn_B1': 8.0,
     'L2_ffn_W3': 6.027,
     'L2_ffn_B3': 8.0,
     'L2_ffn_W2': 5.809,
     'L2_ffn_B2': 200.0,
     'L2_ffn_Bs1': 64.0,
     'L2_ffn_Bs3': 64.0,
     'L2_ffn_Bs2': 200.0,
     'L3_ffn_W_gate': 8.0,
     'L3_ffn_A': 8.0,
     'L3_ffn_B_lora': 8.0,
     'L2_ffn_Ws1': 8.0,
     'L2_ffn_Ws3': 8.0,
     'L2_ffn_Ws2': 8.0,
     'L3_gnn_attn_r': 41.928,
     'L3_gnn_W': 8.0,
     'L3_gnn_attn_l': 8.0,
     'L3_gnn_W_res': 4.66,
     'L3_ffn_W_qkv': 2.905}
    for name, (base, spread) in spreads.items():
        noise = np.random.default_rng([zlib.crc32(name.encode()), seed]).standard_normal(out[name].shape)
        drawn = base * np.exp(spread * noise) if base else spread * noise
        out[name] = jnp.asarray(drawn.astype(out[name].dtype))
    for name, factor in factors.items():
        out[name] = (out[name] * factor).astype(out[name].dtype)
    return out
```

```python
from contextlib import ExitStack

import concourse.bass as bass
from concourse import mybir

P = 128
F32 = mybir.dt.float32
BF16 = mybir.dt.bfloat16
I32 = mybir.dt.int32
ALU = mybir.AluOpType
ACT = mybir.ActivationFunctionType
AX = mybir.AxisListType

N = 256
D = 768
KT = 6
NSLOT = 4
SLOT = 4608
NROW = 3
BIG = -1.0e30
NEDGE_T = 32

COLS = {}


def _cols():
    at = 0
    for name, n in [
        ("g0b1", 6), ("g0b2", 6), ("g0bg", 6), ("g0bq", 6),
        ("f0g1", 6), ("f0b1", 6), ("f0g2", 6), ("f0b2", 6), ("f0Wr", 6), ("f0bq", 6), ("f0bk", 6),
        ("f0bf1", 3), ("f0br", 1),
        ("g1g1", 8), ("g1be1", 8), ("g1br1", 8),
        ("f1bi", 24), ("f1Wr", 48),
        ("f2gw", 48), ("f2gb", 8), ("f2B1", 48), ("f2B3", 48), ("f2Bs1", 6), ("f2Bs3", 6),
        ("g3BD", 256), ("f3bq", 6), ("f3bk", 6), ("f3gw", 48), ("f3gb", 8),
        ("ident", 128), ("iota", 768), ("pidx", 2), ("lt8", 64),
    ]:
        COLS[name] = (at, n)
        at += n
    return at


NCOL = _cols()


class Queue:

    def __init__(self, sem):
        self.sem, self.count, self.items = sem, 0, []

    def do(self, fn, *after):
        self.count += 1
        self.items.append((after, fn, self.sem, 1))
        return (self.sem, self.count)

    def quiet(self, fn, *after):
        self.items.append((after, fn, None, 0))

    def dma(self, fn, sem, *after):
        self.items.append((after, fn, sem, 16))

    def emit(self, eng):
        seen = {}
        for after, fn, sem, inc in self.items:
            for s, v in after:
                if seen.get(id(s), 0) < v:
                    eng.wait_ge(s, v)
                    seen[id(s)] = v
            ins = fn(eng)
            if sem is not None:
                ins.then_inc(sem, inc)


class Bank:

    def __init__(self, t):
        self.t, self.free = t, ()


class Slot:
    def __init__(self, ap, sem):
        self.ap, self.sem, self.loads, self.free = ap, sem, 0, ()


def build(nc, dr, out, dbg=None):
    ctx = ExitStack()
    with ctx:
        def sb(name, n, dt=F32):
            return ctx.enter_context(nc.sbuf_tensor(name, [P, n], dt))

        def newsem(name):
            return ctx.enter_context(nc.semaphore(name))

        banks = [Bank(ctx.enter_context(nc.psum_tensor(f"ps{i}", [P, 512], F32))) for i in range(8)]
        ring = [Slot(sb(f"w{i}", SLOT), newsem(f"s_w{i}")) for i in range(NSLOT)]
        rows = [Slot(sb(f"r{i}", 1024), newsem(f"s_r{i}")) for i in range(NROW)]
        X = sb("X", 1536)
        XN = sb("XN", 1536)
        XTt = sb("XT", 1536)
        cp = sb("cp", NCOL)
        Cn = sb("Cn", 512)
        NM = sb("NM", 512)
        C1 = sb("C1", 512)
        NM1 = sb("NM1", 512)
        AhTt = sb("AhT", 1536)
        SM = sb("SM", 3072)
        WK = sb("WK", 18432)

        s_v, s_s, s_g, s_t = newsem("s_v"), newsem("s_s"), newsem("s_g"), newsem("s_t")
        s_x, s_c, s_e, s_q, s_out, s_dbg = (newsem(n) for n in ("s_x", "s_c", "s_e", "s_q", "s_out", "s_dbg"))
        V, S, G, T, L = Queue(s_v), Queue(s_s), Queue(s_g), Queue(s_t), Queue(None)
        L2 = S

        x3 = X[:, :].rearrange("p (m f) -> p m f", m=2)
        xn3 = XN[:, :].rearrange("p (m f) -> p m f", m=2)
        XT = XTt[:, :].rearrange("p (k n) -> p k n", k=KT)
        AhT = AhTt[:, :].rearrange("p (r k n) -> p r k n", r=3, k=2)
        Cn3, NM3, C13, NM13 = (t[:, :].rearrange("p (m s) -> p m s", m=2) for t in (Cn, NM, C1, NM1))

        def col(name, i=0, n=None):
            a, w = COLS[name]
            return cp[:, a + i:a + i + (w - i if n is None else n)]

        ident = col("ident")
        sm_at = [0]

        def small(n):
            a = sm_at[0]
            sm_at[0] += n
            assert sm_at[0] <= 3072
            return SM[:, a:a + n]

        def wk(_at, **kw):
            n = 1
            for v in kw.values():
                n *= v
            names = list(kw)
            v = WK[:, _at:_at + n]
            if len(names) == 1:
                return v
            return v.rearrange("p (%s) -> p %s" % (" ".join(names), " ".join(names)),
                               **{k: kw[k] for k in names[:-1]})

        turn = [0, 0]

        def load(name, width, index=None):
            s = ring[turn[0] % NSLOT]
            turn[0] += 1
            src = dr[name] if index is None else dr[name][index]
            L.dma(lambda e, s=s, src=src: e.dma_start(s.ap[:, 0:width], src), s.sem, *s.free)
            s.loads += 1
            s.tok = (s.sem, 16 * s.loads)
            return s

        def wv(s, a, kt, n):
            return s.ap[:, a:a + kt * n].rearrange("p (k n) -> p k n", k=kt)

        def load_row(name, width, parts=None):
            s = rows[turn[1] % NROW]
            turn[1] += 1
            if parts is None:
                L.dma(lambda e, s=s: e.dma_start(s.ap[:, 0:width], dr[name].partition_broadcast(P)), s.sem, *s.free)
            else:
                L.dma(lambda e, s=s: e.dma_start(s.ap[0:parts, 0:width], dr[name]), s.sem, *s.free)
            s.loads += 1
            s.tok = (s.sem, 16 * s.loads)
            return s

        bt = [0]

        def bank():
            b = banks[bt[0] % 8]
            bt[0] += 1
            return b

        def mm(b, o, pairs, after, first=True, last=True):
            n = len(pairs)
            tok = None
            for i, (l, r) in enumerate(pairs):
                a = tuple(after) + tuple(b.free) if i == 0 else ()
                fn = lambda e, l=l, r=r, st=(i == 0 and first), sp=(i == n - 1 and last): e.matmul(
                    o, l, r, start=st, stop=sp, skip_group_check=not (first and last))
                if i == n - 1:
                    tok = T.do(fn, *a)
                else:
                    T.quiet(fn, *a)
            return tok

        def tr(b, o, i, after):
            n = i.shape[0]
            return T.do(lambda e: e.transpose(o, i, ident[0:n, 0:n]), *after, *b.free)

        ev = [0]

        def copy(o, i, *after):
            ev[0] += 1
            if ev[0] % 2:
                return S.do(lambda e: e.activation(o, i, ACT.Copy), *after)
            return V.do(lambda e: e.tensor_copy(o, i), *after)

        def act(o, i, f, *after, bias=0.0, scale=1.0, accum=None):
            kw = dict(bias=bias, scale=scale)
            if accum is not None:
                kw["accum_out"] = accum
            return S.do(lambda e: e.activation(o, i, f, **kw), *after)

        def tt(o, a, b, op, *after, q=None):
            return (q or V).do(lambda e: e.tensor_tensor(o, a, b, op), *after)

        def ts(o, a, s1, s2, op0, op1, *after, q=None):
            if op1 is None:
                return (q or V).do(lambda e: e.tensor_scalar(o, a, s1, None, op0), *after)
            return (q or V).do(lambda e: e.tensor_scalar(o, a, s1, s2, op0, op1), *after)

        def stt(o, a, s, b, op0, op1, *after):
            return V.do(lambda e: e.scalar_tensor_tensor(out=o, in0=a, scalar=s, in1=b, op0=op0, op1=op1), *after)

        def red(o, a, op, *after, negate=None):
            if negate:
                return V.do(lambda e: e.tensor_reduce(o, a, AX.X, op, negate=True), *after)
            return V.do(lambda e: e.tensor_reduce(o, a, AX.X, op), *after)

        def ln(src, dst, F, after, dst_free=()):
            half = F // 2
            ag = small(4).rearrange("p (m a) -> p m a", m=2)
            rs = small(2)
            for m in range(2):
                st = small(12)
                for c in range(2):
                    t = V.do(lambda e, m=m, c=c, st=st: e.bn_stats(
                        st[:, 6 * c:6 * c + 6], src[:, m, c * half:(c + 1) * half]), *after)
                t = V.do(lambda e, st=st, m=m: e.bn_aggr(ag[:, m, :], st), t)
            t = ts(rs, ag[:, :, 1], 1e-5, None, ALU.add, None, t)
            t = act(rs, rs, ACT.Sqrt, t)
            t = V.do(lambda e: e.reciprocal(rs, rs), t)
            return [V.do(lambda e, m=m: e.tensor_scalar(
                dst[:, m, 0:F], src[:, m, 0:F], ag[:, m, 0:1], rs[:, m:m + 1], ALU.subtract, ALU.mult), t, *dst_free)
                for m in range(2)]

        def to_T(src, kt, dst, after, evac=None, dst_free=()):
            toks = []
            for k in range(0, kt, 2):
                b = bank()
                for h in range(2):
                    for m in range(2):
                        t = tr(b, b.t[:, h * 256 + m * P:h * 256 + (m + 1) * P], src[:, m, (k + h) * P:(k + h + 1) * P],
                               after)
                if evac is not None:
                    r = [evac(k + h, b.t[:, h * 256:h * 256 + 256], t) for h in range(2)]
                    b.free = tuple(r)
                    toks += r
                else:
                    t = copy(dst[:, k:k + 2, :], b.t[:, :].rearrange("p (k n) -> p k n", k=2), t, *dst_free)
                    b.free = (t,)
                    toks += [t, t]
            return toks

        def lin_node(lhs, after, w, wtok, n, evac, extra=None):
            toks, t = [], None
            for m in range(2):
                for c0 in range(0, n, 512):
                    c1 = min(n, c0 + 512)
                    b = bank()
                    o = b.t[:, 0:c1 - c0]
                    pairs = [(l[:, m * P:(m + 1) * P], r[:, c0:c1]) for l, r in zip(lhs, w)]
                    if extra is not None:
                        pairs.append(extra(m, c0, c1))
                    t = mm(b, o, pairs, tuple(after) + tuple(wtok))
                    r = evac(m, c0, c1, o, t)
                    b.free = (r,)
                    toks.append(r)
            return toks, t

        def lin_T(w, f, rhs, after, n=256):
            b = bank()
            o = b.t[:, 0:n]
            t = mm(b, o, [(l[:, f * P:(f + 1) * P], r) for l, r in zip(w, rhs)], after)
            return b, o, t

        def tiles(v, k):
            return [v[:, i, :] for i in range(k)]

        S.dma(lambda e: e.dma_start(cp[:, :], dr["cols"]), s_c)
        ctok = (s_c, 16)
        S.dma(lambda e: e.dma_start(x3, dr["x"].rearrange("(m p) f -> p m f", p=P)), s_x)
        ei = wk(16640, a=96).bitcast(I32)
        S.dma(lambda e: e.dma_start(ei, dr["edges"]), s_e)
        qT = wk(0, k=6, n=512)
        S.dma(lambda e: e.dma_start(wk(0, n=3072), dr["queries"]), s_q)

        ef = wk(16736, a=96)
        et = V.do(lambda e: e.tensor_copy(ef, ei), (s_e, 16))
        dcode = wk(16832, a=32)
        et = stt(dcode, ef[:, 64:96], 256.0, ef[:, 32:64], ALU.mult, ALU.add, et)
        NB = 4
        oh = [wk(14592 + 512 * i, a=512).bitcast(BF16) for i in range(NB)]
        acc = [bank() for _ in range(6)]
        ufree = [()] * NB
        iota = col("iota")
        for c in range(NEDGE_T):
            u = oh[c % NB]
            t1 = ts(u[:, 0:256], iota[:, 0:256], ef[:, c:c + 1], None, ALU.is_equal, None, et, ctok, *ufree[c % NB])
            t2 = ts(u[:, 256:1024], iota, dcode[:, c:c + 1], None, ALU.is_equal, None, et, ctok, *ufree[c % NB])
            for j in range(6):
                fn = lambda e, j=j, u=u, c=c: e.matmul(
                    acc[j].t[:, 0:256], u[:, 256 + j * P:256 + (j + 1) * P], u[:, 0:256],
                    start=(c == 0), stop=(c == NEDGE_T - 1))
                if j == 5:
                    t = T.do(fn, t1, t2)
                else:
                    T.quiet(fn, t1, t2)
            ufree[c % NB] = (t,)
        Cr = wk(13056, r=3, m=2, n=256)
        cnt = small(6)
        crt = []
        for j in range(6):
            r, m = divmod(j, 2)
            a = copy(Cr[:, r, m, :], acc[j].t[:, 0:256], t)
            acc[j].free = (a,)
            crt.append(a)
        a = red(cnt, wk(13056, j=6, n=256), ALU.add, *crt)
        a = tt(Cn3, Cr[:, 0, :, :], Cr[:, 1, :, :], ALU.add, *crt)
        ctot = tt(Cn3, Cn3, Cr[:, 2, :, :], ALU.add, a)
        a = ts(cnt, cnt, 1.0, None, ALU.max, None, ctot)
        a = V.do(lambda e: e.reciprocal(cnt, cnt), a)
        Cj = wk(13056, j=6, n=256)
        a = tt(Cj, Cj, cnt.unsqueeze(2).broadcast_to((P, 6, 256)), ALU.mult, a)
        aht = []
        for r in range(3):
            b = bank()
            for k in range(2):
                for m in range(2):
                    t = tr(b, b.t[:, k * 256 + m * P:k * 256 + (m + 1) * P], Cr[:, r, m, k * P:(k + 1) * P], (a,))
            t = copy(AhT[:, r, :, :], b.t[:, :].rearrange("p (k n) -> p k n", k=2), t)
            b.free = (t,)
            aht.append(t)
        nmt = ts(NM[:, :], Cn[:, :], 0.0, BIG, ALU.is_equal, ALU.mult, ctot)
        t = V.do(lambda e: e.tensor_copy(C1[:, :], Cn[:, :]), ctot)
        for m in range(2):
            t = tt(C13[:, m, m * P:(m + 1) * P], C13[:, m, m * P:(m + 1) * P], ident, ALU.add, t, ctok)
        c1t = ts(NM1[:, :], C1[:, :], 0.0, BIG, ALU.is_equal, ALU.mult, t)

        lt = ln(x3, xn3, D, [(s_x, 16)])
        xtt = to_T(xn3, KT, XT, [*lt, ctok])

        qgT = wk(3072, k=6, n=512)
        w = load("Wgq", SLOT)
        wt = tiles(wv(w, 0, 6, 768), 6)
        qgt = []
        for f in range(6):
            b, o, t = lin_T(wt, f, tiles(qT, 6), [w.tok, (s_q, 16)], n=512)
            t2 = act(qgT[:, f, :], o, ACT.Identity, t, ctok, bias=col("g0bg", f, 1))
            b.free = (t2,)
            qgt.append(t2)
        w.free = (t,)

        hT = wk(6144, k=6, n=256)
        hgT = wk(7680, k=6, n=256)
        qiT = wk(9216, k=6, n=256)
        aT = wk(10752, k=6, n=256)
        ahT = wk(12288, r=3, k=6, n=256)
        TB = [wk(12288 + 2048 * i, n=32, l=64) for i in range(3)]

        def rgcn(hN, hNt, hTin, hTt, rel, root, bcol, out_free):
            at = {}
            for r in range(3):
                for f in range(6):
                    if f % 2 == 0:
                        b = bank()
                    h = (f % 2) * 256
                    t = mm(b, b.t[:, h:h + 256],
                           [(hN[:, k, f * P:(f + 1) * P], AhT[:, r, k, :]) for k in range(2)], [*hNt, *aht])
                    if f % 2:
                        t = copy(ahT[:, r, f - 1:f + 1, :], b.t[:, :].rearrange("p (k n) -> p k n", k=2), t,
                                 *out_free)
                        b.free = (t,)
                        at[r, f] = at[r, f - 1] = t
            bs = [bank() for _ in range(3)]
            for i in range(4):
                w = load(root, SLOT) if i == 0 else load(rel, SLOT, i - 1)
                W = wv(w, 0, 6, 768)
                for f in range(6):
                    b, h = bs[f // 2], (f % 2) * 256
                    for k in range(6):
                        rhs = hTin[:, k, :] if i == 0 else ahT[:, i - 1, k, :]
                        aft = []
                        if k == 0:
                            aft = [w.tok] + (list(b.free) + list(hTt) if i == 0 else [])
                        if i > 0 and f == 0:
                            aft.append(at[i - 1, k])
                        fn = lambda e, b=b, h=h, W=W, k=k, f=f, rhs=rhs, st=(i == 0 and k == 0 and f % 2 == 0), \
                            sp=(i == 3 and k == 5): e.matmul(
                            b.t[:, h:h + 256], W[:, k, f * P:(f + 1) * P], rhs, start=st, stop=sp,
                            skip_group_check=True)
                        if k == 5:
                            t = T.do(fn, *aft)
                        else:
                            T.quiet(fn, *aft)
                    if i == 3:
                        if f % 2 == 0:
                            prev = t
                w.free = (t,)
            toks = []
            for f in range(6):
                b, h = bs[f // 2], (f % 2) * 256
                r = act(hT[:, f, :], b.t[:, h:h + 256], ACT.Relu, t, bias=col(bcol, f, 1))
                toks.append(r)
                b.free = (r,)
            return toks, t

        tbf = [()] * 3
        tbi = [0]

        def gate(ht):
            w = load("Wgh", SLOT)
            wt = tiles(wv(w, 0, 6, 768), 6)
            hgt = []
            for f in range(6):
                b, o, t = lin_T(wt, f, tiles(hT, 6), [w.tok, *ht])
                r = act(hgT[:, f, :], o, ACT.Copy, t)
                b.free = (r,)
                hgt.append(r)
            w.free = (t,)
            qit = []
            for f in range(6):
                for bb in range(8):
                    i = tbi[0] % 3
                    tbi[0] += 1
                    B = TB[i]
                    hv = hgT[:, f, bb * 32:(bb + 1) * 32].unsqueeze(2).broadcast_to((P, 32, 64))
                    qv = qgT[:, f, bb * 64:(bb + 1) * 64].unsqueeze(1).broadcast_to((P, 32, 64))
                    q2 = qT[:, f, bb * 64:(bb + 1) * 64].unsqueeze(1).broadcast_to((P, 32, 64))
                    t = tt(B, hv, qv, ALU.add, hgt[f], qgt[f], *tbf[i], q=G)
                    t = act(B, B, ACT.Sigmoid, t)
                    t = tt(B, B, q2, ALU.mult, t)
                    t = red(qiT[:, f, bb * 32:(bb + 1) * 32], B, ALU.add, t)
                    tbf[i] = (t,)
                qit.append(t)
            wa = load("Wqh", SLOT)
            wb = load("Wqq", SLOT)
            wt = tiles(wv(wa, 0, 6, 768), 6) + tiles(wv(wb, 0, 6, 768), 6)
            at = []
            for f in range(6):
                b, o, t = lin_T(wt, f, tiles(hT, 6) + tiles(qiT, 6), [wa.tok, wb.tok, *ht, *qit])
                r = act(aT[:, f, :], o, ACT.Sigmoid, t, bias=col("g0bq", f, 1))
                b.free = (r,)
                at.append(r)
            wa.free = wb.free = (t,)
            r = act(qiT, qiT, ACT.Tanh, t)
            r = tt(qiT, qiT, hT, ALU.subtract, r, t)
            r = tt(qiT, qiT, aT, ALU.mult, r, *at)
            r = tt(hT, hT, qiT, ALU.add, r, t)
            return r

        ht, _ = rgcn(xn3, lt, XT, xtt, "Wrel1", "Wroot1", "g0b1", [])
        r = gate(ht)
        hnt = []
        for m in range(2):
            for c in range(2):
                b = bank()
                for k in range(3):
                    f = c * 3 + k
                    t = tr(b, b.t[:, k * P:(k + 1) * P], hT[:, f, m * P:(m + 1) * P], (r,))
                t = copy(xn3[:, m, c * 384:(c + 1) * 384], b.t[:, 0:384], t)
                b.free = (t,)
                hnt.append(t)
        last_red = [x for y in tbf for x in y]
        ht, _ = rgcn(xn3, hnt, hT, [r], "Wrel2", "Wroot2", "g0b2", last_red)
        r = gate(ht)
        xt = []
        for m in range(2):
            for c in range(2):
                b = bank()
                for k in range(3):
                    f = c * 3 + k
                    t = tr(b, b.t[:, k * P:(k + 1) * P], hT[:, f, m * P:(m + 1) * P], (r,))
                xv = x3[:, m, c * 384:(c + 1) * 384]
                t = tt(xv, xv, b.t[:, 0:384], ALU.add, t)
                b.free = (t,)
                xt.append(t)

        ndbg = [0]
        dbg_after = []

        def snapshot(toks):
            if dbg is None:
                return []
            i = ndbg[0]
            ndbg[0] += 1
            L.dma(lambda e: e.dma_start(dbg[i].rearrange("(m p) f -> p m f", p=P), x3), s_dbg, *toks)
            return [(s_dbg, 16 * ndbg[0])]

        xt = list(xt) + snapshot(xt)

        def attention(qTv, kTv, vv, after, E0, ctx_out):
            Eb = [wk(E0 + 512 * i, m=2, n=256) for i in range(3)]
            Pb = [wk(E0 + 1536 + 512 * i, k=2, n=256) for i in range(3)]
            efree, pfree = [()] * 3, [()] * 3
            st = {}
            toks = []

            def scores(h):
                p, k = (h % 2) * 64, h // 2
                b = bank()
                for m in range(2):
                    t = mm(b, b.t[:, m * 256:(m + 1) * 256],
                           [(qTv[p:p + 64, k, m * P:(m + 1) * P], kTv[p:p + 64, k, :])], after)
                mx, sm = small(2), small(2)
                bv = b.t[:, :].rearrange("p (m n) -> p m n", m=2)
                t = red(mx, bv, ALU.max, t)
                t = ts(mx, mx, -0.125, None, ALU.mult, None, t)
                E = Eb[h % 3]
                for m in range(2):
                    t2 = act(E[:, m, :], bv[:, m, :], ACT.Exp, t, *efree[h % 3], bias=mx[:, m:m + 1], scale=0.125,
                             accum=sm[:, m:m + 1])
                b.free = (t2,)
                t = V.do(lambda e: e.reciprocal(sm, sm), t2)
                for m in range(2):
                    t3 = ts(E[:, m, :], E[:, m, :], sm[:, m:m + 1], None, ALU.mult, None, t)
                st[h] = t3

            def turn_p(h):
                b = bank()
                E = Eb[h % 3]
                for k in range(2):
                    for m in range(2):
                        t = tr(b, b.t[:, k * 256 + m * P:k * 256 + (m + 1) * P], E[:, m, k * P:(k + 1) * P],
                               (st[h],))
                efree[h % 3] = (t,)
                t = copy(Pb[h % 3], b.t[:, :].rearrange("p (k n) -> p k n", k=2), t, *pfree[h % 3])
                b.free = (t,)
                st[h] = t

            def mix(h):
                p = (h % 2) * 64
                if p == 0:
                    st["b"] = bank()
                b = st["b"]
                Pt = Pb[h % 3]
                t = mm(b, b.t[p:p + 64, 0:256],
                       [(vv[:, k, h * 64:(h + 1) * 64], Pt[:, k, :]) for k in range(2)], [st[h], *after])
                pfree[h % 3] = (t,)
                if p:
                    t = ctx_out(h // 2, b.t[:, 0:256], t)
                    b.free = (t,)
                    toks.append(t)

            for h in range(14):
                if h < 12:
                    scores(h)
                if 1 <= h < 13:
                    turn_p(h - 1)
                if h >= 2:
                    mix(h - 2)
            return toks

        lt = ln(x3, xn3, D, xt)
        HN = wk(0, m=2, f=768)
        lt2 = ln(xn3, HN, D, lt)
        nT = XT
        nt = to_T(HN, KT, nT, lt2, evac=lambda k, p, t: act(
            nT[:, k, :], p, ACT.Identity, t, bias=col("f0b1", k, 1), scale=col("f0g1", k, 1)))
        b = bank()
        t = mm(b, b.t[:, 0:256], [(col("f0Wr", k, 1).broadcast_to((P, P)), nT[:, k, :]) for k in range(6)], nt)
        srow = wk(1536, n=256)
        srt = act(srow, b.t[:, 0:256], ACT.Sigmoid, t, bias=col("f0br"))
        b.free = (srt,)
        b = bank()
        for m in range(2):
            t = tr(b, b.t[:, m * P:(m + 1) * P], srow[:, m * P:(m + 1) * P], (srt,))
        scol = small(2)
        t = V.do(lambda e, b=b: e.tensor_copy(scol, b.t[:, 0:256:128]), t)
        b.free = (t,)
        Gt = wk(1792, n=256)
        Qt = wk(2048, n=256)
        rk = small(2)
        mk2 = small(4)
        for m in range(2):
            sc = scol[:, m:m + 1]
            t = ts(Qt, iota[:, 0:256], col("pidx", m, 1), None, ALU.is_lt, None, t)
            t = stt(Qt, srow, sc, Qt, ALU.is_equal, ALU.mult, t)
            t = ts(Gt, srow, sc, None, ALU.is_lt, None, t)
            t = tt(Gt, Gt, Qt, ALU.add, t)
            t = red(rk[:, m:m + 1], Gt, ALU.add, t)
        mkv = mk2.rearrange("p (m a) -> p m a", m=2)
        t = ts(mkv[:, :, 0], rk, 38.0, None, ALU.is_lt, None, t)
        mkt = ts(mkv[:, :, 1], rk, 38.0, None, ALU.is_ge, None, t)
        b = bank()
        for m in range(2):
            for a in range(2):
                t = tr(b, b.t[:, a * 256 + m * P:a * 256 + (m + 1) * P],
                       mk2[:, 2 * m + a:2 * m + a + 1].broadcast_to((P, P)), (mkt,))
        mrow = wk(2304, a=2, n=256)
        mrt = V.do(lambda e, b=b: e.tensor_copy(wk(2304, n=512), b.t[:, :]), t)
        b.free = (mrt,)
        b = bank()
        for m in range(2):
            t = mm(b, b.t[0:2, m * P:(m + 1) * P], [(mk2[:, 2 * m:2 * m + 2], ident)], [mkt])
        mT = wk(2816, n=256)
        mtt = V.do(lambda e, b=b: e.tensor_copy(mT[0:2, :], b.t[0:2, 0:256]), t)
        b.free = (mtt,)
        ssum, pool = small(1), small(6)
        t = red(ssum, srow, ALU.add, srt)
        t = ts(ssum, ssum, 1e-6, None, ALU.add, None, t)
        t = V.do(lambda e: e.reciprocal(ssum, ssum), t)
        for k in range(6):
            t1 = V.do(lambda e, k=k: e.tensor_tensor_reduce(Gt, nT[:, k, :], srow, 1.0, 0.0, ALU.mult, ALU.add,
                                                           pool[:, k:k + 1]), t, nt[k], mkt)
            t = t1
        t = ts(pool, pool, ssum, None, ALU.mult, None, t)
        mixT = wk(3072, k=6, n=256)
        for k in range(6):
            t1 = stt(mixT[:, k, :], srow, pool[:, k:k + 1], nT[:, k, :], ALU.mult, ALU.add, t)
        mixt = tt(mixT, mixT, mrow[:, 1, :].unsqueeze(1).broadcast_to((P, 6, 256)), ALU.mult, t1, mrt)

        qA, kA = wk(4608, k=6, n=256), wk(6144, k=6, n=256)
        vA = wk(7680, m=2, f=768)
        ct = wk(9216, k=6, n=256)
        qk = []
        for name, dst, bc in (("f0Wq", qA, "f0bq"), ("f0Wk", kA, "f0bk")):
            w = load(name, SLOT)
            wt = tiles(wv(w, 0, 6, 768), 6)
            for f in range(6):
                b, o, t = lin_T(wt, f, tiles(nT, 6), [w.tok, *nt])
                r = act(dst[:, f, :], o, ACT.Identity, t, bias=col(bc, f, 1))
                b.free = (r,)
                qk.append(r)
            w.free = (t,)
        w = load("f0Wv", SLOT)
        rb = load_row("f0bv", 768)
        vt, t = lin_node(tiles(nT, 6), nt, tiles(wv(w, 0, 6, 768), 6), [w.tok], 768,
                         lambda m, c0, c1, p, t: tt(vA[:, m, c0:c1], p, rb.ap[:, c0:c1], ALU.add, t, rb.tok))
        w.free, rb.free = (t,), tuple(vt)
        ctt = attention(qA, kA, vA, [*qk, *vt], 10752, lambda k, p, t: tt(
            ct[:, k, :], p, mrow[:, 0, :], ALU.mult, t, mrt))
        wo, wm = load("f0Wo", SLOT), load("f0Wm", SLOT)
        rb = load_row("f0bom", 768, parts=2)
        hx = wk(0, m=2, f=768)
        ot, t = lin_node(tiles(ct, 6) + tiles(mixT, 6), [*ctt, mixt, rb.tok, mtt],
                         tiles(wv(wo, 0, 6, 768), 6) + tiles(wv(wm, 0, 6, 768), 6), [wo.tok, wm.tok], 768,
                         lambda m, c0, c1, p, t: tt(hx[:, m, c0:c1], p, xn3[:, m, c0:c1], ALU.add, t),
                         extra=lambda m, c0, c1: (mT[0:2, m * P:(m + 1) * P], rb.ap[0:2, c0:c1]))
        wo.free = wm.free = rb.free = (t,)
        lt = ln(hx, xn3, D, ot)
        nt = to_T(xn3, KT, nT, [*lt, t], evac=lambda k, p, t: act(
            nT[:, k, :], p, ACT.Identity, t, bias=col("f0b2", k, 1), scale=col("f0g2", k, 1)))
        w = load("f0W12", SLOT)
        w1 = tiles(wv(w, 0, 6, 384), 6)
        w2 = tiles(wv(w, 2304, 3, 768), 3)
        gT = wk(4608, k=3, n=256)
        gt = []
        for f in range(3):
            b, o, t = lin_T(w1, f, tiles(nT, 6), [w.tok, *nt])
            r = act(gT[:, f, :], o, ACT.Gelu, t, bias=col("f0bf1", f, 1))
            b.free = (r,)
            gt.append(r)
        rb = load_row("f0bf2", 768)
        t = tt(x3, x3, hx, ALU.add, *ot)
        t = tt(x3, x3, rb.ap[:, 0:768].unsqueeze(1).broadcast_to((P, 2, 768)), ALU.add, t, rb.tok)
        rb.free = (t,)
        xt, t = lin_node(tiles(gT, 3), gt, w2, [], 768, lambda m, c0, c1, p, tk, t=t: tt(
            x3[:, m, c0:c1], x3[:, m, c0:c1], p, ALU.add, tk, t))
        w.free = (t,)
        xt = list(xt) + snapshot(xt)

        def head_dots(xl, H, C, row_s, row_d, after, tmp):
            res = []
            t = None
            for row in (row_s, row_d):
                a = small(2 * H).rearrange("p (m h) -> p m h", m=2)
                for m in range(2):
                    x4 = xl[:, m, :].rearrange("p (h c) -> p h c", h=H)
                    r4 = row.ap[:, 0:H * C].rearrange("p (h c) -> p h c", h=H)
                    t4 = tmp[:, 0:H * C].rearrange("p (h c) -> p h c", h=H)
                    t = tt(t4, x4, r4, ALU.mult, *after, row.tok, *([t] if t else []))
                    t = red(a[:, m, :], t4, ALU.add, t)
                row.free = (t,)
                res.append((a, t))
            return res

        def gat(H, C, xl, xlt, row_s, row_d, Cm, NMm, cmt, E0, o_evac, free=()):
            tmp = WK[:, E0:E0 + 3072]
            (asr, ast), (ads, adt) = head_dots(xl, H, C, row_s, row_d, [*xlt, *free], tmp)
            E = [wk(E0 + m * H * 256, h=H, n=256) for m in range(2)]
            PT = [wk(E0 + 2 * H * 256 + 512 * i, k=2, n=256) for i in range(3)]
            et = [None, None]
            for h0 in range(0, H, 2):
                h1 = min(H, h0 + 2)
                b = bank()
                for h in range(h0, h1):
                    for k in range(2):
                        t = tr(b, b.t[:, (h - h0) * 256 + k * P:(h - h0) * 256 + (k + 1) * P],
                               asr[:, k, h:h + 1].broadcast_to((P, P)), (ast, adt))
                pv = b.t[:, 0:(h1 - h0) * 256].rearrange("p (h n) -> p h n", n=256)
                for m in range(2):
                    et[m] = tt(E[m][:, h0:h1, :], pv,
                               ads[:, m, h0:h1].unsqueeze(2).broadcast_to((P, h1 - h0, 256)), ALU.add, t, adt)
                b.free = (et[1],)
            dens = []
            for m in range(2):
                Ef = WK[:, E0 + m * H * 256:E0 + (m + 1) * H * 256]
                t = stt(Ef, Ef, 0.2, Ef, ALU.mult, ALU.max, et[m])
                t = tt(E[m], E[m], NMm[:, m, :].unsqueeze(1).broadcast_to((P, H, 256)), ALU.add, t, *cmt)
                mx, den = small(H), small(H)
                t = red(mx, E[m], ALU.max, t)
                t = tt(E[m], E[m], mx.unsqueeze(2).broadcast_to((P, H, 256)), ALU.subtract, t)
                t = act(Ef, Ef, ACT.Exp, t)
                t = tt(E[m], E[m], Cm[:, m, :].unsqueeze(1).broadcast_to((P, H, 256)), ALU.mult, t)
                et[m] = t
                t = red(den, E[m], ALU.add, t)
                t = ts(den, den, 1e-16, None, ALU.add, None, t)
                t = V.do(lambda e, den=den: e.reciprocal(den, den), t)
                dens.append((den, t))
            pfree = [()] * 3
            pt = {}
            per = max(1, min(4, 512 // C))
            toks = []
            hold = {}

            def turn_p(h):
                b = bank()
                for k in range(2):
                    for m in range(2):
                        t = tr(b, b.t[:, k * 256 + m * P:k * 256 + (m + 1) * P], E[m][:, h, k * P:(k + 1) * P],
                               (et[m],))
                t = copy(PT[h % 3], b.t[:, :].rearrange("p (k n) -> p k n", k=2), t, *pfree[h % 3])
                b.free = (t,)
                pt[h] = t

            def agg(h):
                Pt = PT[h % 3]
                for m in range(2):
                    for c0 in range(0, C, 512):
                        c1 = min(C, c0 + 512)
                        j = h % per
                        if j == 0:
                            hold[m] = bank()
                        b = hold[m]
                        t = mm(b, b.t[:, j * C:j * C + c1 - c0],
                               [(Pt[:, k, m * P:(m + 1) * P], xl[:, k, h * C + c0:h * C + c1]) for k in range(2)],
                               [pt[h], *xlt])
                        if j == per - 1 or h == H - 1:
                            den, dt = dens[m]
                            r = o_evac(m, h - j, h + 1, c0, c1, b.t[:, 0:j * C + c1 - c0], den, (t, dt))
                            b.free = (r,)
                            toks.append(r)
                pfree[h % 3] = (t,)

            for h in range(H + 1):
                if h < H:
                    turn_p(h)
                if h >= 1:
                    agg(h - 1)
            return toks, t

        def scale_evac(dst, C):
            def f(m, h0, h1, c0, c1, p, den, toks):
                if c1 - c0 < C:
                    return V.do(lambda e: e.tensor_scalar(dst[:, m, c0:c1], p, den[:, h0:h0 + 1], None, ALU.mult),
                                *toks)
                n = h1 - h0
                return tt(dst[:, m, h0 * C:h1 * C].rearrange("p (h c) -> p h c", h=n),
                          p.rearrange("p (h c) -> p h c", h=n),
                          den[:, h0:h1].unsqueeze(2).broadcast_to((P, n, C)), ALU.mult, *toks)
            return f

        def bcast2(row, n):
            return row.ap[:, 0:n].unsqueeze(1).broadcast_to((P, 2, n))

        lt = ln(x3, xn3, D, xt)
        xtt = to_T(xn3, KT, XT, lt)
        xl = wk(0, m=2, f=1024)
        xlt = []
        for c in range(2):
            w = load("g1W1", 3072, c)
            a, t = lin_node(tiles(XT, 6), xtt, tiles(wv(w, 0, 6, 512), 6), [w.tok], 512,
                            lambda m, c0, c1, p, t, c=c: copy(xl[:, m, c * 512:(c + 1) * 512], p, t))
            w.free = (t,)
            xlt += a
        rT = wk(2048, k=8, n=256)
        rt = []
        for c in range(2):
            w = load("g1Wr1", 3072, c)
            wt = tiles(wv(w, 0, 6, 512), 6)
            for f in range(4):
                b, o, t = lin_T(wt, f, tiles(XT, 6), [w.tok, *xtt])
                r = act(rT[:, c * 4 + f, :], o, ACT.Identity, t, bias=col("g1br1", c * 4 + f, 1))
                b.free = (r,)
                rt.append(r)
            w.free = (t,)
        rs, rd = load_row("g1as1", 1024), load_row("g1ad1", 1024)
        o1 = wk(4096, m=2, f=1024)
        ot, t = gat(4, 256, xl, xlt, rs, rd, C13, NM13, [c1t], 6144, scale_evac(o1, 256))
        rb = load_row("g1b1", 1024)
        t = tt(o1, o1, bcast2(rb, 1024), ALU.add, *ot, rb.tok)
        rb.free = (t,)
        lt = ln(o1, o1, 1024, [t])
        h1T = wk(0, k=8, n=256)
        nt = to_T(o1, 8, h1T, lt, evac=lambda k, p, t: act(
            h1T[:, k, :], p, ACT.Relu, t, *ot, bias=col("g1be1", k, 1), scale=col("g1g1", k, 1)))
        h1t = tt(h1T, h1T, rT, ALU.add, *nt, *rt)
        xl = wk(2048, m=2, f=768)
        ws = [load("g1W2", 3072, c) for c in range(2)]
        wt = [x for w in ws for x in tiles(wv(w, 0, 4, 768), 4)]
        xlt, t = lin_node(tiles(h1T, 8), [h1t], wt, [w.tok for w in ws], 768,
                          lambda m, c0, c1, p, t: copy(xl[:, m, c0:c1], p, t))
        for w in ws:
            w.free = (t,)
        ws = [load("g1Wr2", 3072, c) for c in range(2)]
        wt = [x for w in ws for x in tiles(wv(w, 0, 4, 768), 4)]
        rb = load_row("g1br2", 768)
        r2t, t = lin_node(tiles(h1T, 8), [h1t], wt, [w.tok for w in ws], 768,
                          lambda m, c0, c1, p, t: tt(x3[:, m, c0:c1], x3[:, m, c0:c1], p, ALU.add, t, *ot))
        for w in ws:
            w.free = (t,)
        r2t = tt(x3, x3, bcast2(rb, 768), ALU.add, *r2t, rb.tok)
        rb.free = (r2t,)
        rs, rd = load_row("g1as2", 768), load_row("g1ad2", 768)
        o1 = wk(3584, m=2, f=768)
        ot, t = gat(1, 768, xl, xlt, rs, rd, C13, NM13, [c1t], 6144, scale_evac(o1, 768))
        rb = load_row("g1b2", 768)
        t = tt(o1, o1, bcast2(rb, 768), ALU.add, *ot, rb.tok)
        rb.free = (t,)
        lt = ln(o1, o1, 768, [t])
        rb = load_row("g1g2", 768)
        t = tt(o1, o1, bcast2(rb, 768), ALU.mult, *lt, rb.tok)
        rb.free = (t,)
        rb = load_row("g1be2", 768)
        t = tt(o1, o1, bcast2(rb, 768), ALU.add, t, rb.tok)
        rb.free = (t,)
        t = tt(x3, x3, o1, ALU.add, t, r2t)
        xt = [t] + snapshot([t])

        lt8 = col("lt8").rearrange("p (e j) -> p e j", e=8)

        def top2(val, n, t):
            g = small(2 * n * n).rearrange("p (m e j) -> p m e j", m=2, e=n)
            q = small(2 * n * n).rearrange("p (m e j) -> p m e j", m=2, e=n)
            sel = small(2 * n).rearrange("p (m e) -> p m e", m=2)
            for m in range(2):
                vj = val[:, m, :].unsqueeze(1).broadcast_to((P, n, n))
                ve = val[:, m, :].unsqueeze(2).broadcast_to((P, n, n))
                a = tt(q[:, m, :, :], vj, ve, ALU.is_equal, t)
                a = tt(q[:, m, :, :], q[:, m, :, :], lt8[:, 0:n, 0:n], ALU.mult, a)
                b = tt(g[:, m, :, :], vj, ve, ALU.is_gt, t)
                b = tt(g[:, m, :, :], g[:, m, :, :], q[:, m, :, :], ALU.add, a, b)
                b = red(sel[:, m, :], g[:, m, :, :], ALU.add, b)
            return sel, ts(sel, sel, 2.0, None, ALU.is_lt, None, b)

        def gate_logits(wname, xT, xtt):
            b = bank()
            wvw = col(wname).rearrange("p (k e) -> p k e", k=6)
            for m in range(2):
                t = mm(b, b.t[:, 8 * m:8 * m + 8],
                       [(xT[:, k, m * P:(m + 1) * P], wvw[:, k, :]) for k in range(6)], xtt)
            return b, b.t[:, 0:16].rearrange("p (m e) -> p m e", m=2), t

        def softmax8(z, t):
            mx, sm = small(2), small(2)
            t = red(mx, z, ALU.max, t)
            t = tt(z, z, mx.unsqueeze(2).broadcast_to((P, 2, 8)), ALU.subtract, t)
            t = act(z, z, ACT.Exp, t)
            return sm, t

        def norm8(z, w, sm, t):
            t = red(sm, w, ALU.add, t)
            t = V.do(lambda e: e.reciprocal(sm, sm), t)
            return tt(z, z, sm.unsqueeze(2).broadcast_to((P, 2, 8)), ALU.mult, t)

        def comb_T(comb, n, t, at):
            b = bank()
            for m in range(2):
                t2 = mm(b, b.t[0:n, m * P:(m + 1) * P], [(comb[:, m, :], ident)], [t])
            o = wk(at, n=256)
            r = V.do(lambda e: e.tensor_copy(o[0:n, :], b.t[0:n, 0:256]), t2)
            b.free = (r,)
            return o, r

        lt = ln(x3, xn3, D, xt)
        xtt = to_T(xn3, KT, XT, lt)
        b, z, t = gate_logits("f1Wr", XT, xtt)
        lg = small(16).rearrange("p (m e) -> p m e", m=2)
        t = V.do(lambda e, z=z: e.tensor_copy(lg, z), t)
        b.free = (t,)
        sel, t = top2(lg, 8, t)
        sm, t = softmax8(lg, t)
        t = tt(lg, lg, sel, ALU.mult, t)
        cbt = norm8(lg, lg, sm, t)
        comb = lg
        cT, cTt = comb_T(comb, 8, cbt, 0)
        rb = load_row("f1bo", 768, parts=8)
        xt = [None] * 4
        for m in range(2):
            for ci, (c0, c1) in enumerate(((0, 512), (512, 768))):
                b = bank()
                t = mm(b, b.t[:, 0:c1 - c0], [(cT[0:8, m * P:(m + 1) * P], rb.ap[0:8, c0:c1])], [cTt, rb.tok])
                xt[2 * m + ci] = tt(x3[:, m, c0:c1], x3[:, m, c0:c1], b.t[:, 0:c1 - c0], ALU.add, t, *lt)
                b.free = (xt[2 * m + ci],)
        rb.free = (t,)
        gbuf = [wk(256 + 768 * i, k=3, n=256) for i in range(2)]
        gfree = [(), ()]
        pend = []

        def down(w, w2, gv, gt, comb, e, gi):
            idx = [0]

            def evac(m, c0, c1, p, t):
                i = idx[0]
                idx[0] += 1
                xv = x3[:, m, c0:c1]
                xt[i] = stt(xv, p, comb[:, m, e:e + 1], xv, ALU.mult, ALU.add, t, xt[i], cbt) if comb is not None \
                    else tt(xv, xv, p, ALU.add, t, xt[i])
                return xt[i]
            _, t = lin_node(tiles(gv, 3), gt, w2, [w.tok], 768, evac)
            gfree[gi] = (t,)
            w.free = (t,)

        for e in range(8):
            w = load("f1W", SLOT, e)
            w1 = tiles(wv(w, 0, 6, 384), 6)
            w2 = tiles(wv(w, 2304, 3, 768), 3)
            gv = gbuf[e % 2]
            gt = []
            for f in range(3):
                b, o, t = lin_T(w1, f, tiles(XT, 6), [w.tok, *xtt])
                r = act(gv[:, f, :], o, ACT.Gelu, t, *gfree[e % 2], bias=col("f1bi", e * 3 + f, 1))
                b.free = (r,)
                gt.append(r)
            if pend:
                down(*pend.pop())
            pend.append((w, w2, gv, gt, comb, e, e % 2))
        down(*pend.pop())
        xt = list(xt) + snapshot(xt)

        lt = ln(x3, xn3, D, xt)
        xtt = to_T(xn3, KT, XT, lt)
        xl = wk(0, m=2, f=1024)
        xlt = []
        for c in range(2):
            w = load("g2W1", 3072, c)
            a, t = lin_node(tiles(XT, 6), xtt, tiles(wv(w, 0, 6, 512), 6), [w.tok], 512,
                            lambda m, c0, c1, p, t, c=c: copy(xl[:, m, c * 512:(c + 1) * 512], p, t, *xt[:4]))
            w.free = (t,)
            xlt += a
        rs, rd = load_row("g2as1", 1024), load_row("g2ad1", 1024)
        o1 = wk(2048, m=2, f=1024)
        ot, t = gat(8, 128, xl, xlt, rs, rd, Cn3, NM3, [nmt], 6144, scale_evac(o1, 128))
        rb = load_row("g2b1", 1024)
        t = tt(o1, o1, bcast2(rb, 1024), ALU.add, *ot, rb.tok)
        rb.free = (t,)
        h1T = wk(4096, k=8, n=256)
        nt = to_T(o1, 8, h1T, [t], evac=lambda k, p, t: act(h1T[:, k, :], p, ACT.Relu, t))
        xl = wk(0, m=2, f=768)
        ws = [load("g2W2", 3072, c) for c in range(2)]
        wt = [x for w in ws for x in tiles(wv(w, 0, 4, 768), 4)]
        xlt, t = lin_node(tiles(h1T, 8), nt, wt, [w.tok for w in ws], 768,
                          lambda m, c0, c1, p, t: copy(xl[:, m, c0:c1], p, t, *ot))
        for w in ws:
            w.free = (t,)
        rs, rd = load_row("g2as2", 768), load_row("g2ad2", 768)
        o1 = wk(2048, m=2, f=768)
        ot, t = gat(1, 768, xl, xlt, rs, rd, Cn3, NM3, [nmt], 6144, scale_evac(o1, 768))
        rb = load_row("g2b2", 768)
        t = tt(o1, o1, bcast2(rb, 768), ALU.add, *ot, rb.tok)
        rb.free = (t,)
        t = tt(x3, x3, o1, ALU.add, t)
        xt = [t] + snapshot([t])

        lt = ln(x3, xn3, D, xt)
        xtt = to_T(xn3, KT, XT, lt)
        b, z, t = gate_logits("f2gw", XT, xtt)
        sc = small(16).rearrange("p (m e) -> p m e", m=2)
        t = V.do(lambda e, z=z: e.tensor_copy(sc, z), t)
        b.free = (t,)
        sm, t = softmax8(sc, t)
        t = norm8(sc, sc, sm, t)
        sg = small(16).rearrange("p (m e) -> p m e", m=2)
        t = tt(sg, sc, col("f2gb").unsqueeze(1).broadcast_to((P, 2, 8)), ALU.add, t)
        gs = small(8).rearrange("p (m g) -> p m g", m=2)
        t = red(gs, sg.rearrange("p m (g a) -> p m g a", a=2), ALU.add, t)
        keep, t = top2(gs, 4, t)
        t = ts(keep, keep, 1.0, -BIG, ALU.subtract, ALU.mult, t)
        for m in range(2):
            t = tt(sg[:, m, :].rearrange("p (g a) -> p g a", a=2), sg[:, m, :].rearrange("p (g a) -> p g a", a=2),
                   keep[:, m, :].unsqueeze(2).broadcast_to((P, 4, 2)), ALU.add, t)
        sel, t = top2(sg, 8, t)
        comb9 = small(18).rearrange("p (m e) -> p m e", m=2)
        t = V.do(lambda e: e.memset(comb9[:, :, 8:9], 1.0), t)
        cbt = tt(comb9[:, :, 0:8], sc, sel, ALU.mult, t)
        cT, cTt = comb_T(comb9, 9, cbt, 0)
        rb = load_row("f2B2", 768, parts=9)
        xt = [None] * 4
        for m in range(2):
            for ci, (c0, c1) in enumerate(((0, 512), (512, 768))):
                b = bank()
                t = mm(b, b.t[:, 0:c1 - c0], [(cT[0:9, m * P:(m + 1) * P], rb.ap[0:9, c0:c1])], [cTt, rb.tok])
                xt[2 * m + ci] = tt(x3[:, m, c0:c1], x3[:, m, c0:c1], b.t[:, 0:c1 - c0], ALU.add, t, *lt)
                b.free = (xt[2 * m + ci],)
        rb.free = (t,)
        hb = [wk(256 + 3072 * i, k=6, n=256) for i in range(2)]
        sb2 = [wk(256 + 3072 * i + 1536, k=3, n=256) for i in range(2)]
        gb2 = [wk(256 + 3072 * i + 2304, k=3, n=256) for i in range(2)]
        gfree[:] = [(), ()]
        hfree = [(), ()]
        pend = []
        for e in range(9):
            i = e % 2
            n1, n3 = ("f2Ws1", "f2Ws3") if e == 8 else ("f2W1", "f2W3")
            wa = load(n1, SLOT, None if e == 8 else e)
            wb = load(n3, SLOT, None if e == 8 else e)
            wta, wtb = tiles(wv(wa, 0, 6, 768), 6), tiles(wv(wb, 0, 6, 768), 6)
            b1 = (lambda f: col("f2Bs1", f, 1)) if e == 8 else (lambda f, e=e: col("f2B1", e * 6 + f, 1))
            b3 = (lambda f: col("f2Bs3", f, 1)) if e == 8 else (lambda f, e=e: col("f2B3", e * 6 + f, 1))
            H = hb[i]
            r1 = []
            for f in range(6):
                b, o, t = lin_T(wta, f, tiles(XT, 6), [wa.tok, *xtt])
                r = act(H[:, f, :], o, ACT.Identity, t, *hfree[i], bias=b1(f))
                b.free = (r,)
                r1.append(r)
            wa.free = (t,)
            if pend:
                down(*pend.pop())
            r3 = []
            for f in range(6):
                b, o, t = lin_T(wtb, f, tiles(XT, 6), [wb.tok])
                r = stt(H[:, f, :], o, b3(f), H[:, f, :], ALU.add, ALU.mult, t, r1[f])
                b.free = (r,)
                r3.append(r)
            wb.free = (t,)
            hg, hl, sg_, gv = H[:, 0:3, :], H[:, 3:6, :], sb2[i], gb2[i]
            t = ts(hg, hg, 7.0, None, ALU.min, None, *r3)
            t1 = act(sg_, hg, ACT.Sigmoid, t, *hfree[i], scale=1.702)
            t = ts(hl, hl, 7.0, -7.0, ALU.min, ALU.max, *r3)
            t = V.do(lambda e_, hl=hl, hg=hg: e_.scalar_tensor_tensor(
                out=hl, in0=hl, scalar=1.0, in1=hg, op0=ALU.add, op1=ALU.mult), t, t1)
            t = tt(gv, hl, sg_, ALU.mult, t, t1, *gfree[i])
            hfree[i] = (t,)
            wc = load("f2Ws2" if e == 8 else "f2W2", 2304, None if e == 8 else e)
            pend.append((wc, tiles(wv(wc, 0, 3, 768), 3), gv, [t], comb9 if e < 8 else None, e, i))
        down(*pend.pop())
        xt = list(xt) + snapshot(xt)

        lt = ln(x3, xn3, D, xt)
        xtt = to_T(xn3, KT, XT, lt)
        ft = wk(0, m=2, f=768)
        res = wk(1536, m=2, f=768)
        BD = col("g3BD")
        ftt = []
        rtt = []
        for m in range(2):
            for k in range(6):
                if k % 2 == 0:
                    b = bank()
                h = (k % 2) * 256
                t = mm(b, b.t[:, h:h + 256], [(XT[:, k, m * P:(m + 1) * P], BD)], [*xtt, ctok])
                if k % 2:
                    pv = b.t[:, :].rearrange("p (k a n) -> p k a n", k=2, a=2)
                    c0 = (k - 1) * P
                    fo = ft[:, m, c0:c0 + 256].rearrange("p (k n) -> p k n", k=2)
                    ro = res[:, m, c0:c0 + 256].rearrange("p (k n) -> p k n", k=2)
                    t1 = act(fo, pv[:, :, 0, :], ACT.Copy, t, *xt[:4])
                    t2 = V.do(lambda e, ro=ro, pv=pv: e.tensor_copy(ro, pv[:, :, 1, :]), t, t1, *xt[:4])
                    b.free = (t1, t2)
                    ftt.append(t1)
                    rtt.append(t2)
        rs, rd = load_row("g3al", 768), load_row("g3ar", 768)
        o1 = wk(3072, m=2, f=768)
        ot, t = gat(12, 64, ft, ftt, rs, rd, Cn3, NM3, [nmt], 4608, scale_evac(o1, 64))
        t = tt(o1, o1, res, ALU.add, *ot, *rtt)
        t = ts(o1, o1, 0.0, None, ALU.max, None, t)
        t = tt(x3, x3, o1, ALU.add, t)
        xt = [t] + snapshot([t])

        lt = ln(x3, xn3, D, xt)
        xtt = to_T(xn3, KT, XT, lt)
        b, z, t = gate_logits("f3gw", XT, xtt)
        pr = small(16).rearrange("p (m e) -> p m e", m=2)
        t = tt(pr, z, col("f3gb").unsqueeze(1).broadcast_to((P, 2, 8)), ALU.add, t)
        b.free = (t,)
        sm, t = softmax8(pr, t)
        t = norm8(pr, pr, sm, t)
        sel, t = top2(pr, 8, t)
        t = tt(pr, pr, sel, ALU.mult, t)
        t = ts(pr, pr, 2.0, None, ALU.mult, None, t)
        wl = load("f3lora", 3072)
        A6 = tiles(wv(wl, 0, 6, 128), 6)
        ad = wk(0, m=2, f=128)
        adt = []
        for m in range(2):
            b = bank()
            t2 = mm(b, b.t[:, 0:P], [(XT[:, k, m * P:(m + 1) * P], A6[k]) for k in range(6)], [*xtt, wl.tok])
            r = tt(ad[:, m, :].rearrange("p (n r) -> p n r", n=8),
                   b.t[:, 0:P].rearrange("p (n r) -> p n r", n=8),
                   pr[:, m, :].unsqueeze(2).broadcast_to((P, 8, 16)), ALU.mult, t2, t)
            b.free = (r,)
            adt.append(r)
        adT = wk(256, n=256)
        b = bank()
        for m in range(2):
            t2 = tr(b, b.t[:, m * P:(m + 1) * P], ad[:, m, :], (adt[m],))
        adTt = V.do(lambda e, b=b: e.tensor_copy(adT, b.t[:, 0:256]), t2)
        b.free = (adTt,)
        LB = wl.ap[:, 768:3072]
        qA, kA = wk(512, k=6, n=256), wk(2048, k=6, n=256)
        vA = wk(3584, m=2, f=768)
        qk = []
        for j, (dst, bc) in enumerate(((qA, "f3bq"), (kA, "f3bk"))):
            w = load("f3Wqkv", SLOT, j)
            wt = tiles(wv(w, 0, 6, 768), 6) + [LB[:, j * 768:(j + 1) * 768]]
            for f in range(6):
                b, o, t = lin_T(wt, f, tiles(XT, 6) + [adT], [w.tok, *xtt, adTt])
                r = act(dst[:, f, :], o, ACT.Identity, t, bias=col(bc, f, 1))
                b.free = (r,)
                qk.append(r)
            w.free = (t,)
        w = load("f3Wqkv", SLOT, 2)
        rb = load_row("f3bv", 768)
        vt, t = lin_node(tiles(XT, 6) + [adT], [*xtt, adTt], tiles(wv(w, 0, 6, 768), 6) + [LB[:, 1536:2304]],
                         [w.tok], 768,
                         lambda m, c0, c1, p, t: tt(vA[:, m, c0:c1], p, rb.ap[:, c0:c1], ALU.add, t, rb.tok))
        w.free, wl.free, rb.free = (t,), (t,), tuple(vt)
        ct = wk(5120, k=6, n=256)
        ctt = attention(qA, kA, vA, [*qk, *vt], 6656, lambda k, p, t: copy(ct[:, k, :], p, t))
        w = load("f3Wp", SLOT)
        rb = load_row("f3bp", 768)
        t = tt(x3, x3, bcast2(rb, 768), ALU.add, rb.tok, *lt)
        xt, t = lin_node(tiles(ct, 6), ctt, tiles(wv(w, 0, 6, 768), 6), [w.tok], 768,
                         lambda m, c0, c1, p, tk, t=t: tt(x3[:, m, c0:c1], x3[:, m, c0:c1], p, ALU.add, tk, t))
        snapshot(xt)
        L.dma(lambda e: e.dma_start(out.rearrange("(m p) f -> p m f", p=P), x3), s_out, *xt)
        L.quiet(lambda e: e.wait_ge(s_out, 16))
        if dbg is not None:
            L.quiet(lambda e: e.wait_ge(s_dbg, 16 * ndbg[0]))

        block = ctx.enter_context(nc.Block())

        @block.sync
        def _(e):
            L.emit(e)

        @block.scalar
        def _(e):
            S.emit(e)

        @block.vector
        def _(e):
            V.emit(e)

        @block.gpsimd
        def _(e):
            G.emit(e)

        @block.tensor
        def _(e):
            T.emit(e)


def _lay(i):
    import numpy as np

    def W(w):
        k, n = w.shape
        return w.reshape(k // P, P, n).transpose(1, 0, 2).reshape(P, -1)

    def C(v):
        return np.asarray(v).reshape(-1, P).T

    def wide(v):
        v = np.asarray(v).reshape(-1)
        return np.broadcast_to(v, (P, v.size))

    a = {}
    i = {k: np.asarray(v) for k, v in i.items()}
    a["x"] = i["x"]
    a["edges"] = np.concatenate([i[k].reshape(P, NEDGE_T) for k in ("src", "dst", "edge_type_3")], 1)
    a["queries"] = W(i["L0_gnn_query_embs"].reshape(512, D).T)
    for n in ("1", "2"):
        a["Wrel" + n] = np.stack([W(w) for w in i["L0_gnn_W_rel" + n]])
        a["Wroot" + n] = W(i["L0_gnn_W_root" + n])
    a["Wgh"], a["Wgq"] = W(i["L0_gnn_Wg"][:, :D].T), W(i["L0_gnn_Wg"][:, D:].T)
    a["Wqh"], a["Wqq"] = W(i["L0_gnn_Wq"][:, :D].T), W(i["L0_gnn_Wq"][:, D:].T)
    for n in "qkvom":
        a["f0W" + n] = W(i["L0_ffn_W" + n])
    a["f0W12"] = np.concatenate([W(i["L0_ffn_W1"]), W(i["L0_ffn_W2"])], 1)
    a["f0bv"], a["f0bf2"] = i["L0_ffn_bv"], i["L0_ffn_bf2"]
    a["f0bom"] = np.stack([i["L0_ffn_bo"], i["L0_ffn_bm"]])
    for n in ("W1", "Wr1"):
        a["g1" + n] = np.stack([W(i["L1_gnn_" + n][:, c * 512:(c + 1) * 512]) for c in range(2)])
    for n in ("W2", "Wr2"):
        a["g1" + n] = np.stack([W(i["L1_gnn_" + n][c * 512:(c + 1) * 512]) for c in range(2)])
    for n, m in (("as1", "a_src1"), ("ad1", "a_dst1"), ("as2", "a_src2"), ("ad2", "a_dst2"), ("b1", "b1"),
                 ("b2", "b2"), ("g2", "g2"), ("be2", "be2"), ("br2", "br2")):
        a["g1" + n] = i["L1_gnn_" + m].reshape(-1)
    a["f1W"] = np.stack([np.concatenate([W(p.T), W(q.T)], 1) for p, q in zip(i["L1_ffn_Wi"], i["L1_ffn_Wo"])])
    a["f1bo"] = i["L1_ffn_bo"]
    a["g2W1"] = np.stack([W(i["L2_gnn_W1"].T[:, c * 512:(c + 1) * 512]) for c in range(2)])
    a["g2W2"] = np.stack([W(i["L2_gnn_W2"].T[c * 512:(c + 1) * 512]) for c in range(2)])
    for n, m in (("as1", "att_src1"), ("ad1", "att_dst1"), ("as2", "att_src2"), ("ad2", "att_dst2"),
                 ("b1", "b1"), ("b2", "b2")):
        a["g2" + n] = i["L2_gnn_" + m].reshape(-1)

    def eo(w):
        return np.concatenate([w[..., ::2], w[..., 1::2]], -1)

    a["f2W1"] = np.stack([W(eo(w)) for w in i["L2_ffn_W1"]])
    a["f2W3"] = np.stack([W(eo(w)) for w in i["L2_ffn_W3"]])
    a["f2W2"] = np.stack([W(w) for w in i["L2_ffn_W2"]])
    a["f2Ws1"], a["f2Ws3"] = W(eo(i["L2_ffn_Ws1"])), W(eo(i["L2_ffn_Ws3"]))
    a["f2Ws2"] = W(i["L2_ffn_Ws2"])
    a["f2B2"] = np.concatenate([i["L2_ffn_B2"], i["L2_ffn_Bs2"][None]])
    a["g3al"], a["g3ar"] = i["L3_gnn_attn_l"].reshape(-1), i["L3_gnn_attn_r"].reshape(-1)
    a["f3lora"] = np.concatenate([W(i["L3_ffn_A"].reshape(128, D).T),
                                  i["L3_ffn_B_lora"].transpose(0, 2, 1).reshape(128, 3 * D)], 1)
    a["f3Wqkv"] = np.stack([W(i["L3_ffn_W_qkv"][c * D:(c + 1) * D].T) for c in range(3)])
    a["f3bv"], a["f3bp"] = i["L3_ffn_b_qkv"][2 * D:], i["L3_ffn_b_proj"]
    a["f3Wp"] = W(i["L3_ffn_W_proj"].T)
    BD = np.zeros((P, 256), np.float32)
    for s in range(2):
        BD[s * 64:(s + 1) * 64, s * 64:(s + 1) * 64] = i["L3_gnn_W"].T
        BD[s * 64:(s + 1) * 64, 128 + s * 64:128 + (s + 1) * 64] = i["L3_gnn_W_res"].T
    c = {
        "g0b1": C(i["L0_gnn_b1"]), "g0b2": C(i["L0_gnn_b2"]), "g0bg": C(i["L0_gnn_bg"]), "g0bq": C(i["L0_gnn_bq"]),
        "f0g1": C(i["L0_ffn_g1"]), "f0b1": C(i["L0_ffn_b1"]), "f0g2": C(i["L0_ffn_g2"]), "f0b2": C(i["L0_ffn_b2"]),
        "f0Wr": C(i["L0_ffn_Wr"]), "f0bq": C(i["L0_ffn_bq"]), "f0bk": C(i["L0_ffn_bk"]),
        "f0bf1": C(i["L0_ffn_bf1"]), "f0br": wide(i["L0_ffn_br"]),
        "g1g1": C(i["L1_gnn_g1"]), "g1be1": C(i["L1_gnn_be1"]), "g1br1": C(i["L1_gnn_br1"]),
        "f1bi": C(i["L1_ffn_bi"]), "f1Wr": W(i["L1_ffn_Wr"].T),
        "f2gw": W(i["L2_ffn_gate_w"].T), "f2gb": wide(i["L2_ffn_gate_b"]),
        "f2B1": C(eo(i["L2_ffn_B1"])), "f2B3": C(eo(i["L2_ffn_B3"])),
        "f2Bs1": C(eo(i["L2_ffn_Bs1"])), "f2Bs3": C(eo(i["L2_ffn_Bs3"])),
        "g3BD": BD, "f3bq": C(i["L3_ffn_b_qkv"][:D]), "f3bk": C(i["L3_ffn_b_qkv"][D:2 * D]),
        "f3gw": W(i["L3_ffn_W_gate"].T), "f3gb": wide(i["L3_ffn_b_gate"]),
        "ident": np.eye(P, dtype=np.float32), "iota": wide(np.arange(768, dtype=np.float32)),
        "pidx": np.arange(256, dtype=np.float32).reshape(2, P).T,
        "lt8": wide(np.tril(np.ones((8, 8), np.float32), -1)),
    }
    a["cols"] = np.concatenate([c[n] for n in COLS], 1).astype(np.float32)
    assert a["cols"].shape == (P, NCOL)
    return {k: np.ascontiguousarray(v) for k, v in a.items()}


DEBUG = False


def kernel(**inputs):
    import concourse.bacc as _bacc
    from concourse.bass_utils import run_bass_kernel_spmd as _run

    nc = _bacc.Bacc("TRN2", target_bir_lowering=False, num_devices=1)
    arrays = _lay(inputs)
    dr = {k: nc.dram_tensor(k + "_in", v.shape, mybir.dt.from_np(v.dtype), kind="ExternalInput").ap()
          for k, v in arrays.items()}
    out = nc.dram_tensor("out", (N, D), F32, kind="ExternalOutput").ap()
    dbg = nc.dram_tensor("dbg", (8, N, D), F32, kind="ExternalOutput").ap() if DEBUG else None
    build(nc, dr, out, dbg)
    r = _run(nc, [{k + "_in": v for k, v in arrays.items()}], core_ids=[0])
    return r.results[0]["out"]
```

```python
from contextlib import ExitStack

import concourse.bass as bass
from concourse import mybir

P = 128
F32 = mybir.dt.float32
BF16 = mybir.dt.bfloat16
I32 = mybir.dt.int32
I16 = mybir.dt.int16
ALU = mybir.AluOpType
ACT = mybir.ActivationFunctionType
AX = mybir.AxisListType

N = 256
D = 768
KT = 6
NSLOT = 4
SLOT = 4608
NROW = 3
BIG = -1.0e30
NEDGE_T = 32
GADD = 8
GPE = (0, 1, 2, 3, 4, 5, 6, 7)

COLS = {}
MARKS = []


def _cols():
    at = 0
    for name, n in [
        ("g0b1", 6), ("g0b2", 6), ("g0bg", 6), ("g0bq", 6),
        ("f0g1", 6), ("f0b1", 6), ("f0g2", 6), ("f0b2", 6), ("f0Wr", 6), ("f0bq", 6), ("f0bk", 6),
        ("f0bf1", 3), ("f0br", 1),
        ("g1g1", 8), ("g1be1", 8), ("g1br1", 8),
        ("f1bi", 24), ("f1Wr", 48),
        ("f2gw", 48), ("f2gb", 8), ("f2B1", 48), ("f2B3", 48), ("f2Bs1", 6), ("f2Bs3", 6),
        ("g3BD", 256), ("f3bq", 6), ("f3bk", 6), ("f3gw", 48), ("f3gb", 8),
        ("ident", 128), ("iota", 768), ("pidx", 2), ("lt8", 64), ("eps", 1),
    ]:
        COLS[name] = (at, n)
        at += n
    return at


NCOL = _cols()


class Queue:

    def __init__(self, sem):
        self.sem, self.count, self.items = sem, 0, []

    def do(self, fn, *after):
        self.count += 1
        self.items.append((after, fn, self.sem, 1))
        return (self.sem, self.count)

    def quiet(self, fn, *after):
        self.items.append((after, fn, None, 0))

    def dma(self, fn, sem, *after):
        self.items.append((after, fn, sem, 16))

    def emit(self, eng):
        seen = {}
        for after, fn, sem, inc in self.items:
            for s, v in after:
                if seen.get(id(s), 0) < v:
                    eng.wait_ge(s, v)
                    seen[id(s)] = v
            ins = fn(eng)
            if sem is not None:
                ins.then_inc(sem, inc)


class Bank:

    def __init__(self, t):
        self.t, self.free = t, ()


class Slot:
    def __init__(self, ap, sem):
        self.ap, self.sem, self.loads, self.free = ap, sem, 0, ()


def build(nc, dr, out, dbg=None):
    ctx = ExitStack()
    with ctx:
        def sb(name, n, dt=F32):
            return ctx.enter_context(nc.sbuf_tensor(name, [P, n], dt))

        def newsem(name):
            return ctx.enter_context(nc.semaphore(name))

        PS = ctx.enter_context(nc.psum_tensor("PS", [P, 4096], F32))
        banks = [Bank(PS[:, 512 * i:512 * (i + 1)]) for i in range(8)]
        ring = [Slot(sb(f"w{i}", SLOT), newsem(f"s_w{i}")) for i in range(NSLOT)]
        rows = [Slot(sb(f"r{i}", 1024), newsem(f"s_r{i}")) for i in range(NROW)]
        X = sb("X", 1536)
        XN = sb("XN", 1536)
        XTt = sb("XT", 1536)
        cp = sb("cp", NCOL)
        Cn = sb("Cn", 512)
        NM = sb("NM", 512)
        C1 = sb("C1", 512)
        NM1 = sb("NM1", 512)
        AhTt = sb("AhT", 1536)
        SM = sb("SM", 3072)
        WK = sb("WK", 18432)

        s_v, s_s, s_g, s_t = newsem("s_v"), newsem("s_s"), newsem("s_g"), newsem("s_t")
        s_x, s_c, s_e, s_q, s_out, s_dbg = (newsem(n) for n in ("s_x", "s_c", "s_e", "s_q", "s_out", "s_dbg"))
        V, S, G, T, L = Queue(s_v), Queue(s_s), Queue(s_g), Queue(s_t), Queue(None)
        L2 = S

        x3 = X[:, :].rearrange("p (m f) -> p m f", m=2)
        xn3 = XN[:, :].rearrange("p (m f) -> p m f", m=2)
        XT = XTt[:, :].rearrange("p (k n) -> p k n", k=KT)
        AhT = AhTt[:, :].rearrange("p (r k n) -> p r k n", r=3, k=2)
        Cn3, NM3, C13, NM13 = (t[:, :].rearrange("p (m s) -> p m s", m=2) for t in (Cn, NM, C1, NM1))

        def col(name, i=0, n=None):
            a, w = COLS[name]
            return cp[:, a + i:a + i + (w - i if n is None else n)]

        ident = col("ident")
        sm_at = [0]

        def small(n):
            a = sm_at[0]
            sm_at[0] += n
            assert sm_at[0] <= 3072
            return SM[:, a:a + n]

        def wk(_at, **kw):
            n = 1
            for v in kw.values():
                n *= v
            names = list(kw)
            v = WK[:, _at:_at + n]
            if len(names) == 1:
                return v
            return v.rearrange("p (%s) -> p %s" % (" ".join(names), " ".join(names)),
                               **{k: kw[k] for k in names[:-1]})

        turn = [0, 0]

        def load(name, width, index=None):
            s = ring[turn[0] % NSLOT]
            turn[0] += 1
            src = dr[name] if index is None else dr[name][index]
            L.dma(lambda e, s=s, src=src: e.dma_start(s.ap[:, 0:width], src), s.sem, *s.free)
            s.loads += 1
            s.tok = (s.sem, 16 * s.loads)
            return s

        def wv(s, a, kt, n):
            return s.ap[:, a:a + kt * n].rearrange("p (k n) -> p k n", k=kt)

        def load_row(name, width, parts=None):
            s = rows[turn[1] % NROW]
            turn[1] += 1
            if parts is None:
                L.dma(lambda e, s=s: e.dma_start(s.ap[:, 0:width], dr[name].partition_broadcast(P)), s.sem, *s.free)
            else:
                L.dma(lambda e, s=s: e.dma_start(s.ap[0:parts, 0:width], dr[name]), s.sem, *s.free)
            s.loads += 1
            s.tok = (s.sem, 16 * s.loads)
            return s

        bt = [0]

        def bank():
            b = banks[bt[0] % 8]
            bt[0] += 1
            return b

        def mm(b, o, pairs, after, first=True, last=True):
            n = len(pairs)
            tok = None
            for i, pr_ in enumerate(pairs):
                l, r = pr_[0], pr_[1]
                a = tuple(after) + tuple(b.free) if i == 0 else ()
                a += tuple(pr_[2:])
                fn = lambda e, l=l, r=r, st=(i == 0 and first), sp=(i == n - 1 and last): e.matmul(
                    o, l, r, start=st, stop=sp, skip_group_check=not (first and last))
                if i == n - 1:
                    tok = T.do(fn, *a)
                else:
                    T.quiet(fn, *a)
            return tok

        def tr(b, o, i, after):
            n = i.shape[0]
            return T.do(lambda e: e.transpose(o, i, ident[0:n, 0:n]), *after, *b.free)

        ev = [0]

        def copy(o, i, *after):
            ev[0] += 1
            if ev[0] % 2:
                return S.do(lambda e: e.activation(o, i, ACT.Copy), *after)
            return V.do(lambda e: e.tensor_copy(o, i), *after)

        def act(o, i, f, *after, bias=0.0, scale=1.0, accum=None):
            kw = dict(bias=bias, scale=scale)
            if accum is not None:
                kw["accum_out"] = accum
            return S.do(lambda e: e.activation(o, i, f, **kw), *after)

        def tt(o, a, b, op, *after, q=None):
            return (q or V).do(lambda e: e.tensor_tensor(o, a, b, op), *after)

        def ts(o, a, s1, s2, op0, op1, *after, q=None):
            if op1 is None:
                return (q or V).do(lambda e: e.tensor_scalar(o, a, s1, None, op0), *after)
            return (q or V).do(lambda e: e.tensor_scalar(o, a, s1, s2, op0, op1), *after)

        def stt(o, a, s, b, op0, op1, *after):
            return V.do(lambda e: e.scalar_tensor_tensor(out=o, in0=a, scalar=s, in1=b, op0=op0, op1=op1), *after)

        def red(o, a, op, *after, negate=None):
            if negate:
                return V.do(lambda e: e.tensor_reduce(o, a, AX.X, op, negate=True), *after)
            return V.do(lambda e: e.tensor_reduce(o, a, AX.X, op), *after)

        def ln(src, dst, F, after, dst_free=()):
            half = F // 2
            ag = small(4).rearrange("p (m a) -> p m a", m=2)
            rs = small(2)
            sts = [small(12), small(12)]
            for m in range(2):
                for c in range(2):
                    t = V.do(lambda e, m=m, c=c: e.bn_stats(
                        sts[m][:, 6 * c:6 * c + 6], src[:, m, c * half:(c + 1) * half]), *per_tile(after, m))
                t = V.do(lambda e, m=m: e.bn_aggr(ag[:, m, :], sts[m]), t)
            t = act(rs, ag[:, :, 1], ACT.Sqrt, t, bias=col("eps"))
            t = V.do(lambda e: e.reciprocal(rs, rs), t)
            return [V.do(lambda e, m=m: e.tensor_scalar(
                dst[:, m, 0:F], src[:, m, 0:F], ag[:, m, 0:1], rs[:, m:m + 1], ALU.subtract, ALU.mult), t, *dst_free)
                for m in range(2)]

        def per_tile(after, m):
            return after[m] if isinstance(after, tuple) else after

        def to_T(src, kt, dst, after, evac=None, dst_free=()):
            bs = [bank() for _ in range(kt // 2)]
            for m in range(2):
                for k in range(kt):
                    b, h = bs[k // 2], (k % 2) * 256
                    t = tr(b, b.t[:, h + m * P:h + (m + 1) * P], src[:, m, k * P:(k + 1) * P], per_tile(after, m))
                    if m and k % 2:
                        b.tok = t
            toks = []
            for k in range(0, kt, 2):
                b = bs[k // 2]
                if evac is not None:
                    r = [evac(k + h, b.t[:, h * 256:h * 256 + 256], b.tok) for h in range(2)]
                    b.free = tuple(r)
                    toks += r
                else:
                    t = copy(dst[:, k:k + 2, :], b.t[:, :].rearrange("p (k n) -> p k n", k=2), b.tok, *dst_free)
                    b.free = (t,)
                    toks += [t, t]
            return toks

        def lin_node(lhs, after, w, wtok, n, evac, extra=None):
            toks, t = [], None
            for m in range(2):
                for c0 in range(0, n, 512):
                    c1 = min(n, c0 + 512)
                    b = bank()
                    o = b.t[:, 0:c1 - c0]
                    pairs = [(l[:, m * P:(m + 1) * P], r[:, c0:c1]) for l, r in zip(lhs, w)]
                    if extra is not None:
                        pairs.append(extra(m, c0, c1))
                    t = mm(b, o, pairs, tuple(after) + tuple(wtok))
                    r = evac(m, c0, c1, o, t)
                    b.free = (r,)
                    toks.append(r)
            return toks, t

        def lin_T(w, f, rhs, after, n=256):
            b = bank()
            o = b.t[:, 0:n]
            t = mm(b, o, [(l[:, f * P:(f + 1) * P], r) for l, r in zip(w, rhs)], after)
            return b, o, t

        def pair(lt, *more):
            return ([lt[0], *more], [lt[1], *more])

        def tiles(v, k):
            return [v[:, i, :] for i in range(k)]

        MARKS.append(("adj", len(T.items)))
        ei = wk(16640, a=96).bitcast(I32)
        L.dma(lambda e: e.dma_start(ei, dr["edges"]), s_e)
        L.dma(lambda e: e.dma_start(x3, dr["x"].rearrange("(m p) f -> p m f", p=P)), s_x)
        L.dma(lambda e: e.dma_start(cp[:, :], dr["cols"]), s_c)
        ctok = (s_c, 16)
        qT = wk(0, k=6, n=512)
        L.dma(lambda e: e.dma_start(wk(0, n=3072), dr["queries"]), s_q)

        lt = ln(x3, xn3, D, [(s_x, 16), ctok])
        xtt = to_T(xn3, KT, XT, pair(lt, ctok))

        ef = wk(16736, a=96)
        et = V.do(lambda e: e.tensor_copy(ef, ei), (s_e, 16))
        dcode = wk(16832, a=32)
        et = stt(dcode, ef[:, 64:96], 256.0, ef[:, 32:64], ALU.mult, ALU.add, et)
        NB = 4
        oh = [wk(14592 + 512 * i, a=512).bitcast(BF16) for i in range(NB)]
        acc = [bank() for _ in range(6)]
        ufree = [()] * NB
        iota = col("iota")
        io16 = wk(16896, a=384).bitcast(I16)
        iot = V.do(lambda e: e.tensor_copy(io16, iota), ctok)
        for c in range(NEDGE_T):
            u = oh[c % NB]
            t1 = ts(u[:, 0:256], io16[:, 0:256], ef[:, c:c + 1], None, ALU.is_equal, None, et, iot, *ufree[c % NB])
            t2 = ts(u[:, 256:1024], io16, dcode[:, c:c + 1], None, ALU.is_equal, None, et, iot, *ufree[c % NB])
            for j in range(6):
                fn = lambda e, j=j, u=u, c=c: e.matmul(
                    acc[j].t[:, 0:256], u[:, 256 + j * P:256 + (j + 1) * P], u[:, 0:256],
                    start=(c == 0), stop=(c == NEDGE_T - 1))
                fr = acc[j].free if c == 0 else ()
                if j == 5:
                    t = T.do(fn, t1, t2, *fr)
                else:
                    T.quiet(fn, t1, t2, *fr)
            ufree[c % NB] = (t,)
        Cr = wk(13056, r=3, m=2, n=256)
        cnt = small(6)
        crt = []
        for j in range(6):
            r, m = divmod(j, 2)
            a = copy(Cr[:, r, m, :], acc[j].t[:, 0:256], t)
            acc[j].free = (a,)
            crt.append(a)
        qgT = wk(3072, k=6, n=512)
        w = load("Wgq", SLOT)
        wt = tiles(wv(w, 0, 6, 768), 6)
        qgt = []
        for f in range(6):
            b, o, t = lin_T(wt, f, tiles(qT, 6), [w.tok, (s_q, 16)], n=512)
            t2 = act(qgT[:, f, :], o, ACT.Identity, t, ctok, bias=col("g0bg", f, 1))
            b.free = (t2,)
            qgt.append(t2)
        w.free = (t,)

        a = red(cnt, wk(13056, j=6, n=256), ALU.add, *crt)
        a = tt(Cn3, Cr[:, 0, :, :], Cr[:, 1, :, :], ALU.add, *crt)
        ctot = tt(Cn3, Cn3, Cr[:, 2, :, :], ALU.add, a)
        a = ts(cnt, cnt, 1.0, None, ALU.max, None, ctot)
        a = V.do(lambda e: e.reciprocal(cnt, cnt), a)
        Cj = wk(13056, j=6, n=256)
        a = tt(Cj, Cj, cnt.unsqueeze(2).broadcast_to((P, 6, 256)), ALU.mult, a)
        aht = []
        for r in range(3):
            b = bank()
            for k in range(2):
                for m in range(2):
                    t = tr(b, b.t[:, k * 256 + m * P:k * 256 + (m + 1) * P], Cr[:, r, m, k * P:(k + 1) * P], (a,))
            t = copy(AhT[:, r, :, :], b.t[:, :].rearrange("p (k n) -> p k n", k=2), t)
            b.free = (t,)
            aht.append(t)
        nmt = ts(NM[:, :], Cn[:, :], 0.0, BIG, ALU.is_equal, ALU.mult, ctot)
        t = V.do(lambda e: e.tensor_copy(C1[:, :], Cn[:, :]), ctot)
        for m in range(2):
            t = tt(C13[:, m, m * P:(m + 1) * P], C13[:, m, m * P:(m + 1) * P], ident, ALU.add, t, ctok)
        c1t = ts(NM1[:, :], C1[:, :], 0.0, BIG, ALU.is_equal, ALU.mult, t)

        MARKS.append(("L0gnn", len(T.items)))
        hT = wk(6144, k=6, n=256)
        qiT = wk(7680, k=6, n=256)
        hgT = XN[:, :].rearrange("p (k n) -> p k n", k=KT)
        aT = XT
        ahT = wk(12288, r=3, k=6, n=256)
        NTB = 4
        TB = [wk(9216 + 2048 * i, n=32, l=64) for i in range(NTB)]
        SP3 = [PS[:, 1024 * (i + 1):1024 * (i + 2)].rearrange("p (n l) -> p n l", l=64) for i in range(3)]

        def rgcn(hN, hNt, hTin, hTt, rel, root, bcol, out_free):
            at = {}
            for r in range(3):
                for f in range(6):
                    if f % 2 == 0:
                        b = bank()
                    h = (f % 2) * 256
                    t = mm(b, b.t[:, h:h + 256],
                           [(hN[:, k, f * P:(f + 1) * P], AhT[:, r, k, :]) for k in range(2)], [*hNt, *aht])
                    if f % 2:
                        t = copy(ahT[:, r, f - 1:f + 1, :], b.t[:, :].rearrange("p (k n) -> p k n", k=2), t,
                                 *out_free)
                        b.free = (t,)
                        at[r, f] = at[r, f - 1] = t
            bs = [bank() for _ in range(3)]
            for i in range(4):
                w = load(root, SLOT) if i == 0 else load(rel, SLOT, i - 1)
                W = wv(w, 0, 6, 768)
                for f in range(6):
                    b, h = bs[f // 2], (f % 2) * 256
                    for k in range(6):
                        rhs = hTin[:, k, :] if i == 0 else ahT[:, i - 1, k, :]
                        aft = []
                        if k == 0:
                            aft = [w.tok] + (list(b.free) + list(hTt) if i == 0 else [])
                        if i > 0 and f == 0:
                            aft.append(at[i - 1, k])
                        fn = lambda e, b=b, h=h, W=W, k=k, f=f, rhs=rhs, st=(i == 0 and k == 0 and f % 2 == 0), \
                            sp=(i == 3 and k == 5): e.matmul(
                            b.t[:, h:h + 256], W[:, k, f * P:(f + 1) * P], rhs, start=st, stop=sp,
                            skip_group_check=True)
                        if k == 5:
                            t = T.do(fn, *aft)
                        else:
                            T.quiet(fn, *aft)
                    if i == 3:
                        if f % 2 == 0:
                            prev = t
                w.free = (t,)
            toks = []
            for f in range(6):
                b, h = bs[f // 2], (f % 2) * 256
                r = act(hT[:, f, :], b.t[:, h:h + 256], ACT.Relu, t, bias=col(bcol, f, 1))
                toks.append(r)
                b.free = (r,)
            return toks, t

        def gate(ht, xn_free):
            w = load("Wgh", SLOT)
            wt = tiles(wv(w, 0, 6, 768), 6)
            hgt = []
            for f in range(6):
                b, o, t = lin_T(wt, f, tiles(hT, 6), [w.tok, *ht])
                r = act(hgT[:, f, :], o, ACT.Copy, t, *xn_free)
                b.free = (r,)
                hgt.append(r)
            w.free = (t,)
            tbf = [()] * NTB
            spf = [tuple(x for i in (2 * j + 2, 2 * j + 3) for x in banks[i].free) for j in range(3)]
            qit = [[] for _ in range(6)]
            prod, part = {}, {}
            NBK = 48

            def finish(i):
                f, bb = divmod(i, 8)
                dst = qiT[:, f, bb * 32:(bb + 1) * 32]
                if i in part:
                    b, t = part[i]
                    r = red(dst, b.t.rearrange("p (n l) -> p n l", l=16), ALU.add, t)
                    b.free = (r,)
                else:
                    r = red(dst, TB[i % NTB], ALU.add, prod[i])
                    tbf[i % NTB] = (r,)
                qit[f].append(r)

            sums = {}

            def add(i):
                f, bb = divmod(i, 8)
                B = TB[i % NTB]
                hv = hgT[:, f, bb * 32:(bb + 1) * 32].unsqueeze(2).broadcast_to((P, 32, 64))
                qv = qgT[:, f, bb * 64:(bb + 1) * 64].unsqueeze(1).broadcast_to((P, 32, 64))
                sums[i] = tt(B, hv, qv, ALU.add, hgt[f], qgt[f], *tbf[i % NTB], q=V if i % GADD == GADD - 1 else G)

            add(0)
            for i in range(NBK):
                f, bb = divmod(i, 8)
                B = TB[i % NTB]
                q2 = qT[:, f, bb * 64:(bb + 1) * 64].unsqueeze(1).broadcast_to((P, 16, 64))
                ta = sums.pop(i)
                for h in range(2):
                    j = (2 * i + h) % 3
                    Bh = B[:, 16 * h:16 * (h + 1), :]
                    t = act(SP3[j], Bh, ACT.Sigmoid, ta, *spf[j])
                    t = tt(Bh, SP3[j], q2, ALU.mult, t)
                    spf[j] = (t,)
                prod[i] = t
                if i >= 2 and i - 2 in part:
                    finish(i - 2)
                if i % 8 not in GPE:
                    finish(i)
                else:
                    b = banks[i % 2]
                    t = mm(b, b.t, [(ident, B[:, :, 16 * c:16 * (c + 1)]) for c in range(4)], [t])
                    tbf[i % NTB] = (t,)
                    part[i] = (b, t)
                if i + 1 < NBK:
                    add(i + 1)
            for i in (NBK - 2, NBK - 1):
                if i in part:
                    finish(i)
            for j in range(3):
                banks[2 * j + 2].free = banks[2 * j + 3].free = spf[j]
            qit = [x for y in qit for x in y]
            wa = load("Wqh", SLOT)
            wb = load("Wqq", SLOT)
            wt = tiles(wv(wa, 0, 6, 768), 6) + tiles(wv(wb, 0, 6, 768), 6)
            at = []
            for f in range(6):
                b, o, t = lin_T(wt, f, tiles(hT, 6) + tiles(qiT, 6), [wa.tok, wb.tok, *ht, *qit])
                r = act(aT[:, f, :], o, ACT.Sigmoid, t, bias=col("g0bq", f, 1))
                b.free = (r,)
                at.append(r)
            wa.free = wb.free = (t,)
            r = act(qiT, qiT, ACT.Tanh, t)
            r = tt(qiT, qiT, hT, ALU.subtract, r, t)
            r = tt(qiT, qiT, aT, ALU.mult, r, *at)
            r = tt(hT, hT, qiT, ALU.add, r, t)
            return r, qit

        ht, _ = rgcn(xn3, lt, XT, xtt, "Wrel1", "Wroot1", "g0b1", [])
        r, gl = gate(ht, [])
        hnt = []
        for m in range(2):
            for c in range(2):
                b = bank()
                for k in range(3):
                    f = c * 3 + k
                    t = tr(b, b.t[:, k * P:(k + 1) * P], hT[:, f, m * P:(m + 1) * P], (r,))
                t = copy(xn3[:, m, c * 384:(c + 1) * 384], b.t[:, 0:384], t)
                b.free = (t,)
                hnt.append(t)
        last_red = gl
        ht, _ = rgcn(xn3, hnt, hT, [r], "Wrel2", "Wroot2", "g0b2", last_red)
        r, gl = gate(ht, [])
        xt = []
        for m in range(2):
            for c in range(2):
                b = bank()
                for k in range(3):
                    f = c * 3 + k
                    t = tr(b, b.t[:, k * P:(k + 1) * P], hT[:, f, m * P:(m + 1) * P], (r,))
                xv = x3[:, m, c * 384:(c + 1) * 384]
                t = tt(xv, xv, b.t[:, 0:384], ALU.add, t)
                b.free = (t,)
                xt.append(t)

        ndbg = [0]
        dbg_after = []

        def snapshot(toks):
            if dbg is None:
                return []
            i = ndbg[0]
            ndbg[0] += 1
            L.dma(lambda e: e.dma_start(dbg[i].rearrange("(m p) f -> p m f", p=P), x3), s_dbg, *toks)
            return [(s_dbg, 16 * ndbg[0])]

        xt = list(xt) + snapshot(xt)

        def attention(qTv, kTv, vv, after, E0, ctx_out):
            Eb = [wk(E0 + 512 * i, m=2, n=256) for i in range(3)]
            Pb = [wk(E0 + 1536 + 512 * i, k=2, n=256) for i in range(3)]
            efree, pfree = [()] * 3, [()] * 3
            st = {}
            toks = []

            def scores(h):
                p, k = (h % 2) * 64, h // 2
                b = bank()
                for m in range(2):
                    t = mm(b, b.t[:, m * 256:(m + 1) * 256],
                           [(qTv[p:p + 64, k, m * P:(m + 1) * P], kTv[p:p + 64, k, :])], after)
                mx, sm = small(2), small(2)
                bv = b.t[:, :].rearrange("p (m n) -> p m n", m=2)
                t = red(mx, bv, ALU.max, t)
                t = ts(mx, mx, -0.125, None, ALU.mult, None, t)
                E = Eb[h % 3]
                for m in range(2):
                    t2 = act(E[:, m, :], bv[:, m, :], ACT.Exp, t, *efree[h % 3], bias=mx[:, m:m + 1], scale=0.125,
                             accum=sm[:, m:m + 1])
                b.free = (t2,)
                t = V.do(lambda e: e.reciprocal(sm, sm), t2)
                for m in range(2):
                    t3 = ts(E[:, m, :], E[:, m, :], sm[:, m:m + 1], None, ALU.mult, None, t)
                st[h] = t3

            def turn_p(h):
                b = bank()
                E = Eb[h % 3]
                for k in range(2):
                    for m in range(2):
                        t = tr(b, b.t[:, k * 256 + m * P:k * 256 + (m + 1) * P], E[:, m, k * P:(k + 1) * P],
                               (st[h],))
                efree[h % 3] = (t,)
                t = copy(Pb[h % 3], b.t[:, :].rearrange("p (k n) -> p k n", k=2), t, *pfree[h % 3])
                b.free = (t,)
                st[h] = t

            def mix(h):
                p = (h % 2) * 64
                if p == 0:
                    st["b"] = bank()
                b = st["b"]
                Pt = Pb[h % 3]
                t = mm(b, b.t[p:p + 64, 0:256],
                       [(vv[:, k, h * 64:(h + 1) * 64], Pt[:, k, :]) for k in range(2)], [st[h], *after])
                pfree[h % 3] = (t,)
                if p:
                    t = ctx_out(h // 2, b.t[:, 0:256], t)
                    b.free = (t,)
                    toks.append(t)

            for h in range(14):
                if h < 12:
                    scores(h)
                if 1 <= h < 13:
                    turn_p(h - 1)
                if h >= 2:
                    mix(h - 2)
            return toks

        MARKS.append(("L0ffn", len(T.items)))
        lt = ln(x3, xn3, D, xt)
        HN = wk(0, m=2, f=768)
        lt2 = ln(xn3, HN, D, lt)
        nT = XT
        nt = to_T(HN, KT, nT, pair(lt2), evac=lambda k, p, t: act(
            nT[:, k, :], p, ACT.Identity, t, bias=col("f0b1", k, 1), scale=col("f0g1", k, 1)))
        b = bank()
        t = mm(b, b.t[:, 0:256], [(col("f0Wr", k, 1).broadcast_to((P, P)), nT[:, k, :]) for k in range(6)], nt)
        srow = wk(1536, n=256)
        srt = act(srow, b.t[:, 0:256], ACT.Sigmoid, t, bias=col("f0br"))
        b.free = (srt,)
        b = bank()
        for m in range(2):
            t = tr(b, b.t[:, m * P:(m + 1) * P], srow[:, m * P:(m + 1) * P], (srt,))
        scol = small(2)
        t = V.do(lambda e, b=b: e.tensor_copy(scol, b.t[:, 0:256:128]), t)
        b.free = (t,)
        Gt = wk(1792, n=256)
        Qt = wk(2048, n=256)
        rk = small(2)
        mk2 = small(4)
        for m in range(2):
            sc = scol[:, m:m + 1]
            t = ts(Qt, iota[:, 0:256], col("pidx", m, 1), None, ALU.is_lt, None, t)
            t = stt(Qt, srow, sc, Qt, ALU.is_equal, ALU.mult, t)
            t = ts(Gt, srow, sc, None, ALU.is_lt, None, t)
            t = tt(Gt, Gt, Qt, ALU.add, t)
            t = red(rk[:, m:m + 1], Gt, ALU.add, t)
        mkv = mk2.rearrange("p (m a) -> p m a", m=2)
        t = ts(mkv[:, :, 0], rk, 38.0, None, ALU.is_lt, None, t)
        mkt = ts(mkv[:, :, 1], rk, 38.0, None, ALU.is_ge, None, t)
        b = bank()
        for m in range(2):
            for a in range(2):
                t = tr(b, b.t[:, a * 256 + m * P:a * 256 + (m + 1) * P],
                       mk2[:, 2 * m + a:2 * m + a + 1].broadcast_to((P, P)), (mkt,))
        mrow = wk(2304, a=2, n=256)
        mrt = V.do(lambda e, b=b: e.tensor_copy(wk(2304, n=512), b.t[:, :]), t)
        b.free = (mrt,)
        b = bank()
        for m in range(2):
            t = mm(b, b.t[0:2, m * P:(m + 1) * P], [(mk2[:, 2 * m:2 * m + 2], ident)], [mkt])
        mT = wk(2816, n=256)
        mtt = V.do(lambda e, b=b: e.tensor_copy(mT[0:2, :], b.t[0:2, 0:256]), t)
        b.free = (mtt,)
        ssum, pool = small(1), small(6)
        t = red(ssum, srow, ALU.add, srt)
        t = ts(ssum, ssum, 1e-6, None, ALU.add, None, t)
        t = V.do(lambda e: e.reciprocal(ssum, ssum), t)
        for k in range(6):
            t1 = V.do(lambda e, k=k: e.tensor_tensor_reduce(Gt, nT[:, k, :], srow, 1.0, 0.0, ALU.mult, ALU.add,
                                                           pool[:, k:k + 1]), t, nt[k], mkt)
            t = t1
        t = ts(pool, pool, ssum, None, ALU.mult, None, t)
        mixT = wk(3072, k=6, n=256)
        for k in range(6):
            t1 = stt(mixT[:, k, :], srow, pool[:, k:k + 1], nT[:, k, :], ALU.mult, ALU.add, t)
        mixt = tt(mixT, mixT, mrow[:, 1, :].unsqueeze(1).broadcast_to((P, 6, 256)), ALU.mult, t1, mrt)

        qA, kA = wk(4608, k=6, n=256), wk(6144, k=6, n=256)
        vA = wk(7680, m=2, f=768)
        ct = wk(9216, k=6, n=256)
        qk = []
        for name, dst, bc in (("f0Wq", qA, "f0bq"), ("f0Wk", kA, "f0bk")):
            w = load(name, SLOT)
            wt = tiles(wv(w, 0, 6, 768), 6)
            for f in range(6):
                b, o, t = lin_T(wt, f, tiles(nT, 6), [w.tok, *nt])
                r = act(dst[:, f, :], o, ACT.Identity, t, bias=col(bc, f, 1))
                b.free = (r,)
                qk.append(r)
            w.free = (t,)
        w = load("f0Wv", SLOT)
        rb = load_row("f0bv", 768)
        vt, t = lin_node(tiles(nT, 6), nt, tiles(wv(w, 0, 6, 768), 6), [w.tok], 768,
                         lambda m, c0, c1, p, t: tt(vA[:, m, c0:c1], p, rb.ap[:, c0:c1], ALU.add, t, rb.tok))
        w.free, rb.free = (t,), tuple(vt)
        ctt = attention(qA, kA, vA, [*qk, *vt], 10752, lambda k, p, t: tt(
            ct[:, k, :], p, mrow[:, 0, :], ALU.mult, t, mrt))
        wo, wm = load("f0Wo", SLOT), load("f0Wm", SLOT)
        rb = load_row("f0bom", 768, parts=2)
        hx = wk(0, m=2, f=768)
        ot, t = lin_node(tiles(ct, 6) + tiles(mixT, 6), [*ctt, mixt, rb.tok, mtt],
                         tiles(wv(wo, 0, 6, 768), 6) + tiles(wv(wm, 0, 6, 768), 6), [wo.tok, wm.tok], 768,
                         lambda m, c0, c1, p, t: tt(hx[:, m, c0:c1], p, xn3[:, m, c0:c1], ALU.add, t),
                         extra=lambda m, c0, c1: (mT[0:2, m * P:(m + 1) * P], rb.ap[0:2, c0:c1]))
        wo.free = wm.free = rb.free = (t,)
        lt = ln(hx, xn3, D, ot)
        nt = to_T(xn3, KT, nT, [*lt, t], evac=lambda k, p, t: act(
            nT[:, k, :], p, ACT.Identity, t, bias=col("f0b2", k, 1), scale=col("f0g2", k, 1)))
        w = load("f0W12", SLOT)
        w1 = tiles(wv(w, 0, 6, 384), 6)
        w2 = tiles(wv(w, 2304, 3, 768), 3)
        gT = wk(4608, k=3, n=256)
        gt = []
        for f in range(3):
            b, o, t = lin_T(w1, f, tiles(nT, 6), [w.tok, *nt])
            r = act(gT[:, f, :], o, ACT.Gelu, t, bias=col("f0bf1", f, 1))
            b.free = (r,)
            gt.append(r)
        rb = load_row("f0bf2", 768)
        t = tt(x3, x3, hx, ALU.add, *ot)
        t = tt(x3, x3, rb.ap[:, 0:768].unsqueeze(1).broadcast_to((P, 2, 768)), ALU.add, t, rb.tok)
        rb.free = (t,)
        xt, t = lin_node(tiles(gT, 3), gt, w2, [], 768, lambda m, c0, c1, p, tk, t=t: tt(
            x3[:, m, c0:c1], x3[:, m, c0:c1], p, ALU.add, tk, t))
        w.free = (t,)
        xt = list(xt) + snapshot(xt)

        def ttr(o, a, b, op0, op1, init, acc, *after):
            return V.do(lambda e: e.tensor_tensor_reduce(o, a, b, 1.0, init, op0, op1, acc), *after)

        def head_dots(xl, H, C, row_s, row_d, after, tmp):
            res = []
            t = None
            for row in (row_s, row_d):
                a = small(2 * H).rearrange("p (m h) -> p m h", m=2)
                for m in range(2):
                    if H <= 8:
                        for h in range(H):
                            t = ttr(tmp[:, h * C:(h + 1) * C], xl[:, m, h * C:(h + 1) * C],
                                    row.ap[:, h * C:(h + 1) * C], ALU.mult, ALU.add, 0.0, a[:, m, h:h + 1],
                                    *after, row.tok, *([t] if t else []))
                        continue
                    x4 = xl[:, m, :].rearrange("p (h c) -> p h c", h=H)
                    r4 = row.ap[:, 0:H * C].rearrange("p (h c) -> p h c", h=H)
                    t4 = tmp[:, 0:H * C].rearrange("p (h c) -> p h c", h=H)
                    t = tt(t4, x4, r4, ALU.mult, *after, row.tok, *([t] if t else []))
                    t = red(a[:, m, :], t4, ALU.add, t)
                row.free = (t,)
                res.append((a, t))
            return res

        def gat(H, C, xl, xlt, row_s, row_d, Cm, NMm, cmt, E0, o_evac, free=(), during=None):
            tmp = WK[:, E0:E0 + 3072]
            (asr, ast), (ads, adt) = head_dots(xl, H, C, row_s, row_d, [*xlt, *free], tmp)
            E = wk(E0, m=2, h=H, n=256)
            PT = [wk(E0 + 2 * H * 256 + 512 * i, k=2, n=256) for i in range(3)]
            F = [wk(E0 + 2 * H * 256 + 1536 + 512 * i, m=2, n=256) for i in range(3)]
            mx = small(2 * H).rearrange("p (m h) -> p m h", m=2)
            for h0 in range(0, H, 2):
                h1 = min(H, h0 + 2)
                b = bank()
                for h in range(h0, h1):
                    for k in range(2):
                        t = tr(b, b.t[:, (h - h0) * 256 + k * P:(h - h0) * 256 + (k + 1) * P],
                               asr[:, k, h:h + 1].broadcast_to((P, P)), (ast, adt))
                for h in range(h0, h1):
                    for m in range(2):
                        r = ttr(E[:, m, h, :], b.t[:, (h - h0) * 256:(h - h0 + 1) * 256], NMm[:, m, :], ALU.add,
                                ALU.max, 3.0 * BIG, mx[:, m, h:h + 1], t, *cmt)
                b.free = (r,)
            if during is not None:
                during()
            b1, b2, den = (small(2 * H).rearrange("p (m h) -> p m h", m=2) for _ in range(3))
            t = tt(mx, mx, ads, ALU.add, r)
            t = stt(mx, mx, 0.2, mx, ALU.mult, ALU.max, t)
            t2 = stt(b2, ads, 0.2, mx, ALU.mult, ALU.subtract, t)
            t1 = tt(b1, ads, mx, ALU.subtract, t)
            ffree, pfree = [()] * 3, [()] * 3
            pt, et = {}, {}
            per = max(1, min(4, 512 // C))
            toks = []
            hold = {}

            def soft(h):
                Fh = F[h % 3]
                for m in range(2):
                    act(Fh[:, m, :], E[:, m, h, :], ACT.Exp, t1, t2, r, *ffree[h % 3], bias=b1[:, m, h:h + 1])
                    a = act(E[:, m, h, :], E[:, m, h, :], ACT.Exp, bias=b2[:, m, h:h + 1], scale=0.2)
                a = tt(E[:, :, h, :], E[:, :, h, :], Fh, ALU.max, a)
                ffree[h % 3] = (a,)
                for m in range(2):
                    et[h] = ttr(E[:, m, h, :], E[:, m, h, :], Cm[:, m, :], ALU.mult, ALU.add, 0.0,
                                den[:, m, h:h + 1], a)

            def turn_p(h):
                b = bank()
                for k in range(2):
                    for m in range(2):
                        t = tr(b, b.t[:, k * 256 + m * P:k * 256 + (m + 1) * P], E[:, m, h, k * P:(k + 1) * P],
                               (et[h],))
                t = copy(PT[h % 3], b.t[:, :].rearrange("p (k n) -> p k n", k=2), t, *pfree[h % 3])
                b.free = (t,)
                pt[h] = t

            def agg(h):
                Pt = PT[h % 3]
                j = h % per
                if j == per - 1 or h == H - 1:
                    dv = den[:, :, h - j:h + 1]
                    dt = ts(dv, dv, 1e-16, None, ALU.add, None, et[h])
                    dt = V.do(lambda e: e.reciprocal(dv, dv), dt)
                for m in range(2):
                    for c0 in range(0, C, 512):
                        c1 = min(C, c0 + 512)
                        if j == 0:
                            hold[m] = bank()
                        b = hold[m]
                        t = mm(b, b.t[:, j * C:j * C + c1 - c0],
                               [(Pt[:, k, m * P:(m + 1) * P], xl[:, k, h * C + c0:h * C + c1]) for k in range(2)],
                               [pt[h], *xlt])
                        if j == per - 1 or h == H - 1:
                            q = o_evac(m, h - j, h + 1, c0, c1, b.t[:, 0:j * C + c1 - c0], den[:, m, :], (t, dt))
                            b.free = (q,)
                            toks.append(q)
                pfree[h % 3] = (t,)

            for h in range(H + 2):
                if h < H:
                    soft(h)
                if 1 <= h < H + 1:
                    turn_p(h - 1)
                if h >= 2:
                    agg(h - 2)
            return toks, t

        def scale_evac(dst, C):
            def f(m, h0, h1, c0, c1, p, den, toks):
                if c1 - c0 < C:
                    return V.do(lambda e: e.tensor_scalar(dst[:, m, c0:c1], p, den[:, h0:h0 + 1], None, ALU.mult),
                                *toks)
                n = h1 - h0
                return tt(dst[:, m, h0 * C:h1 * C].rearrange("p (h c) -> p h c", h=n),
                          p.rearrange("p (h c) -> p h c", h=n),
                          den[:, h0:h1].unsqueeze(2).broadcast_to((P, n, C)), ALU.mult, *toks)
            return f

        def bcast2(row, n):
            return row.ap[:, 0:n].unsqueeze(1).broadcast_to((P, 2, n))

        MARKS.append(("L1gnn", len(T.items)))
        lt = ln(x3, xn3, D, xt)
        xtt = to_T(xn3, KT, XT, pair(lt))
        xl = wk(0, m=2, f=1024)
        xlt = []
        for c in range(2):
            w = load("g1W1", 3072, c)
            a, t = lin_node(tiles(XT, 6), xtt, tiles(wv(w, 0, 6, 512), 6), [w.tok], 512,
                            lambda m, c0, c1, p, t, c=c: copy(xl[:, m, c * 512:(c + 1) * 512], p, t))
            w.free = (t,)
            xlt += a
        rT = wk(2048, k=8, n=256)
        rt = []

        def skip1():
            for c in range(2):
                w = load("g1Wr1", 3072, c)
                wt = tiles(wv(w, 0, 6, 512), 6)
                for f in range(4):
                    b, o, t = lin_T(wt, f, tiles(XT, 6), [w.tok, *xtt])
                    r = act(rT[:, c * 4 + f, :], o, ACT.Identity, t, bias=col("g1br1", c * 4 + f, 1))
                    b.free = (r,)
                    rt.append(r)
                w.free = (t,)

        rs, rd = load_row("g1as1", 1024), load_row("g1ad1", 1024)
        o1 = wk(4096, m=2, f=1024)
        ot, t = gat(4, 256, xl, xlt, rs, rd, C13, NM13, [c1t], 6144, scale_evac(o1, 256),
                    during=skip1)
        rb = load_row("g1b1", 1024)
        t = tt(o1, o1, bcast2(rb, 1024), ALU.add, *ot, rb.tok)
        rb.free = (t,)
        lt = ln(o1, o1, 1024, [t])
        h1T = wk(0, k=8, n=256)
        nt = to_T(o1, 8, h1T, lt, evac=lambda k, p, t: act(
            h1T[:, k, :], p, ACT.Relu, t, *ot, bias=col("g1be1", k, 1), scale=col("g1g1", k, 1)))
        h1t = tt(h1T, h1T, rT, ALU.add, *nt, *rt)
        xl = wk(2048, m=2, f=768)
        ws = [load("g1W2", 3072, c) for c in range(2)]
        wt = [x for w in ws for x in tiles(wv(w, 0, 4, 768), 4)]
        xlt, t = lin_node(tiles(h1T, 8), [h1t], wt, [w.tok for w in ws], 768,
                          lambda m, c0, c1, p, t: copy(xl[:, m, c0:c1], p, t))
        for w in ws:
            w.free = (t,)
        r2 = []

        def skip2():
            ws = [load("g1Wr2", 3072, c) for c in range(2)]
            wt = [x for w in ws for x in tiles(wv(w, 0, 4, 768), 4)]
            rb = load_row("g1br2", 768)
            r2t, t = lin_node(tiles(h1T, 8), [h1t], wt, [w.tok for w in ws], 768,
                              lambda m, c0, c1, p, t: tt(x3[:, m, c0:c1], x3[:, m, c0:c1], p, ALU.add, t, *lt))
            for w in ws:
                w.free = (t,)
            r2t = tt(x3, x3, bcast2(rb, 768), ALU.add, *r2t, rb.tok)
            rb.free = (r2t,)
            r2.append(r2t)

        rs, rd = load_row("g1as2", 768), load_row("g1ad2", 768)
        o1 = wk(3584, m=2, f=768)
        ot, t = gat(1, 768, xl, xlt, rs, rd, C13, NM13, [c1t], 6144, scale_evac(o1, 768),
                    during=skip2)
        rb = load_row("g1b2", 768)
        t = tt(o1, o1, bcast2(rb, 768), ALU.add, *ot, rb.tok)
        rb.free = (t,)
        lt = ln(o1, o1, 768, [t])
        rb = load_row("g1g2", 768)
        t = tt(o1, o1, bcast2(rb, 768), ALU.mult, *lt, rb.tok)
        rb.free = (t,)
        rb = load_row("g1be2", 768)
        t = tt(o1, o1, bcast2(rb, 768), ALU.add, t, rb.tok)
        rb.free = (t,)
        t = tt(x3, x3, o1, ALU.add, t, *r2)
        xt = [t] + snapshot([t])

        lt8 = col("lt8").rearrange("p (e j) -> p e j", e=8)

        def top2(val, n, t):
            g = small(2 * n * n).rearrange("p (m e j) -> p m e j", m=2, e=n)
            q = small(2 * n * n).rearrange("p (m e j) -> p m e j", m=2, e=n)
            sel = small(2 * n).rearrange("p (m e) -> p m e", m=2)
            for m in range(2):
                vj = val[:, m, :].unsqueeze(1).broadcast_to((P, n, n))
                ve = val[:, m, :].unsqueeze(2).broadcast_to((P, n, n))
                a = tt(q[:, m, :, :], vj, ve, ALU.is_equal, t)
                a = tt(q[:, m, :, :], q[:, m, :, :], lt8[:, 0:n, 0:n], ALU.mult, a)
                b = tt(g[:, m, :, :], vj, ve, ALU.is_gt, t)
                b = tt(g[:, m, :, :], g[:, m, :, :], q[:, m, :, :], ALU.add, a, b)
                b = red(sel[:, m, :], g[:, m, :, :], ALU.add, b)
            return sel, ts(sel, sel, 2.0, None, ALU.is_lt, None, b)

        def gate_logits(wname, xT, xtt):
            b = bank()
            wvw = col(wname).rearrange("p (k e) -> p k e", k=6)
            for m in range(2):
                t = mm(b, b.t[:, 8 * m:8 * m + 8],
                       [(xT[:, k, m * P:(m + 1) * P], wvw[:, k, :]) for k in range(6)], xtt)
            return b, b.t[:, 0:16].rearrange("p (m e) -> p m e", m=2), t

        def softmax8(z, t):
            mx, sm = small(2), small(2)
            t = red(mx, z, ALU.max, t)
            t = tt(z, z, mx.unsqueeze(2).broadcast_to((P, 2, 8)), ALU.subtract, t)
            t = act(z, z, ACT.Exp, t)
            return sm, t

        def norm8(z, w, sm, t):
            t = red(sm, w, ALU.add, t)
            t = V.do(lambda e: e.reciprocal(sm, sm), t)
            return tt(z, z, sm.unsqueeze(2).broadcast_to((P, 2, 8)), ALU.mult, t)

        def comb_T(comb, n, t, at):
            b = bank()
            for m in range(2):
                t2 = mm(b, b.t[0:n, m * P:(m + 1) * P], [(comb[:, m, :], ident)], [t])
            o = wk(at, n=256)
            r = V.do(lambda e: e.tensor_copy(o[0:n, :], b.t[0:n, 0:256]), t2)
            b.free = (r,)
            return o, r

        MARKS.append(("L1ffn", len(T.items)))
        lt = ln(x3, xn3, D, xt)
        xtt = to_T(xn3, KT, XT, pair(lt))
        b, z, t = gate_logits("f1Wr", XT, xtt)
        lg = small(16).rearrange("p (m e) -> p m e", m=2)
        t = V.do(lambda e, z=z: e.tensor_copy(lg, z), t)
        b.free = (t,)
        sel, t = top2(lg, 8, t)
        sm, t = softmax8(lg, t)
        t = tt(lg, lg, sel, ALU.mult, t)
        cbt = norm8(lg, lg, sm, t)
        comb = lg
        xt = [None] * 4

        def biases(comb, n, row):
            cT, cTt = comb_T(comb, n, cbt, 0)
            rb = load_row(row, 768, parts=n)
            for m in range(2):
                for ci, (c0, c1) in enumerate(((0, 512), (512, 768))):
                    b = bank()
                    t = mm(b, b.t[:, 0:c1 - c0], [(cT[0:n, m * P:(m + 1) * P], rb.ap[0:n, c0:c1])], [cTt, rb.tok])
                    xt[2 * m + ci] = tt(x3[:, m, c0:c1], x3[:, m, c0:c1], b.t[:, 0:c1 - c0], ALU.add, t, *lt)
                    b.free = (xt[2 * m + ci],)
            rb.free = (t,)

        gbuf = [wk(256 + 768 * i, k=3, n=256) for i in range(2)]
        gfree = [(), ()]
        pend = []

        def down(w, w2, gv, gt, comb, e, gi):
            idx = [0]

            def evac(m, c0, c1, p, t):
                i = idx[0]
                idx[0] += 1
                xv = x3[:, m, c0:c1]
                xt[i] = stt(xv, p, comb[:, m, e:e + 1], xv, ALU.mult, ALU.add, t, xt[i], cbt) if comb is not None \
                    else tt(xv, xv, p, ALU.add, t, xt[i])
                return xt[i]
            _, t = lin_node(tiles(gv, 3), gt, w2, [w.tok], 768, evac)
            gfree[gi] = (t,)
            w.free = (t,)

        for e in range(8):
            w = load("f1W", SLOT, e)
            w1 = tiles(wv(w, 0, 6, 384), 6)
            w2 = tiles(wv(w, 2304, 3, 768), 3)
            gv = gbuf[e % 2]
            gt = []
            for f in range(3):
                b, o, t = lin_T(w1, f, tiles(XT, 6), [w.tok, *xtt])
                r = act(gv[:, f, :], o, ACT.Gelu, t, *gfree[e % 2], bias=col("f1bi", e * 3 + f, 1))
                b.free = (r,)
                gt.append(r)
            if e == 0:
                biases(comb, 8, "f1bo")
            if pend:
                down(*pend.pop())
            pend.append((w, w2, gv, gt, comb, e, e % 2))
        down(*pend.pop())
        xt0 = list(xt) + snapshot(xt)

        MARKS.append(("L2gnn", len(T.items)))
        lt = ln(x3, xn3, D, xt0)
        xtt = to_T(xn3, KT, XT, pair(lt))
        xl = wk(0, m=2, f=1024)
        xlt = []
        for c in range(2):
            w = load("g2W1", 3072, c)
            a, t = lin_node(tiles(XT, 6), xtt, tiles(wv(w, 0, 6, 512), 6), [w.tok], 512,
                            lambda m, c0, c1, p, t, c=c: copy(xl[:, m, c * 512:(c + 1) * 512], p, t, *xt0[:4]))
            w.free = (t,)
            xlt += a
        rs, rd = load_row("g2as1", 1024), load_row("g2ad1", 1024)
        o1 = wk(2048, m=2, f=1024)
        ot, t = gat(8, 128, xl, xlt, rs, rd, Cn3, NM3, [nmt], 6144, scale_evac(o1, 128))
        rb = load_row("g2b1", 1024)
        t = tt(o1, o1, bcast2(rb, 1024), ALU.add, *ot, rb.tok)
        rb.free = (t,)
        h1T = wk(4096, k=8, n=256)
        nt = to_T(o1, 8, h1T, [t], evac=lambda k, p, t: act(h1T[:, k, :], p, ACT.Relu, t))
        xl = wk(0, m=2, f=768)
        ws = [load("g2W2", 3072, c) for c in range(2)]
        wt = [x for w in ws for x in tiles(wv(w, 0, 4, 768), 4)]
        xlt, t = lin_node(tiles(h1T, 8), nt, wt, [w.tok for w in ws], 768,
                          lambda m, c0, c1, p, t: copy(xl[:, m, c0:c1], p, t, *ot))
        for w in ws:
            w.free = (t,)
        rs, rd = load_row("g2as2", 768), load_row("g2ad2", 768)
        o1 = wk(2048, m=2, f=768)
        ot, t = gat(1, 768, xl, xlt, rs, rd, Cn3, NM3, [nmt], 6144, scale_evac(o1, 768))
        rb = load_row("g2b2", 768)
        t = tt(o1, o1, bcast2(rb, 768), ALU.add, *ot, rb.tok)
        rb.free = (t,)
        t = tt(x3, x3, o1, ALU.add, t)
        xt0 = [t] + snapshot([t])

        MARKS.append(("L2ffn", len(T.items)))
        lt = ln(x3, xn3, D, xt0)
        xtt = to_T(xn3, KT, XT, pair(lt))
        b, z, t = gate_logits("f2gw", XT, xtt)
        sc = small(16).rearrange("p (m e) -> p m e", m=2)
        t = V.do(lambda e, z=z: e.tensor_copy(sc, z), t)
        b.free = (t,)
        sm, t = softmax8(sc, t)
        t = norm8(sc, sc, sm, t)
        sg = small(16).rearrange("p (m e) -> p m e", m=2)
        t = tt(sg, sc, col("f2gb").unsqueeze(1).broadcast_to((P, 2, 8)), ALU.add, t)
        gs = small(8).rearrange("p (m g) -> p m g", m=2)
        t = red(gs, sg.rearrange("p m (g a) -> p m g a", a=2), ALU.add, t)
        keep, t = top2(gs, 4, t)
        t = ts(keep, keep, 1.0, -BIG, ALU.subtract, ALU.mult, t)
        for m in range(2):
            t = tt(sg[:, m, :].rearrange("p (g a) -> p g a", a=2), sg[:, m, :].rearrange("p (g a) -> p g a", a=2),
                   keep[:, m, :].unsqueeze(2).broadcast_to((P, 4, 2)), ALU.add, t)
        sel, t = top2(sg, 8, t)
        comb9 = small(18).rearrange("p (m e) -> p m e", m=2)
        t = V.do(lambda e: e.memset(comb9[:, :, 8:9], 1.0), t)
        cbt = tt(comb9[:, :, 0:8], sc, sel, ALU.mult, t)
        xt[:] = [None] * 4
        hb = [wk(256 + 3072 * i, k=6, n=256) for i in range(2)]
        sb2 = [wk(256 + 3072 * i + 1536, k=3, n=256) for i in range(2)]
        gb2 = [wk(256 + 3072 * i + 2304, k=3, n=256) for i in range(2)]
        gfree[:] = [(), ()]
        hfree = [(), ()]
        pend = []
        for e in range(9):
            i = e % 2
            n1, n3 = ("f2Ws1", "f2Ws3") if e == 8 else ("f2W1", "f2W3")
            wa = load(n1, SLOT, None if e == 8 else e)
            wb = load(n3, SLOT, None if e == 8 else e)
            wta, wtb = tiles(wv(wa, 0, 6, 768), 6), tiles(wv(wb, 0, 6, 768), 6)
            b1 = (lambda f: col("f2Bs1", f, 1)) if e == 8 else (lambda f, e=e: col("f2B1", e * 6 + f, 1))
            b3 = (lambda f: col("f2Bs3", f, 1)) if e == 8 else (lambda f, e=e: col("f2B3", e * 6 + f, 1))
            H = hb[i]
            r1 = []
            for f in range(6):
                b, o, t = lin_T(wta, f, tiles(XT, 6), [wa.tok, *xtt])
                r = act(H[:, f, :], o, ACT.Identity, t, *hfree[i], bias=b1(f))
                b.free = (r,)
                r1.append(r)
            wa.free = (t,)
            if pend:
                down(*pend.pop())
            r3 = []
            for f in range(6):
                b, o, t = lin_T(wtb, f, tiles(XT, 6), [wb.tok])
                r = stt(H[:, f, :], o, b3(f), H[:, f, :], ALU.add, ALU.mult, t, r1[f])
                b.free = (r,)
                r3.append(r)
            wb.free = (t,)
            hg, hl, sg_, gv = H[:, 0:3, :], H[:, 3:6, :], sb2[i], gb2[i]
            t = ts(hg, hg, 7.0, None, ALU.min, None, *r3)
            t1 = act(sg_, hg, ACT.Sigmoid, t, *hfree[i], scale=1.702)
            t = ts(hl, hl, 7.0, -7.0, ALU.min, ALU.max, *r3)
            t = V.do(lambda e_, hl=hl, hg=hg: e_.scalar_tensor_tensor(
                out=hl, in0=hl, scalar=1.0, in1=hg, op0=ALU.add, op1=ALU.mult), t, t1)
            t = tt(gv, hl, sg_, ALU.mult, t, t1, *gfree[i])
            hfree[i] = (t,)
            if e == 0:
                biases(comb9, 9, "f2B2")
            wc = load("f2Ws2" if e == 8 else "f2W2", 2304, None if e == 8 else e)
            pend.append((wc, tiles(wv(wc, 0, 3, 768), 3), gv, [t], comb9 if e < 8 else None, e, i))
        down(*pend.pop())
        xt = list(xt) + snapshot(xt)

        MARKS.append(("L3gnn", len(T.items)))
        lt = ln(x3, xn3, D, xt)
        xtt = to_T(xn3, KT, XT, pair(lt))
        ft = wk(0, m=2, f=768)
        res = wk(1536, m=2, f=768)
        BD = col("g3BD")
        ftt = []
        rtt = []
        for m in range(2):
            for k in range(6):
                if k % 2 == 0:
                    b = bank()
                h = (k % 2) * 256
                t = mm(b, b.t[:, h:h + 256], [(XT[:, k, m * P:(m + 1) * P], BD)], [*xtt, ctok])
                if k % 2:
                    pv = b.t[:, :].rearrange("p (k a n) -> p k a n", k=2, a=2)
                    c0 = (k - 1) * P
                    fo = ft[:, m, c0:c0 + 256].rearrange("p (k n) -> p k n", k=2)
                    ro = res[:, m, c0:c0 + 256].rearrange("p (k n) -> p k n", k=2)
                    t1 = act(fo, pv[:, :, 0, :], ACT.Copy, t, *xt[:4])
                    t2 = V.do(lambda e, ro=ro, pv=pv: e.tensor_copy(ro, pv[:, :, 1, :]), t, t1, *xt[:4])
                    b.free = (t1, t2)
                    ftt.append(t1)
                    rtt.append(t2)
        rs, rd = load_row("g3al", 768), load_row("g3ar", 768)
        o1 = wk(3072, m=2, f=768)
        ot, t = gat(12, 64, ft, ftt, rs, rd, Cn3, NM3, [nmt], 4608, scale_evac(o1, 64))
        t = tt(o1, o1, res, ALU.add, *ot, *rtt)
        t = ts(o1, o1, 0.0, None, ALU.max, None, t)
        t = tt(x3, x3, o1, ALU.add, t)
        xt = [t] + snapshot([t])

        MARKS.append(("L3ffn", len(T.items)))
        lt = ln(x3, xn3, D, xt)
        xtt = to_T(xn3, KT, XT, pair(lt))
        b, z, t = gate_logits("f3gw", XT, xtt)
        pr = small(16).rearrange("p (m e) -> p m e", m=2)
        t = tt(pr, z, col("f3gb").unsqueeze(1).broadcast_to((P, 2, 8)), ALU.add, t)
        b.free = (t,)
        sm, t = softmax8(pr, t)
        t = norm8(pr, pr, sm, t)
        sel, t = top2(pr, 8, t)
        t = tt(pr, pr, sel, ALU.mult, t)
        t = ts(pr, pr, 2.0, None, ALU.mult, None, t)
        wl = load("f3lora", 3072)
        A6 = tiles(wv(wl, 0, 6, 128), 6)
        ad = wk(0, m=2, f=128)
        adt = []
        for m in range(2):
            b = bank()
            t2 = mm(b, b.t[:, 0:P], [(XT[:, k, m * P:(m + 1) * P], A6[k]) for k in range(6)], [*xtt, wl.tok])
            r = tt(ad[:, m, :].rearrange("p (n r) -> p n r", n=8),
                   b.t[:, 0:P].rearrange("p (n r) -> p n r", n=8),
                   pr[:, m, :].unsqueeze(2).broadcast_to((P, 8, 16)), ALU.mult, t2, t)
            b.free = (r,)
            adt.append(r)
        adT = wk(256, n=256)
        b = bank()
        for m in range(2):
            t2 = tr(b, b.t[:, m * P:(m + 1) * P], ad[:, m, :], (adt[m],))
        adTt = V.do(lambda e, b=b: e.tensor_copy(adT, b.t[:, 0:256]), t2)
        b.free = (adTt,)
        LB = wl.ap[:, 768:3072]
        qA, kA = wk(512, k=6, n=256), wk(2048, k=6, n=256)
        vA = wk(3584, m=2, f=768)
        qk = []
        for j, (dst, bc) in enumerate(((qA, "f3bq"), (kA, "f3bk"))):
            w = load("f3Wqkv", SLOT, j)
            wt = tiles(wv(w, 0, 6, 768), 6) + [LB[:, j * 768:(j + 1) * 768]]
            for f in range(6):
                b, o, t = lin_T(wt, f, tiles(XT, 6) + [adT], [w.tok, *xtt, adTt])
                r = act(dst[:, f, :], o, ACT.Identity, t, bias=col(bc, f, 1))
                b.free = (r,)
                qk.append(r)
            w.free = (t,)
        w = load("f3Wqkv", SLOT, 2)
        rb = load_row("f3bv", 768)
        vt, t = lin_node(tiles(XT, 6) + [adT], [*xtt, adTt], tiles(wv(w, 0, 6, 768), 6) + [LB[:, 1536:2304]],
                         [w.tok], 768,
                         lambda m, c0, c1, p, t: tt(vA[:, m, c0:c1], p, rb.ap[:, c0:c1], ALU.add, t, rb.tok))
        w.free, wl.free, rb.free = (t,), (t,), tuple(vt)
        ct = wk(5120, k=6, n=256)
        ctt = attention(qA, kA, vA, [*qk, *vt], 6656, lambda k, p, t: copy(ct[:, k, :], p, t))
        w = load("f3Wp", SLOT)
        rb = load_row("f3bp", 768)
        t = tt(x3, x3, bcast2(rb, 768), ALU.add, rb.tok, *lt)
        xt, t = lin_node(tiles(ct, 6), ctt, tiles(wv(w, 0, 6, 768), 6), [w.tok], 768,
                         lambda m, c0, c1, p, tk, t=t: tt(x3[:, m, c0:c1], x3[:, m, c0:c1], p, ALU.add, tk, t))
        snapshot(xt)
        L.dma(lambda e: e.dma_start(out.rearrange("(m p) f -> p m f", p=P), x3), s_out, *xt)
        L.quiet(lambda e: e.wait_ge(s_out, 16))
        if dbg is not None:
            L.quiet(lambda e: e.wait_ge(s_dbg, 16 * ndbg[0]))

        MARKS.append(("end", len(T.items)))
        block = ctx.enter_context(nc.Block())

        @block.sync
        def _(e):
            L.emit(e)

        @block.scalar
        def _(e):
            S.emit(e)

        @block.vector
        def _(e):
            V.emit(e)

        @block.gpsimd
        def _(e):
            G.emit(e)

        @block.tensor
        def _(e):
            T.emit(e)


def _lay(i):
    import numpy as np

    def W(w):
        k, n = w.shape
        return w.reshape(k // P, P, n).transpose(1, 0, 2).reshape(P, -1)

    def C(v):
        return np.asarray(v).reshape(-1, P).T

    def wide(v):
        v = np.asarray(v).reshape(-1)
        return np.broadcast_to(v, (P, v.size))

    a = {}
    i = {k: np.asarray(v) for k, v in i.items()}
    a["x"] = i["x"]
    a["edges"] = np.concatenate([i[k].reshape(P, NEDGE_T) for k in ("src", "dst", "edge_type_3")], 1)
    a["queries"] = W(i["L0_gnn_query_embs"].reshape(512, D).T)
    for n in ("1", "2"):
        a["Wrel" + n] = np.stack([W(w) for w in i["L0_gnn_W_rel" + n]])
        a["Wroot" + n] = W(i["L0_gnn_W_root" + n])
    a["Wgh"], a["Wgq"] = W(i["L0_gnn_Wg"][:, :D].T), W(i["L0_gnn_Wg"][:, D:].T)
    a["Wqh"], a["Wqq"] = W(i["L0_gnn_Wq"][:, :D].T), W(i["L0_gnn_Wq"][:, D:].T)
    for n in "qkvom":
        a["f0W" + n] = W(i["L0_ffn_W" + n])
    a["f0W12"] = np.concatenate([W(i["L0_ffn_W1"]), W(i["L0_ffn_W2"])], 1)
    a["f0bv"], a["f0bf2"] = i["L0_ffn_bv"], i["L0_ffn_bf2"]
    a["f0bom"] = np.stack([i["L0_ffn_bo"], i["L0_ffn_bm"]])
    for n in ("W1", "Wr1"):
        a["g1" + n] = np.stack([W(i["L1_gnn_" + n][:, c * 512:(c + 1) * 512]) for c in range(2)])
    for n in ("W2", "Wr2"):
        a["g1" + n] = np.stack([W(i["L1_gnn_" + n][c * 512:(c + 1) * 512]) for c in range(2)])
    for n, m in (("as1", "a_src1"), ("ad1", "a_dst1"), ("as2", "a_src2"), ("ad2", "a_dst2"), ("b1", "b1"),
                 ("b2", "b2"), ("g2", "g2"), ("be2", "be2"), ("br2", "br2")):
        a["g1" + n] = i["L1_gnn_" + m].reshape(-1)
    a["f1W"] = np.stack([np.concatenate([W(p.T), W(q.T)], 1) for p, q in zip(i["L1_ffn_Wi"], i["L1_ffn_Wo"])])
    a["f1bo"] = i["L1_ffn_bo"]
    a["g2W1"] = np.stack([W(i["L2_gnn_W1"].T[:, c * 512:(c + 1) * 512]) for c in range(2)])
    a["g2W2"] = np.stack([W(i["L2_gnn_W2"].T[c * 512:(c + 1) * 512]) for c in range(2)])
    for n, m in (("as1", "att_src1"), ("ad1", "att_dst1"), ("as2", "att_src2"), ("ad2", "att_dst2"),
                 ("b1", "b1"), ("b2", "b2")):
        a["g2" + n] = i["L2_gnn_" + m].reshape(-1)

    def eo(w):
        return np.concatenate([w[..., ::2], w[..., 1::2]], -1)

    a["f2W1"] = np.stack([W(eo(w)) for w in i["L2_ffn_W1"]])
    a["f2W3"] = np.stack([W(eo(w)) for w in i["L2_ffn_W3"]])
    a["f2W2"] = np.stack([W(w) for w in i["L2_ffn_W2"]])
    a["f2Ws1"], a["f2Ws3"] = W(eo(i["L2_ffn_Ws1"])), W(eo(i["L2_ffn_Ws3"]))
    a["f2Ws2"] = W(i["L2_ffn_Ws2"])
    a["f2B2"] = np.concatenate([i["L2_ffn_B2"], i["L2_ffn_Bs2"][None]])
    a["g3al"], a["g3ar"] = i["L3_gnn_attn_l"].reshape(-1), i["L3_gnn_attn_r"].reshape(-1)
    a["f3lora"] = np.concatenate([W(i["L3_ffn_A"].reshape(128, D).T),
                                  i["L3_ffn_B_lora"].transpose(0, 2, 1).reshape(128, 3 * D)], 1)
    a["f3Wqkv"] = np.stack([W(i["L3_ffn_W_qkv"][c * D:(c + 1) * D].T) for c in range(3)])
    a["f3bv"], a["f3bp"] = i["L3_ffn_b_qkv"][2 * D:], i["L3_ffn_b_proj"]
    a["f3Wp"] = W(i["L3_ffn_W_proj"].T)
    BD = np.zeros((P, 256), np.float32)
    for s in range(2):
        BD[s * 64:(s + 1) * 64, s * 64:(s + 1) * 64] = i["L3_gnn_W"].T
        BD[s * 64:(s + 1) * 64, 128 + s * 64:128 + (s + 1) * 64] = i["L3_gnn_W_res"].T
    c = {
        "g0b1": C(i["L0_gnn_b1"]), "g0b2": C(i["L0_gnn_b2"]), "g0bg": C(i["L0_gnn_bg"]), "g0bq": C(i["L0_gnn_bq"]),
        "f0g1": C(i["L0_ffn_g1"]), "f0b1": C(i["L0_ffn_b1"]), "f0g2": C(i["L0_ffn_g2"]), "f0b2": C(i["L0_ffn_b2"]),
        "f0Wr": C(i["L0_ffn_Wr"]), "f0bq": C(i["L0_ffn_bq"]), "f0bk": C(i["L0_ffn_bk"]),
        "f0bf1": C(i["L0_ffn_bf1"]), "f0br": wide(i["L0_ffn_br"]),
        "g1g1": C(i["L1_gnn_g1"]), "g1be1": C(i["L1_gnn_be1"]), "g1br1": C(i["L1_gnn_br1"]),
        "f1bi": C(i["L1_ffn_bi"]), "f1Wr": W(i["L1_ffn_Wr"].T),
        "f2gw": W(i["L2_ffn_gate_w"].T), "f2gb": wide(i["L2_ffn_gate_b"]),
        "f2B1": C(eo(i["L2_ffn_B1"])), "f2B3": C(eo(i["L2_ffn_B3"])),
        "f2Bs1": C(eo(i["L2_ffn_Bs1"])), "f2Bs3": C(eo(i["L2_ffn_Bs3"])),
        "g3BD": BD, "f3bq": C(i["L3_ffn_b_qkv"][:D]), "f3bk": C(i["L3_ffn_b_qkv"][D:2 * D]),
        "f3gw": W(i["L3_ffn_W_gate"].T), "f3gb": wide(i["L3_ffn_b_gate"]),
        "ident": np.eye(P, dtype=np.float32), "iota": wide(np.arange(768, dtype=np.float32)),
        "pidx": np.arange(256, dtype=np.float32).reshape(2, P).T,
        "eps": np.full((P, 1), 1e-5, np.float32),
        "lt8": wide(np.tril(np.ones((8, 8), np.float32), -1)),
    }
    a["cols"] = np.concatenate([c[n] for n in COLS], 1).astype(np.float32)
    assert a["cols"].shape == (P, NCOL)
    return {k: np.ascontiguousarray(v) for k, v in a.items()}


DEBUG = False


def kernel(**inputs):
    import concourse.bacc as _bacc
    from concourse.bass_utils import run_bass_kernel_spmd as _run

    nc = _bacc.Bacc("TRN2", target_bir_lowering=False, num_devices=1)
    arrays = _lay(inputs)
    dr = {k: nc.dram_tensor(k + "_in", v.shape, mybir.dt.from_np(v.dtype), kind="ExternalInput").ap()
          for k, v in arrays.items()}
    out = nc.dram_tensor("out", (N, D), F32, kind="ExternalOutput").ap()
    dbg = nc.dram_tensor("dbg", (8, N, D), F32, kind="ExternalOutput").ap() if DEBUG else None
    build(nc, dr, out, dbg)
    r = _run(nc, [{k + "_in": v for k, v in arrays.items()}], core_ids=[0])
    return r.results[0]["out"]
```

```python
from contextlib import ExitStack

import concourse.bass as bass
from concourse import mybir

P = 128
F32 = mybir.dt.float32
BF16 = mybir.dt.bfloat16
FR = mybir.dt.float32r
I32 = mybir.dt.int32
I16 = mybir.dt.int16
ALU = mybir.AluOpType
ACT = mybir.ActivationFunctionType
AX = mybir.AxisListType

N = 256
D = 768
KT = 6
NRAW = 6
TILE = 768
UNIT = 3 * TILE
NPAIR = 4
NROW = 3
BIG = -1.0e30
NEDGE_T = 32
WARM = (14, 8, 8, 8, 8)
GADD = 6
GPE = (0,1,2,3,4,5,6,7)

COLS = {}


def _cols():
    at = 0
    for name, n in [
        ("g0b1", 6), ("g0b2", 6), ("g0bg", 6), ("g0bq", 6),
        ("f0g1", 6), ("f0b1", 6), ("f0g2", 6), ("f0b2", 6), ("f0Wr", 6), ("f0bq", 6), ("f0bk", 6),
        ("f0bf1", 3), ("f0br", 1),
        ("g1g1", 8), ("g1be1", 8), ("g1br1", 8),
        ("f1bi", 24), ("f1Wr", 48),
        ("f2gw", 48), ("f2gb", 8), ("f2B1", 48), ("f2B3", 48), ("f2Bs1", 6), ("f2Bs3", 6),
        ("g3BD", 256), ("f3bq", 6), ("f3bk", 6), ("f3gw", 48), ("f3gb", 8),
        ("ident", 128), ("iota", 768), ("pidx", 2), ("lt8", 64), ("eps", 1),
    ]:
        COLS[name] = (at, n)
        at += n
    return at


NCOL = _cols()


class Queue:

    def __init__(self, sem):
        self.sem, self.count, self.items = sem, 0, []

    def do(self, fn, *after):
        self.count += 1
        self.items.append((after, fn, self.sem, 1))
        return (self.sem, self.count)

    def quiet(self, fn, *after):
        self.items.append((after, fn, None, 0))

    def dma(self, fn, sem, *after):
        self.items.append((after, fn, sem, 16))

    def emit(self, eng):
        seen = {}
        for after, fn, sem, inc in self.items:
            for s, v in after:
                if seen.get(id(s), 0) < v:
                    eng.wait_ge(s, v)
                    seen[id(s)] = v
            ins = fn(eng)
            if sem is not None:
                ins.then_inc(sem, inc)


class Bank:

    def __init__(self, t):
        self.t, self.free = t, ()


class Slot:
    def __init__(self, ap, sem):
        self.ap, self.sem, self.loads, self.free = ap, sem, 0, ()


def build(nc, dr, out):
    ctx = ExitStack()
    with ctx:
        def sb(name, n, dt=F32):
            return ctx.enter_context(nc.sbuf_tensor(name, [P, n], dt))

        def newsem(name):
            return ctx.enter_context(nc.semaphore(name))

        PS = ctx.enter_context(nc.psum_tensor("PS", [P, 4096], F32))
        banks = [Bank(PS[:, 512 * i:512 * (i + 1)]) for i in range(8)]
        ring = [Slot(sb(f"w{i}", UNIT), newsem(f"s_w{i}")) for i in range(NRAW)]
        WH, WL = sb("WH", NPAIR * TILE, FR), sb("WL", NPAIR * TILE, FR)
        rows = [Slot(sb(f"r{i}", 1024), newsem(f"s_r{i}")) for i in range(NROW)]
        X = sb("X", 1536)
        XN = sb("XN", 1536)
        XTt = sb("XT", 1536)
        cp = sb("cp", NCOL)
        Cn = sb("Cn", 512)
        NM = sb("NM", 512)
        C1 = sb("C1", 512)
        NM1 = sb("NM1", 512)
        AhTt = sb("AhT", 1536)
        SM = sb("SM", 2560)
        with nc.sbuf_tensor("pad", [P, 8192], F32), nc.sbuf_tensor("AS", [P, 3072], FR) as AS, \
                nc.sbuf_tensor("XS", [P, 3072], FR) as XS, nc.sbuf_tensor("GS", [P, 3072], FR) as GS:
            pass
        with nc.sbuf_tensor("pad8", [P, 13312], F32), nc.sbuf_tensor("HS", [P, 4096], FR) as HS:
            pass
        WK = sb("WK", 17408)

        s_v, s_s, s_g, s_t = newsem("s_v"), newsem("s_s"), newsem("s_g"), newsem("s_t")
        s_x, s_c, s_e, s_q, s_f, s_out = (newsem(n) for n in (
            "s_x", "s_c", "s_e", "s_q", "s_f", "s_out"))
        V, S, G, T, L = Queue(s_v), Queue(s_s), Queue(s_g), Queue(s_t), Queue(None)
        L2 = S

        x3 = X[:, :].rearrange("p (m f) -> p m f", m=2)
        xn3 = XN[:, :].rearrange("p (m f) -> p m f", m=2)
        XT = XTt[:, :].rearrange("p (k n) -> p k n", k=KT)
        AhT = AhTt[:, :].rearrange("p (r k n) -> p r k n", r=3, k=2)
        Cn3, NM3, C13, NM13 = (t[:, :].rearrange("p (m s) -> p m s", m=2) for t in (Cn, NM, C1, NM1))

        def col(name, i=0, n=None):
            a, w = COLS[name]
            return cp[:, a + i:a + i + (w - i if n is None else n)]

        ident = col("ident")
        sm_at = [0]

        def small(n):
            a = sm_at[0]
            sm_at[0] += n
            assert sm_at[0] <= 2560, sm_at[0]
            return SM[:, a:a + n]

        def wk(_at, **kw):
            n = 1
            for v in kw.values():
                n *= v
            names = list(kw)
            v = WK[:, _at:_at + n]
            if len(names) == 1:
                return v
            return v.rearrange("p (%s) -> p %s" % (" ".join(names), " ".join(names)),
                               **{k: kw[k] for k in names[:-1]})

        turn = [0, 0]

        def load(name, index, unit):
            s = ring[turn[0] % NRAW]
            turn[0] += 1
            src = dr[name] if index is None else dr[name][index]
            w = min(UNIT, src.shape[1] - unit * UNIT)
            src = src[:, unit * UNIT:unit * UNIT + w]
            L.dma(lambda e, s=s, src=src, w=w: e.dma_start(s.ap[:, 0:w], src), s.sem, *s.free)
            s.loads += 1
            s.tok = (s.sem, 16 * s.loads)
            return s

        class Tile:
            pass

        npair = [0]
        pairs_free = [()] * NPAIR

        class Stream:

            def __init__(self, names, split=True, after=(), low=None):
                self.todo, self.tiles, self.at, self.split, self.after = [], [], 0, split, tuple(after)
                self.unit, self.low = None, low or V
                npair[0] += npair[0] % 2
                for name, index, *eng in names:
                    n = dr[name].shape[-1] // TILE
                    self.todo += [(name, index, j, n, eng[0] if eng else self.low) for j in range(n)]

            def make(self):
                name, index, j, n, low = self.todo[len(self.tiles)]
                if j % 3 == 0:
                    self.unit = load(name, index, j // 3)
                u, o = self.unit, (j % 3) * TILE
                t = Tile()
                t.unit, t.last, t.raw, t.tok = u, j % 3 == 2 or j == n - 1, u.ap[:, o:o + TILE], u.tok
                if self.split:
                    i = npair[0] % NPAIR
                    npair[0] += 1
                    t.pair = i
                    h, l = WH[:, i * TILE:(i + 1) * TILE], WL[:, i * TILE:(i + 1) * TILE]
                    a = S.do(lambda e: e.activation(h, t.raw, ACT.Copy), u.tok, *pairs_free[i], *self.after)
                    a = low.do(lambda e: e.tensor_tensor(l, t.raw, h, ALU.subtract), a)
                    t.h, t.l, t.tok = h, l, a
                    if t.last:
                        u.free = (a,)
                self.tiles.append(t)

            def get(self, n=1):
                if self.split:
                    while len(self.tiles) < min(len(self.todo), self.at + NPAIR):
                        self.make()
                else:
                    while len(self.tiles) < self.at + n:
                        self.make()
                r = self.tiles[self.at:self.at + n]
                self.at += n
                return r

            def prime(self):
                if self.split:
                    while len(self.tiles) < min(len(self.todo), NPAIR - 1):
                        self.make()

            def done(self, tiles, tok):
                for t in tiles:
                    if self.split:
                        pairs_free[t.pair] = (tok,)
                    elif t.last:
                        t.unit.free = (tok,)

        def parts(w_is_left, wh, wl, x):
            if wl is None:
                return [(wh, x)] if w_is_left else [(x, wh)]
            xh, xl = x
            if w_is_left:
                return [(wh, xh), (wh, xl), (wl, xh)]
            return [(xh, wh), (xh, wl), (xl, wh)]

        def gemm_T(st, nf, kt, xs, after, evac, f0=0, ks=None):
            toks = []
            for f in range(f0, nf):
                (t,) = st.get()
                b = bank()
                n = 256
                pr_ = []
                for k in range(kt):
                    if st.split:
                        q = parts(True, t.h[:, k * P:(k + 1) * P], t.l[:, k * P:(k + 1) * P], xs(k))
                        if ks is not None and f == f0:
                            q[0] = (*q[0], *ks[k])
                        pr_ += q
                        n = xs(k)[0].shape[-1]
                    else:
                        pr_ += parts(True, t.raw[:, k * P:(k + 1) * P], None, xs(k))
                        n = xs(k).shape[-1]
                tk = mm(b, b.t[:, 0:n], pr_, [t.tok, *after])
                st.done([t], tk)
                r = evac(f, b.t[:, 0:n], tk)
                b.free = (r,)
                toks.append(r)
            return toks, tk

        def gemm_N(st, kt, xs, after, evac, nn=768, more=None, ks=None):
            toks = []
            hold = {}
            step = 256
            for c in range(0, nn, step):
                w = min(step, nn - c)
                tl = st.get(w // P if kt == 6 else 1)
                last = c + w >= nn
                for m in range(2):
                    h = c % 512
                    if h == 0:
                        hold[m] = bank()
                    b = hold[m]
                    pr_ = []
                    for k in range(kt):
                        def view(v):
                            if kt == 6:
                                return v.rearrange("p (t k c) -> p t k c", t=len(tl), k=6)[:, :, k, :]
                            return v.rearrange("p (k c) -> p k c", k=kt)[:, k, :]
                        ms = slice(m * P, (m + 1) * P)
                        i = tl[0].pair
                        wh = view(WH[:, i * TILE:(i + len(tl)) * TILE])
                        wl = view(WL[:, i * TILE:(i + len(tl)) * TILE])
                        x = xs(k)
                        q = parts(False, wh, wl, (x[0][:, ms], x[1][:, ms]))
                        if ks is not None and c == 0:
                            q[0] = (*q[0], *ks[k])
                        pr_ += q
                    if more is not None:
                        pr_ += more(m, c, c + w)
                    tk = mm(b, b.t[:, h:h + w], pr_, [*[t.tok for t in tl], *after])
                    if h + w == 512 or last:
                        c0 = c - h
                        r = evac(m, c0, c + w, b.t[:, 0:h + w], tk)
                        b.free = (r,)
                        toks.append(r)
                st.done(tl, tk)
            return toks, tk

        def load_row(name, width, parts=None):
            s = rows[turn[1] % NROW]
            turn[1] += 1
            if parts is None:
                L.dma(lambda e, s=s: e.dma_start(s.ap[:, 0:width], dr[name].partition_broadcast(P)), s.sem, *s.free)
            else:
                L.dma(lambda e, s=s: e.dma_start(s.ap[0:parts, 0:width], dr[name]), s.sem, *s.free)
            s.loads += 1
            s.tok = (s.sem, 16 * s.loads)
            return s

        bt = [0]

        def bank():
            b = banks[bt[0] % 8]
            bt[0] += 1
            return b

        def mm(b, o, pairs, after, first=True, last=True):
            n = len(pairs)
            tok = None
            for i, pr_ in enumerate(pairs):
                l, r = pr_[0], pr_[1]
                a = tuple(after) + tuple(b.free) if i == 0 else ()
                a += tuple(pr_[2:])
                fn = lambda e, l=l, r=r, st=(i == 0 and first), sp=(i == n - 1 and last): e.matmul(
                    o, l, r, start=st, stop=sp, skip_group_check=not (first and last))
                if i == n - 1:
                    tok = T.do(fn, *a)
                else:
                    T.quiet(fn, *a)
            return tok

        def tr(b, o, i, after):
            n = i.shape[0]
            return T.do(lambda e: e.transpose(o, i, ident[0:n, 0:n]), *after, *b.free)

        ev = [0]

        def copy(o, i, *after):
            ev[0] += 1
            if ev[0] % 2:
                return S.do(lambda e: e.activation(o, i, ACT.Copy), *after)
            return V.do(lambda e: e.tensor_copy(o, i), *after)

        def act(o, i, f, *after, bias=0.0, scale=1.0, accum=None):
            kw = dict(bias=bias, scale=scale)
            if accum is not None:
                kw["accum_out"] = accum
            return S.do(lambda e: e.activation(o, i, f, **kw), *after)

        def tt(o, a, b, op, *after, q=None):
            return (q or V).do(lambda e: e.tensor_tensor(o, a, b, op), *after)

        def ts(o, a, s1, s2, op0, op1, *after, q=None):
            if op1 is None:
                return (q or V).do(lambda e: e.tensor_scalar(o, a, s1, None, op0), *after)
            return (q or V).do(lambda e: e.tensor_scalar(o, a, s1, s2, op0, op1), *after)

        def stt(o, a, s, b, op0, op1, *after):
            return V.do(lambda e: e.scalar_tensor_tensor(out=o, in0=a, scalar=s, in1=b, op0=op0, op1=op1), *after)

        def red(o, a, op, *after, negate=None):
            if negate:
                return V.do(lambda e: e.tensor_reduce(o, a, AX.X, op, negate=True), *after)
            return V.do(lambda e: e.tensor_reduce(o, a, AX.X, op), *after)

        tiny = small(1)
        tinyt = (V.do(lambda e: e.memset(tiny, 1.0)),)

        def fetch(f):
            act(small(1), tiny, f, *tinyt)

        def warm(n):
            b = bank()
            for _ in range(n):
                t = T.do(lambda e: e.matmul(b.t[:, 0:256], ident, col("iota")[:, 0:256], start=True, stop=True),
                         *b.free)
            b.free = (t,)

        def ln(src, dst, F, after, dst_free=(), then=None):
            ag, rs, t = ln_stats(src, F, after)
            if then is not None:
                fetch(then)
            return [V.do(lambda e, m=m: e.tensor_scalar(
                dst[:, m, 0:F], src[:, m, 0:F], ag[:, m, 0:1], rs[:, m:m + 1], ALU.subtract, ALU.mult), t, *dst_free)
                for m in range(2)]

        early = {}

        def xstat(m, c0, c1, t):
            if not early:
                early["buf"] = [small(18), small(18)]
            for c in range(c0 // 256, c1 // 256):
                early[m, c] = V.do(lambda e, c=c, o=early["buf"][m]: e.bn_stats(
                    o[:, 6 * c:6 * c + 6], x3[:, m, 256 * c:256 * (c + 1)]), t)
            return t

        def ln_stats(src, F, after):
            fetch(ACT.Sqrt)
            ag = small(4).rearrange("p (m a) -> p m a", m=2)
            rs = small(2)
            if early:
                sts = early["buf"]
                tk = [[early[m, c] for c in range(3)] for m in range(2)]
                early.clear()
            else:
                half = F // 2
                sts = [small(12), small(12)]
                tk = [[V.do(lambda e, m=m, c=c: e.bn_stats(
                    sts[m][:, 6 * c:6 * c + 6], src[:, m, c * half:(c + 1) * half]), *per_tile(after, m))
                    for c in range(2)] for m in range(2)]
            for m in range(2):
                t = V.do(lambda e, m=m: e.bn_aggr(ag[:, m, :], sts[m]), *tk[m])
            t = act(rs, ag[:, :, 1], ACT.Sqrt, t, bias=col("eps"))
            t = V.do(lambda e: e.reciprocal(rs, rs), t)
            return ag, rs, t

        def per_tile(after, m):
            return after[m] if isinstance(after, tuple) else after

        def to_T(src, kt, dst, after, evac=None, dst_free=(), evac2=None):
            bs = [bank() for _ in range(kt // 2)]
            for m in range(2):
                for k in range(kt):
                    b, h = bs[k // 2], (k % 2) * 256
                    t = tr(b, b.t[:, h + m * P:h + (m + 1) * P], src[:, m, k * P:(k + 1) * P], per_tile(after, m))
                    if m and k % 2:
                        b.tok = t
            toks = []
            for k in range(0, kt, 2):
                b = bs[k // 2]
                if evac2 is not None:
                    r = evac2(k, b.t[:, :].rearrange("p (k n) -> p k n", k=2), b.tok)
                    b.free = (r,)
                    toks.append(r)
                elif evac is not None:
                    r = [evac(k + h, b.t[:, h * 256:h * 256 + 256], b.tok) for h in range(2)]
                    b.free = tuple(r)
                    toks += r
                else:
                    t = copy(dst[:, k:k + 2, :], b.t[:, :].rearrange("p (k n) -> p k n", k=2), b.tok, *dst_free)
                    b.free = (t,)
                    toks += [t, t]
            return toks

        ASv, XSv, GSv = (v[:, :].rearrange("p (a k n) -> p a k n", a=2, k=6) for v in (AS, XS, GS))

        HSv = HS[:, :].rearrange("p (a k n) -> p a k n", a=2, k=8)

        def split(h, l, src, *after, low=None):
            a = S.do(lambda e: e.activation(h, src, ACT.Copy), *after)
            return (low or V).do(lambda e: e.tensor_tensor(l, src, h, ALU.subtract), a)

        def to_split(k, p, t, *after):
            return split(XSv[:, 0, k, :], XSv[:, 1, k, :], p, t, *after)

        def xs_split(k):
            return XSv[:, 0, k, :], XSv[:, 1, k, :]

        def pair(lt, *more):
            return ([lt[0], *more], [lt[1], *more])

        ei = wk(16640, a=96).bitcast(I32)
        L.dma(lambda e: e.dma_start(ei, dr["edges"]), s_e)
        io16 = wk(16896, a=384).bitcast(I16)
        L.dma(lambda e: e.dma_start(io16, dr["iota16"]), s_e)
        L.dma(lambda e: e.dma_start(x3, dr["x"].rearrange("(m p) f -> p m f", p=P)), s_x)
        L.dma(lambda e: e.dma_start(cp[:, :], dr["cols"]), s_c)
        ctok = (s_c, 16)
        qT = wk(0, k=6, n=512)
        L.dma(lambda e: e.dma_start(wk(0, n=3072), dr["queries"]), s_q)

        qh, ql = (v[:, :].rearrange("p (k n) -> p k n", k=6) for v in (AS, XS))
        sq = Stream([("Wgq", None)], after=[(s_q, 16)], low=G)
        sq.prime()
        qst = [split(qh[:, k, :], ql[:, k, :], qT[:, k, :], (s_q, 16), low=G) for k in range(6)]
        ef = wk(16736, a=96)
        et = V.do(lambda e: e.tensor_copy(ef, ei), (s_e, 32))
        dcode = wk(16832, a=32)
        et = stt(dcode, ef[:, 64:96], 256.0, ef[:, 32:64], ALU.mult, ALU.add, et)
        NB = 4
        oh = [wk(14592 + 512 * i, a=512).bitcast(BF16) for i in range(NB)]
        acc = [bank() for _ in range(6)]
        ufree = [()] * NB
        iota = col("iota")
        for c in range(NEDGE_T):
            u = oh[c % NB]
            t1 = ts(u[:, 0:256], io16[:, 0:256], ef[:, c:c + 1], None, ALU.is_equal, None, et, *ufree[c % NB])
            t2 = ts(u[:, 256:1024], io16, dcode[:, c:c + 1], None, ALU.is_equal, None, et, *ufree[c % NB])
            for j in range(6):
                fn = lambda e, j=j, u=u, c=c: e.matmul(
                    acc[j].t[:, 0:256], u[:, 256 + j * P:256 + (j + 1) * P], u[:, 0:256],
                    start=(c == 0), stop=(c == NEDGE_T - 1))
                fr = acc[j].free if c == 0 else ()
                if j == 5:
                    t = T.do(fn, t1, t2, *fr)
                else:
                    T.quiet(fn, t1, t2, *fr)
            ufree[c % NB] = (t,)
        Cr = wk(6144, r=3, m=2, n=256)
        cnt = small(6)
        crt = []
        for j in range(6):
            r, m = divmod(j, 2)
            a = copy(Cr[:, r, m, :], acc[j].t[:, 0:256], t)
            acc[j].free = (a,)
            crt.append(a)
        lt = ln(x3, xn3, D, [(s_x, 16), ctok])
        qgT = wk(3072, k=6, n=512)

        def query_gates(f0, f1):
            return gemm_T(sq, f1, 6, lambda k: (qh[:, k, :], ql[:, k, :]), qst, lambda f, p, t: act(
                qgT[:, f, :], p, ACT.Identity, t, ctok, bias=col("g0bg", f, 1)), f0=f0)

        qgt, _ = query_gates(0, 4)
        a = red(cnt, wk(6144, j=6, n=256), ALU.add, *crt)
        a = tt(Cn3, Cr[:, 0, :, :], Cr[:, 1, :, :], ALU.add, *crt)
        ctot = tt(Cn3, Cn3, Cr[:, 2, :, :], ALU.add, a)
        a = ts(cnt, cnt, 1.0, None, ALU.max, None, ctot)
        a = V.do(lambda e: e.reciprocal(cnt, cnt), a)
        Cj = wk(6144, j=6, n=256)
        a = tt(Cj, Cj, cnt.unsqueeze(2).broadcast_to((P, 6, 256)), ALU.mult, a)
        aht = []
        for r in range(3):
            b = bank()
            for k in range(2):
                for m in range(2):
                    t = tr(b, b.t[:, k * 256 + m * P:k * 256 + (m + 1) * P], Cr[:, r, m, k * P:(k + 1) * P], (a,))
            t = copy(AhT[:, r, :, :], b.t[:, :].rearrange("p (k n) -> p k n", k=2), t)
            b.free = (t,)
            aht.append(t)
        xtt = to_T(xn3, KT, XT, pair(lt, ctok))
        u, qglast = query_gates(4, 6)
        qgt += u
        nmt = ts(NM[:, :], Cn[:, :], 0.0, BIG, ALU.is_equal, ALU.mult, ctot)
        t = V.do(lambda e: e.tensor_copy(C1[:, :], Cn[:, :]), ctot)
        for m in range(2):
            t = tt(C13[:, m, m * P:(m + 1) * P], C13[:, m, m * P:(m + 1) * P], ident, ALU.add, t, ctok)
        c1t = ts(NM1[:, :], C1[:, :], 0.0, BIG, ALU.is_equal, ALU.mult, t)

        hT = wk(6144, k=6, n=256)
        qiT = wk(7680, k=6, n=256)
        hgT = XN[:, :].rearrange("p (k n) -> p k n", k=KT)
        aT = XT
        NTB = 4
        TB = [wk(9216 + 2048 * i, n=32, l=64) for i in range(NTB)]
        SP3 = [PS[:, 1024 * (i + 1):1024 * (i + 2)].rearrange("p (n l) -> p n l", l=64) for i in range(3)]

        def split6(dst, src, *after):
            r = []
            for k in range(0, 6, 2):
                t = split(dst[:, 0, k:k + 2, :], dst[:, 1, k:k + 2, :], src[:, k:k + 2, :], *after)
                r += [[t], [t]]
            return r

        def rgcn_stream(i):
            return Stream([("Wroot" + i, None)] + [("Wrel" + i, r) for r in range(3)])

        def products(st, bs, first, last, x, after):
            toks = []
            for f in range(6):
                (w,) = st.get()
                b, h = bs[f // 2], (f % 2) * 256
                pr_ = [(k, q) for k in range(6) for q in parts(
                    True, w.h[:, k * P:(k + 1) * P], w.l[:, k * P:(k + 1) * P], (x[:, 0, k, :], x[:, 1, k, :]))]
                n = len(pr_)
                seen = -1
                for j, (k, q) in enumerate(pr_):
                    aft = []
                    if j == 0:
                        aft = [w.tok, *(b.free if first else ())]
                    if f == 0 and k != seen:
                        aft += after[k]
                        seen = k
                    fn = lambda e, b=b, h=h, q=q, a=(first and j == 0 and f % 2 == 0), z=(last and j == n - 1): \
                        e.matmul(b.t[:, h:h + 256], q[0], q[1], start=a, stop=z, skip_group_check=True)
                    if j == n - 1:
                        t = T.do(fn, *aft)
                    else:
                        T.quiet(fn, *aft)
                st.done([w], t)
                toks.append(t)
            return toks

        def rgcn(st, hN, hNt, hTin, hTt, bcol, out_free):
            def aggregate(r, dst, free):
                at = []
                for f in range(0, 6, 2):
                    b = bank()
                    for h in range(2):
                        t = mm(b, b.t[:, h * 256:(h + 1) * 256],
                               [(hN[:, k, (f + h) * P:(f + h + 1) * P], AhT[:, r, k, :]) for k in range(2)],
                               [*hNt, *aht])
                    t = split(dst[:, 0, f:f + 2, :], dst[:, 1, f:f + 2, :],
                              b.t[:, :].rearrange("p (k n) -> p k n", k=2), t, *free)
                    b.free = (t,)
                    at += [[t], [t]]
                return at

            xs = split6(ASv, hTin, *hTt, *out_free)
            a0 = aggregate(0, XSv, out_free)
            a1 = aggregate(1, GSv, out_free)
            bs = [bank() for _ in range(3)]
            products(st, bs, True, False, ASv, xs)
            t = products(st, bs, False, False, XSv, a0)
            a2 = aggregate(2, XSv, t[5:])
            products(st, bs, False, False, GSv, a1)
            t = products(st, bs, False, True, XSv, a2)
            toks = []
            for f in range(6):
                b, h = bs[f // 2], (f % 2) * 256
                r = act(hT[:, f, :], b.t[:, h:h + 256], ACT.Relu, t[f | 1], bias=col(bcol, f, 1))
                b.free = (r,)
                toks.append(split(GSv[:, 0, f, :], GSv[:, 1, f, :], hT[:, f, :], r))
            return toks

        def gate(sg, ht, xn_free, then):
            hgt = []

            def hg(f):
                (w,) = sg.get()
                b = banks[f % 2]
                pr_ = []
                for k in range(6):
                    q = parts(True, w.h[:, k * P:(k + 1) * P], w.l[:, k * P:(k + 1) * P],
                              (GSv[:, 0, k, :], GSv[:, 1, k, :]))
                    pr_ += [(*q[0], ht[k]), *q[1:]] if f == 0 else q
                t = mm(b, b.t[:, 0:256], pr_, [w.tok])
                sg.done([w], t)
                r = act(hgT[:, f, :], b.t[:, 0:256], ACT.Copy, t, *xn_free)
                b.free = (r,)
                hgt.append(r)
                return t

            tbf = [()] * NTB
            spf = [tuple(x for i in (2 * j + 2, 2 * j + 3) for x in banks[i].free) for j in range(3)]
            qit = [[] for _ in range(6)]
            prod, part = {}, {}
            NBK = 48

            def finish(i):
                f, bb = divmod(i, 8)
                dst = qiT[:, f, bb * 32:(bb + 1) * 32]
                if i in part:
                    b, t = part[i]
                    r = red(dst, b.t[:, 0:256].rearrange("p (n l) -> p n l", l=8), ALU.add, t)
                    b.free = (r,)
                else:
                    r = red(dst, TB[i % NTB], ALU.add, prod[i])
                    tbf[i % NTB] = (r,)
                qit[f].append(r)

            sums = {}

            def add(i):
                f, bb = divmod(i, 8)
                B = TB[i % NTB]
                hv = hgT[:, f, bb * 32:(bb + 1) * 32].unsqueeze(2).broadcast_to((P, 32, 64))
                qv = qgT[:, f, bb * 64:(bb + 1) * 64].unsqueeze(1).broadcast_to((P, 32, 64))
                sums[i] = tt(B, hv, qv, ALU.add, hgt[f], qgt[f], *tbf[i % NTB], q=V if i % GADD == GADD - 1 else G)

            def attend(i):
                f, bb = divmod(i, 8)
                B = TB[i % NTB]
                q2 = qT[:, f, bb * 64:(bb + 1) * 64].unsqueeze(1).broadcast_to((P, 16, 64))
                ta = sums.pop(i)
                for h in range(2):
                    j = (2 * i + h) % 3
                    Bh = B[:, 16 * h:16 * (h + 1), :]
                    t = act(SP3[j], Bh, ACT.Sigmoid, ta, *spf[j])
                    t = tt(Bh, SP3[j], q2, ALU.mult, t)
                    spf[j] = (t,)
                prod[i] = t

            hg(0)
            add(0)
            add(1)
            hg(1)
            attend(0)
            hg(2)
            hg(3)
            attend(1)
            hg(4)
            t = hg(5)
            tbf[2] = tbf[3] = (t,)
            sa = None
            for i in range(NBK):
                if i == 6:
                    sa = Stream([("Wqh", None), ("Wqq", None)])
                if i in (8, 14, 20):
                    sa.make()
                if i > 1:
                    attend(i)
                if i >= 2 and i - 2 in part:
                    finish(i - 2)
                if i % 8 not in GPE:
                    finish(i)
                else:
                    b = banks[i % 2]
                    B = TB[i % NTB]
                    t = mm(b, b.t[:, 0:256], [(ident, B[:, :, 8 * c:8 * (c + 1)]) for c in range(8)], [prod[i]])
                    tbf[i % NTB] = (t,)
                    part[i] = (b, t)
                if i + 2 < NBK:
                    add(i + 2)
            for i in (NBK - 2, NBK - 1):
                if i in part:
                    finish(i)
            for j in range(3):
                banks[2 * j + 2].free = banks[2 * j + 3].free = spf[j]
            hs = split6(XSv, hT, *tbf[1], *tbf[2])
            bs = [bank() for _ in range(3)]
            products(sa, bs, True, False, XSv, hs)
            qs = [[split(GSv[:, 0, k, :], GSv[:, 1, k, :], qiT[:, k, :], *qit[k], *tbf[2], *tbf[3])]
                  for k in range(6)]
            t = products(sa, bs, False, True, GSv, qs)
            gl = [x for y in qit for x in y]
            u = []
            for c in range(0, 6, 2):
                qv, hv = qiT[:, c:c + 2, :], hT[:, c:c + 2, :]
                r = act(qv, qv, ACT.Tanh, *qs[c], *qs[c + 1])
                u.append(tt(qv, qv, hv, ALU.subtract, r))
            then()
            r = []
            for c in range(0, 6, 2):
                qv, hv = qiT[:, c:c + 2, :], hT[:, c:c + 2, :]
                b = bs[c // 2]
                for h in range(2):
                    a = act(aT[:, c + h, :], b.t[:, h * 256:(h + 1) * 256], ACT.Sigmoid, t[c + 1],
                            bias=col("g0bq", c + h, 1))
                b.free = (a,)
                a = tt(qv, qv, aT[:, c:c + 2, :], ALU.mult, a, u[c // 2])
                r.append(tt(hv, hv, qv, ALU.add, a))
            return r, gl

        def to_nodes(r, evac):
            toks = []
            for c in range(3):
                b = bank()
                for m in range(2):
                    for k in range(2):
                        t = tr(b, b.t[:, m * 256 + k * P:m * 256 + (k + 1) * P],
                               hT[:, 2 * c + k, m * P:(m + 1) * P], (r[c],))
                t = evac(slice(c * 256, (c + 1) * 256), b.t[:, :].rearrange("p (m f) -> p m f", m=2), t)
                b.free = (t,)
                toks.append(t)
            return toks

        nxt = {}

        def start(name, st):
            nxt[name] = st
            st.prime()

        start("r1", rgcn_stream("1"))
        ht = rgcn(nxt["r1"], xn3, lt, XT, xtt, "g0b1", [qglast])
        r, gl = gate(Stream([("Wgh", None)]), ht, [], lambda: start("r2", rgcn_stream("2")))
        hnt = to_nodes(r, lambda c, p, t: copy(xn3[:, :, c], p, t))
        ht = rgcn(nxt["r2"], xn3, hnt, hT, r, "g0b2", gl)
        r, gl = gate(Stream([("Wgh", None)]), ht, [], lambda: None)

        def add_x(c, p, t):
            t = tt(x3[:, :, c], x3[:, :, c], p, ALU.add, t)
            for m in range(2):
                xstat(m, c.start, c.stop, t)
            return t

        xt = to_nodes(r, add_x)

        def attention(qTv, kTv, vv, after, E0, ctx_out, beside=None):
            Eb = [wk(E0 + 512 * i, m=2, n=256) for i in range(3)]
            Pb = [wk(E0 + 1536 + 512 * i, k=2, n=256) for i in range(3)]
            efree, pfree = [()] * 3, [()] * 3
            st = {}
            toks = []
            fetch(ACT.Exp)

            def scores(h):
                p, k = (h % 2) * 64, h // 2
                b = bank()
                for m in range(2):
                    t = mm(b, b.t[:, m * 256:(m + 1) * 256],
                           [(qTv[p:p + 64, k, m * P:(m + 1) * P], kTv[p:p + 64, k, :])], after)
                mx, sm = small(2), small(2)
                bv = b.t[:, :].rearrange("p (m n) -> p m n", m=2)
                t = red(mx, bv, ALU.max, t)
                t = ts(mx, mx, -0.125, None, ALU.mult, None, t)
                E = Eb[h % 3]
                for m in range(2):
                    t2 = act(E[:, m, :], bv[:, m, :], ACT.Exp, t, *efree[h % 3], bias=mx[:, m:m + 1], scale=0.125,
                             accum=sm[:, m:m + 1])
                b.free = (t2,)
                st[h] = (sm, t2)

            def scale(h):
                sm, t2 = st[h]
                E = Eb[h % 3]
                t = V.do(lambda e: e.reciprocal(sm, sm), t2)
                for m in range(2):
                    t3 = ts(E[:, m, :], E[:, m, :], sm[:, m:m + 1], None, ALU.mult, None, t)
                st[h] = t3

            def turn_p(h):
                b = bank()
                E = Eb[h % 3]
                for k in range(2):
                    for m in range(2):
                        t = tr(b, b.t[:, k * 256 + m * P:k * 256 + (m + 1) * P], E[:, m, k * P:(k + 1) * P],
                               (st[h],))
                efree[h % 3] = (t,)
                t = copy(Pb[h % 3], b.t[:, :].rearrange("p (k n) -> p k n", k=2), t, *pfree[h % 3])
                b.free = (t,)
                st[h] = t

            def mix(h):
                p = (h % 2) * 64
                if p == 0:
                    st["b"] = bank()
                b = st["b"]
                Pt = Pb[h % 3]
                t = mm(b, b.t[p:p + 64, 0:256],
                       [(vv[:, k, h * 64:(h + 1) * 64], Pt[:, k, :]) for k in range(2)], [st[h], *after])
                pfree[h % 3] = (t,)
                if p:
                    t = ctx_out(h // 2, b.t[:, 0:256], t)
                    b.free = (t,)
                    toks.append(t)

            for h in range(15):
                if h < 12:
                    scores(h)
                    if beside is not None:
                        beside(h)
                if 1 <= h < 13:
                    scale(h - 1)
                if 2 <= h < 14:
                    turn_p(h - 2)
                if h >= 3:
                    mix(h - 3)
            return toks

        def ups_downs(n, ups, downs):
            o = [ups[0]]
            for i in range(1, n):
                o += [ups[i], downs[i - 1]]
            return o + [downs[n - 1]]

        tl = [("f0Wq", None), ("f0Wk", None), ("f0Wv", None), ("f0Wom", None), ("f0W12", None),
              ("g1W1", None, G), ("g1Wr1", None, G), ("g1W2", None, G), ("g1Wr2", None, G)]
        tl += ups_downs(8, [("f1Wi", e) for e in range(8)], [("f1Wo", e) for e in range(8)])
        tl += [("g2W1", None, G), ("g2W2", None, G)]
        for e in range(9):
            tl.append(("f2W1", e) if e < 8 else ("f2Ws1", None))
            if e:
                tl.append(("f2W2", e - 1))
            tl.append(("f2W3", e) if e < 8 else ("f2Ws3", None))
        st = Stream(tl + [("f2Ws2", None)], after=xt)
        st.prime()
        lt = ln(x3, xn3, D, xt)
        warm(WARM[0])
        HN = wk(0, m=2, f=768)
        lt2 = ln(xn3, HN, D, lt, then=ACT.Sigmoid)
        warm(WARM[1])
        nT = XT

        def affine_split(src, after, g, be):
            r = []

            def f(k, p, t):
                for i in range(2):
                    if k == 2:
                        t = ts(nT[:, k + i, :], p[:, i, :], col(g, k + i, 1), col(be, k + i, 1), ALU.mult, ALU.add, t)
                    else:
                        t = act(nT[:, k + i, :], p[:, i, :], ACT.Identity, t, bias=col(be, k + i, 1),
                                scale=col(g, k + i, 1))
                r.append(t)
                return t
            to_T(src, KT, None, after, evac2=f)
            ks = []
            for k in range(0, 6, 2):
                t = split(XSv[:, 0, k:k + 2, :], XSv[:, 1, k:k + 2, :], nT[:, k:k + 2, :], r[k // 2])
                ks += [[t], [t]]
            return r, ks

        r, ks = affine_split(HN, pair(lt2), "f0g1", "f0b1")
        nt = [x for x in r for _ in range(2)]
        zb = bank()
        t = mm(zb, zb.t[:, 0:256], [(col("f0Wr", k, 1).broadcast_to((P, P)), nT[:, k, :]) for k in range(6)], nt)
        srow = wk(1536, n=256)
        srt = act(srow, zb.t[:, 0:256], ACT.Sigmoid, t, bias=col("f0br"))
        zb.free = (srt,)
        qA, kA = wk(3072, k=6, n=256), wk(4608, k=6, n=256)
        vA = wk(6144, m=2, f=768)
        qk, _ = gemm_T(st, 6, 6, xs_split, [], ks=ks, evac=lambda f, p, t: act(
            qA[:, f, :], p, ACT.Identity, t, bias=col("f0bq", f, 1)))
        b = bank()
        for m in range(2):
            t = tr(b, b.t[:, m * P:(m + 1) * P], srow[:, m * P:(m + 1) * P], (srt,))
        scol = small(2)
        t = V.do(lambda e, b=b: e.tensor_copy(scol, b.t[:, 0:256:128]), t)
        b.free = (t,)
        Gt = wk(1792, n=256)
        Qt = wk(2048, n=256)
        rk = small(2)
        mk2 = small(4)
        for m in range(2):
            sc = scol[:, m:m + 1]
            t = ts(Qt, iota[:, 0:256], col("pidx", m, 1), None, ALU.is_lt, None, t)
            t = stt(Qt, srow, sc, Qt, ALU.is_equal, ALU.mult, t)
            t = ts(Gt, srow, sc, None, ALU.is_lt, None, t)
            t = tt(Gt, Gt, Qt, ALU.add, t)
            t = red(rk[:, m:m + 1], Gt, ALU.add, t)
        mkv = mk2.rearrange("p (m a) -> p m a", m=2)
        t = ts(mkv[:, :, 0], rk, 38.0, None, ALU.is_lt, None, t)
        mkt = ts(mkv[:, :, 1], rk, 38.0, None, ALU.is_ge, None, t)
        a, _ = gemm_T(st, 6, 6, xs_split, [], lambda f, p, t: act(
            kA[:, f, :], p, ACT.Identity, t, bias=col("f0bk", f, 1)))
        qk += a
        b = bank()
        for m in range(2):
            for a in range(2):
                t = tr(b, b.t[:, a * 256 + m * P:a * 256 + (m + 1) * P],
                       mk2[:, 2 * m + a:2 * m + a + 1].broadcast_to((P, P)), (mkt,))
        mrow = wk(2304, a=2, n=256)
        mrt = V.do(lambda e, b=b: e.tensor_copy(wk(2304, n=512), b.t[:, :]), t)
        b.free = (mrt,)
        b = bank()
        for m in range(2):
            t = mm(b, b.t[0:2, m * P:(m + 1) * P], [(mk2[:, 2 * m:2 * m + 2], ident)], [mkt])
        mT = wk(2816, n=256)
        mtt = V.do(lambda e, b=b: e.tensor_copy(mT[0:2, :], b.t[0:2, 0:256]), t)
        b.free = (mtt,)
        rb = load_row("f0bv", 768)
        vt, vlast = gemm_N(st, 6, xs_split, [],
                           lambda m, c0, c1, p, t: tt(vA[:, m, c0:c1], p, rb.ap[:, c0:c1], ALU.add, t, rb.tok))
        rb.free = tuple(vt)
        ssum, pool = small(1), small(6)
        mixT = wk(0, k=6, n=256)
        mix = {}

        def pooled(h):
            if h == 0:
                t = red(ssum, srow, ALU.add, srt)
                t = ts(ssum, ssum, 1e-6, None, ALU.add, None, t)
                mix["t"] = V.do(lambda e: e.reciprocal(ssum, ssum), t)
            if h < 6:
                mix["t"] = V.do(lambda e: e.tensor_tensor_reduce(
                    Gt, nT[:, h, :], srow, 1.0, 0.0, ALU.mult, ALU.add, pool[:, h:h + 1]), nt[h], mkt, mix["t"])
                return
            k = h - 6
            if k == 0:
                mix["t"] = ts(pool, pool, ssum, None, ALU.mult, None, mix["t"])
            stt(mixT[:, k, :], srow, pool[:, k:k + 1], nT[:, k, :], ALU.mult, ALU.add, mix["t"])
            t = (V.sem, V.count)
            if k == 5:
                t = tt(mixT, mixT, mrow[:, 1, :].unsqueeze(1).broadcast_to((P, 6, 256)), ALU.mult, t, mrt, q=G)
                mix["m"] = split(GSv[:, 0, :, :], GSv[:, 1, :, :], mixT, t, low=G)

        ctmp = [wk(10752 + 256 * i, n=256) for i in range(2)]
        cfree = [(), ()]

        def ctx_masked(k, p, t):
            c = ctmp[k % 2]
            r = tt(c, p, mrow[:, 0, :], ALU.mult, t, mrt, *cfree[k % 2])
            cs = to_split(k, c, r, vlast)
            cfree[k % 2] = (cs,)
            ctt.append(cs)
            return r

        ctt = []
        attention(qA, kA, vA, [*qk, *vt], 7680, ctx_masked, beside=pooled)
        mixt = mix["m"]
        rb = load_row("f0bom", 768, parts=2)
        hx = wk(0, m=2, f=768)
        toks = []
        ob = {}
        for c in range(0, 768, 256):
            to = st.get(2)
            h = c % 512
            if h == 0:
                ob = {m: bank() for m in range(2)}
            for part in range(2):
                if part:
                    to = st.get(2)
                src = (lambda k: xs_split(k)) if part == 0 else (lambda k: (GSv[:, 0, k, :], GSv[:, 1, k, :]))
                i = to[0].pair
                wh = WH[:, i * TILE:(i + 2) * TILE].rearrange("p (t k c) -> p t k c", t=2, k=6)
                wl = WL[:, i * TILE:(i + 2) * TILE].rearrange("p (t k c) -> p t k c", t=2, k=6)
                for m in range(2):
                    b = ob[m]
                    pr_ = []
                    for k in range(6):
                        x = src(k)
                        ms = slice(m * P, (m + 1) * P)
                        pr_ += parts(False, wh[:, :, k, :], wl[:, :, k, :], (x[0][:, ms], x[1][:, ms]))
                    o = b.t[:, h:h + 256]
                    if part == 0:
                        pr_ += [(mT[0:2, m * P:(m + 1) * P], rb.ap[0:2, c:c + 256], rb.tok, mtt)]
                    n = len(pr_)
                    for q, pp in enumerate(pr_):
                        fn = lambda e, pp=pp, o=o, a=(part == 0 and q == 0), z=(part == 1 and q == n - 1): e.matmul(
                            o, pp[0], pp[1], start=a, stop=z, skip_group_check=True)
                        aft = [*pp[2:]]
                        if q == 0:
                            aft += [*[x.tok for x in to], *(ctt if part == 0 else [mixt]), *b.free]
                        if q == n - 1:
                            t = T.do(fn, *aft)
                        else:
                            T.quiet(fn, *aft)
                    if part and (h + 256 == 512 or c == 512):
                        c0 = c - h
                        r = tt(hx[:, m, c0:c + 256], b.t[:, 0:h + 256], xn3[:, m, c0:c + 256], ALU.add, t, mixt)
                        b.free = (r,)
                        toks.append(r)
                st.done(to, t)
        rb.free = (t,)
        ot = toks
        lt = ln(hx, xn3, D, ot, then=ACT.Gelu)
        warm(WARM[2])
        _, ks = affine_split(xn3, pair(lt, t), "f0g2", "f0b2")
        gtmp = wk(3072, k=3, n=256)
        GH = [GS[:, 1536 * i:1536 * (i + 1)].rearrange("p (a k n) -> p a k n", a=2, k=3) for i in range(2)]

        def gelu_split(i, bias, *free):
            def f(k, p, t):
                t = act(gtmp[:, k, :], p, ACT.Gelu, t, bias=bias(k))
                return split(GH[i][:, 0, k, :], GH[i][:, 1, k, :], gtmp[:, k, :], t, *free)
            return f

        gt, _ = gemm_T(st, 3, 6, xs_split, [], gelu_split(0, lambda k: col("f0bf1", k, 1)), ks=ks)
        rb = load_row("f0bf2", 768)
        t = tt(x3, x3, hx, ALU.add, *ot)
        t = tt(x3, x3, rb.ap[:, 0:768].unsqueeze(1).broadcast_to((P, 2, 768)), ALU.add, t, rb.tok)
        rb.free = (t,)
        xt, t = gemm_N(st, 3, lambda k: (GH[0][:, 0, k, :], GH[0][:, 1, k, :]), gt, lambda m, c0, c1, p, tk, t=t: xstat(
            m, c0, c1, tt(x3[:, m, c0:c1], x3[:, m, c0:c1], p, ALU.add, tk, t)))

        def ttr(o, a, b, op0, op1, init, acc, *after):
            return V.do(lambda e: e.tensor_tensor_reduce(o, a, b, 1.0, init, op0, op1, acc), *after)

        def head_dots(xl, H, C, row_s, row_d, after, tmp, ready):
            res = []
            t = None
            if ready is not None:
                parted = H == 1
                if parted:
                    H, C = 3, C // 3
                ab = [small(2 * H).rearrange("p (m h) -> p m h", m=2) for _ in range(2)]
                used = [()] * (3072 // C)
                n_used = 0
                for h in range(H):
                    for m in range(2):
                        for a, row in zip(ab, (row_s, row_d)):
                            j, n = n_used % len(used), h * C
                            i = j * C
                            n_used += 1
                            t = ttr(tmp[:, i:i + C], xl[:, m, n:n + C], row.ap[:, n:n + C], ALU.mult, ALU.add, 0.0,
                                    a[:, m, h:h + 1], *ready(m, h), row.tok, *after, *used[j])
                            used[j] = (t,)
                row_s.free = row_d.free = (t,)
                if parted:
                    s1 = [small(2).rearrange("p (m h) -> p m h", m=2) for _ in range(2)]
                    return [(o, red(o[:, :, 0], a, ALU.add, t)) for o, a in zip(s1, ab)]
                return [(a, t) for a in ab]
            for i, row in enumerate((row_s, row_d)):
                a = small(2 * H).rearrange("p (m h) -> p m h", m=2)
                p = []
                for m in range(2):
                    x4 = xl[:, m, :].rearrange("p (h c) -> p h c", h=H)
                    r4 = row.ap[:, 0:H * C].rearrange("p (h c) -> p h c", h=H)
                    t4 = tmp[:, (2 * i + m) * H * C:(2 * i + m + 1) * H * C].rearrange("p (h c) -> p h c", h=H)
                    p.append((t4, tt(t4, x4, r4, ALU.mult, *after, row.tok, q=(V, G)[i])))
                row.free = (p[1][1],)
                res.append((a, p))
            return [(a, [red(a[:, m, :], p[m][0], ALU.add, p[m][1]) for m in range(2)][1]) for a, p in res]

        def gat(H, C, xl, xlt, row_s, row_d, Cm, NMm, cmt, E0, o_evac, free=(), during=None, ready=None):
            tmp = WK[:, E0:E0 + 3072]
            fetch(ACT.Exp)
            (asr, ast), (ads, adt) = head_dots(
                xl, H, C, row_s, row_d, [*(() if ready else xlt), *free], tmp, ready)
            if during is not None:
                during[0]()
            E = wk(E0, m=2, h=H, n=256)
            PT = [wk(E0 + 2 * H * 256 + 512 * i, k=2, n=256) for i in range(3)]
            F = [wk(E0 + 2 * H * 256 + 1536 + 512 * i, m=2, n=256) for i in range(3)]
            mx = small(2 * H).rearrange("p (m h) -> p m h", m=2)
            b1, b2, den = (small(2 * H).rearrange("p (m h) -> p m h", m=2) for _ in range(3))
            ready_h = {}

            def group(g0):
                g1 = min(H, g0 + 4)
                for h0 in range(g0, g1, 2):
                    h1 = min(g1, h0 + 2)
                    b = bank()
                    for h in range(h0, h1):
                        for k in range(2):
                            t = tr(b, b.t[:, (h - h0) * 256 + k * P:(h - h0) * 256 + (k + 1) * P],
                                   asr[:, k, h:h + 1].broadcast_to((P, P)), (ast, adt))
                    for h in range(h0, h1):
                        for m in range(2):
                            r = ttr(E[:, m, h, :], b.t[:, (h - h0) * 256:(h - h0 + 1) * 256], NMm[:, m, :], ALU.add,
                                    ALU.max, 3.0 * BIG, mx[:, m, h:h + 1], t, *cmt)
                    b.free = (r,)
                mg, ag_, b1g, b2g = (v[:, :, g0:g1] for v in (mx, ads, b1, b2))
                t = tt(mg, mg, ag_, ALU.add, r)
                t = stt(mg, mg, 0.2, mg, ALU.mult, ALU.max, t)
                t2 = stt(b2g, ag_, 0.2, mg, ALU.mult, ALU.subtract, t)
                t1 = tt(b1g, ag_, mg, ALU.subtract, t)
                for h in range(g0, g1):
                    ready_h[h] = (t1, t2, r)

            group(0)
            ffree, pfree = [()] * 3, [()] * 3
            pt, et = {}, {}
            per = max(1, min(4, 512 // C))
            toks = []
            hold = {}

            def soft(h):
                Fh = F[h % 3]
                for m in range(2):
                    act(Fh[:, m, :], E[:, m, h, :], ACT.Exp, *ready_h[h], *ffree[h % 3], bias=b1[:, m, h:h + 1])
                    et[h] = act(E[:, m, h, :], E[:, m, h, :], ACT.Exp, bias=b2[:, m, h:h + 1], scale=0.2)

            def weigh(h):
                Fh, a = F[h % 3], et[h]
                a = tt(E[:, :, h, :], E[:, :, h, :], Fh, ALU.max, a)
                ffree[h % 3] = (a,)
                for m in range(2):
                    et[h] = ttr(E[:, m, h, :], E[:, m, h, :], Cm[:, m, :], ALU.mult, ALU.add, 0.0,
                                den[:, m, h:h + 1], a)

            def turn_p(h):
                b = bank()
                for k in range(2):
                    for m in range(2):
                        t = tr(b, b.t[:, k * 256 + m * P:k * 256 + (m + 1) * P], E[:, m, h, k * P:(k + 1) * P],
                               (et[h],))
                t = copy(PT[h % 3], b.t[:, :].rearrange("p (k n) -> p k n", k=2), t, *pfree[h % 3])
                b.free = (t,)
                pt[h] = t

            def agg(h):
                Pt = PT[h % 3]
                j = h % per
                if j == per - 1 or h == H - 1:
                    dv = den[:, :, h - j:h + 1]
                    dt = ts(dv, dv, 1e-16, None, ALU.add, None, et[h])
                    dt = V.do(lambda e: e.reciprocal(dv, dv), dt)
                for m in range(2):
                    for c0 in range(0, C, 512):
                        c1 = min(C, c0 + 512)
                        if j == 0:
                            hold[m] = bank()
                        b = hold[m]
                        t = mm(b, b.t[:, j * C:j * C + c1 - c0],
                               [(Pt[:, k, m * P:(m + 1) * P], xl[:, k, h * C + c0:h * C + c1]) for k in range(2)],
                               [pt[h], *xlt])
                        if j == per - 1 or h == H - 1:
                            q = o_evac(m, h - j, h + 1, c0, c1, b.t[:, 0:j * C + c1 - c0], den[:, m, :], (t, dt))
                            b.free = (q,)
                            toks.append(q)
                pfree[h % 3] = (t,)

            soft(0)
            for h in range(H + 2):
                if h + 1 < H:
                    soft(h + 1)
                if h < H:
                    weigh(h)
                if h % 4 == 1 and h + 3 < H:
                    group(h + 3)
                if h == 0 and during is not None:
                    during[1]()
                if 1 <= h < H + 1:
                    turn_p(h - 1)
                if h >= 2:
                    agg(h - 2)
            return toks, t

        def scale_evac(dst, C):
            def f(m, h0, h1, c0, c1, p, den, toks):
                if c1 - c0 < C:
                    return V.do(lambda e: e.tensor_scalar(dst[:, m, c0:c1], p, den[:, h0:h0 + 1], None, ALU.mult),
                                *toks)
                n = h1 - h0
                return tt(dst[:, m, h0 * C:h1 * C].rearrange("p (h c) -> p h c", h=n),
                          p.rearrange("p (h c) -> p h c", h=n),
                          den[:, h0:h1].unsqueeze(2).broadcast_to((P, n, C)), ALU.mult, *toks)
            return f

        def scale_add(dst, src, C, *after):
            def f(m, h0, h1, c0, c1, p, den, toks):
                for h in range(h0, h1):
                    a = h * C + c0
                    o = (h - h0) * C
                    t = stt(dst[:, m, a:a + c1 - c0], p[:, o:o + c1 - c0], den[:, h:h + 1], src(m, slice(a, a + c1 - c0)),
                            ALU.mult, ALU.add, *toks, *after)
                return t
            return f

        def bcast2(row, n):
            return row.ap[:, 0:n].unsqueeze(1).broadcast_to((P, 2, n))

        def lin8(st, after, evac, us=range(3)):
            toks = []
            for u in us:
                bs = [bank(), bank()]
                for k in range(8):
                    j = (8 * u + k) % 3
                    if j == 0:
                        (w,) = st.get()
                        st.w = w
                    w = st.w
                    aft = [w.tok] if j == 0 else []
                    wh, wl = w.h[:, j * 256:(j + 1) * 256], w.l[:, j * 256:(j + 1) * 256]
                    for m in range(2):
                        ms = slice(m * P, (m + 1) * P)
                        pr_ = parts(False, wh, wl, (HSv[:, 0, k, ms], HSv[:, 1, k, ms]))
                        b = bs[m]
                        for q, pp in enumerate(pr_):
                            fn = lambda e, pp=pp, b=b, a=(k == 0 and q == 0), z=(k == 7 and q == 2): e.matmul(
                                b.t[:, 0:256], pp[0], pp[1], start=a, stop=z)
                            x = []
                            if q == 0:
                                x = aft + (list(b.free) if k == 0 else []) + (list(after[k]) if u == us[0] else [])
                            if q == 2 and (k == 7 or (m == 1 and j == 2)):
                                t = T.do(fn, *x)
                            else:
                                T.quiet(fn, *x)
                        if k == 7:
                            r = evac(m, u * 256, (u + 1) * 256, b.t[:, 0:256], t)
                            b.free = (r,)
                            toks.append(r)
                    if j == 2:
                        st.done([w], t)
            return toks

        def to_XS(lt, keep=False):
            ks = []

            def evac2(k, p, t):
                t = split(XSv[:, 0, k:k + 2, :], XSv[:, 1, k:k + 2, :], p, t)
                ks.extend([[t], [t]])
                return t
            to_T(xn3, KT, None, pair(lt), evac2=evac2)
            if not keep:
                return ks
            return ks, [tt(XT[:, k:k + 2, :], XSv[:, 0, k:k + 2, :], XSv[:, 1, k:k + 2, :], ALU.add, *ks[k], q=G)
                        for k in range(0, 6, 2)]

        lt = ln(x3, xn3, D, xt)
        warm(WARM[4])
        ks = to_XS(lt)
        xl = wk(0, m=2, f=1024)
        xlt, _ = gemm_N(st, 6, xs_split, [], lambda m, c0, c1, p, t: copy(xl[:, m, c0:c1], p, t), nn=1024, ks=ks)
        rT = wk(2048, k=8, n=256)
        rt = []


        def skip1(f0, f1):
            a, _ = gemm_T(st, f1, 6, xs_split, [],
                          lambda f, p, t: act(rT[:, f, :], p, ACT.Identity, t, bias=col("g1br1", f, 1)), f0=f0)
            rt.extend(a)

        rs, rd, rb = load_row("g1as1", 1024), load_row("g1ad1", 1024), load_row("g1b1", 1024)
        o1 = wk(4096, m=2, f=1024)
        ot, t = gat(4, 256, xl, xlt, rs, rd, C13, NM13, [c1t], 6144,
                    scale_add(o1, lambda m, c: rb.ap[:, c], 256, rb.tok), during=(lambda: skip1(0, 4), lambda: skip1(4, 8)),
                    ready=lambda m, h: [xlt[2 * (h // 2) + m]])
        rb.free = tuple(ot)
        lt = ln(o1, o1, 1024, ot)
        warm(WARM[3])
        h1T = wk(0, k=8, n=256)
        h1t = []
        pre = []

        def hidden1(k, p, t):
            for i in range(2):
                t = act(h1T[:, k + i, :], p[:, i, :], ACT.Relu, t, *ot, bias=col("g1be1", k + i, 1),
                        scale=col("g1g1", k + i, 1))
            pre.append(tt(h1T[:, k:k + 2, :], h1T[:, k:k + 2, :], rT[:, k:k + 2, :], ALU.add, t, *rt))
            return t

        to_T(o1, 8, None, lt, evac2=hidden1)
        for k in range(0, 8, 2):
            a = split(HSv[:, 0, k:k + 2, :], HSv[:, 1, k:k + 2, :], h1T[:, k:k + 2, :], pre[k // 2])
            h1t += [[a], [a]]
        xl = wk(2048, m=2, f=768)
        xlt = lin8(st, h1t, lambda m, c0, c1, p, t: copy(xl[:, m, c0:c1], p, t))
        r2 = []
        held = {}

        def skip2(us):
            r2.extend(lin8(st, h1t, lambda m, c0, c1, p, a: tt(
                x3[:, m, c0:c1], x3[:, m, c0:c1], p, ALU.add, a, *lt), us=us))
            if us[0] == 2:
                rb, rc = load_row("g1br2", 768), load_row("g1be2", 768)
                t = tt(x3, x3, bcast2(rb, 768), ALU.add, rb.tok, *r2, q=G)
                t = tt(x3, x3, bcast2(rc, 768), ALU.add, rc.tok, t, q=G)
                rb.free = rc.free = (t,)
                r2.append(t)

        rs, rd = load_row("g1as2", 768), load_row("g1ad2", 768)
        o1 = wk(3584, m=2, f=768)

        def late(m, c):
            return held["b"].ap[:, c]

        def skip2_and_rows():
            skip2(range(2, 3))
            held["b"], held["g"] = load_row("g1b2", 768), load_row("g1g2", 768)

        def last_evac(m, h0, h1, c0, c1, p, den, toks):
            return scale_add(o1, late, 768, held["b"].tok)(m, h0, h1, c0, c1, p, den, toks)

        ot, t = gat(1, 768, xl, xlt, rs, rd, C13, NM13, [c1t], 6144, last_evac,
                    during=(lambda: skip2(range(0, 2)), skip2_and_rows),
                    ready=lambda m, h: [xlt[2 * h + m]])
        held["b"].free = tuple(ot)
        rg = held["g"]
        ag, rr, t = ln_stats(o1, 768, ot)
        xt = []
        for m in range(2):
            a = stt(o1[:, m, :], o1[:, m, :], ag[:, m, 0:1], rg.ap[:, 0:768], ALU.subtract, ALU.mult, t, rg.tok)
            xt.append(xstat(m, 0, 768, stt(x3[:, m, :], o1[:, m, :], rr[:, m:m + 1], x3[:, m, :], ALU.mult, ALU.add,
                                           a, *r2)))
        rg.free = tuple(xt)

        lt8 = col("lt8").rearrange("p (e j) -> p e j", e=8)

        def top2(val, n, t):
            g = small(2 * n * n).rearrange("p (m e j) -> p m e j", m=2, e=n)
            q = small(2 * n * n).rearrange("p (m e j) -> p m e j", m=2, e=n)
            sel = small(2 * n).rearrange("p (m e) -> p m e", m=2)
            for m in range(2):
                vj = val[:, m, :].unsqueeze(1).broadcast_to((P, n, n))
                ve = val[:, m, :].unsqueeze(2).broadcast_to((P, n, n))
                a = tt(q[:, m, :, :], vj, ve, ALU.is_equal, t)
                a = tt(q[:, m, :, :], q[:, m, :, :], lt8[:, 0:n, 0:n], ALU.mult, a)
                b = tt(g[:, m, :, :], vj, ve, ALU.is_gt, t)
                b = tt(g[:, m, :, :], g[:, m, :, :], q[:, m, :, :], ALU.add, a, b)
                b = red(sel[:, m, :], g[:, m, :, :], ALU.add, b)
            return sel, ts(sel, sel, 2.0, None, ALU.is_lt, None, b)

        def gate_logits(wname, xT, xtt):
            b = bank()
            wvw = col(wname).rearrange("p (k e) -> p k e", k=6)
            for m in range(2):
                t = mm(b, b.t[:, 8 * m:8 * m + 8],
                       [(xT[:, k, m * P:(m + 1) * P], wvw[:, k, :]) for k in range(6)], xtt)
            return b, b.t[:, 0:16].rearrange("p (m e) -> p m e", m=2), t

        def softmax8(z, t):
            mx, sm = small(2), small(2)
            t = red(mx, z, ALU.max, t)
            t = tt(z, z, mx.unsqueeze(2).broadcast_to((P, 2, 8)), ALU.subtract, t)
            t = act(z, z, ACT.Exp, t)
            return sm, t

        def norm8(z, w, sm, t):
            t = red(sm, w, ALU.add, t)
            t = V.do(lambda e: e.reciprocal(sm, sm), t)
            return tt(z, z, sm.unsqueeze(2).broadcast_to((P, 2, 8)), ALU.mult, t)

        def comb_T(comb, n, t, at):
            b = bank()
            for m in range(2):
                t2 = mm(b, b.t[0:n, m * P:(m + 1) * P], [(comb[:, m, :], ident)], [t])
            o = XN[:, 0:256]
            r = V.do(lambda e: e.tensor_copy(o[0:n, :], b.t[0:n, 0:256]), t2)
            b.free = (r,)
            return o, r

        lt = ln(x3, xn3, D, xt, then=ACT.Gelu)
        warm(WARM[4])
        ks, xtt = to_XS(lt, keep=True)
        cbt = comb = None

        def route1():
            b, z, t = gate_logits("f1Wr", XT, xtt)
            lg = small(16).rearrange("p (m e) -> p m e", m=2)
            t = V.do(lambda e, z=z: e.tensor_copy(lg, z), t)
            b.free = (t,)
            sel, t = top2(lg, 8, t)
            sm, t = softmax8(lg, t)
            t = tt(lg, lg, sel, ALU.mult, t)
            cbt = norm8(lg, lg, sm, t)
            comb = lg
            return comb, cbt

        xt = [None] * 4

        def biases(comb, n, row):
            cT, cTt = comb_T(comb, n, cbt, 0)
            rb = load_row(row, 768, parts=n)
            for m in range(2):
                for ci, (c0, c1) in enumerate(((0, 512), (512, 768))):
                    b = bank()
                    t = mm(b, b.t[:, 0:c1 - c0], [(cT[0:n, m * P:(m + 1) * P], rb.ap[0:n, c0:c1])], [cTt, rb.tok])
                    xt[2 * m + ci] = tt(x3[:, m, c0:c1], x3[:, m, c0:c1], b.t[:, 0:c1 - c0], ALU.add, t, *lt)
                    b.free = (xt[2 * m + ci],)
            rb.free = (t,)

        gfree = [(), ()]
        pend = []

        def down(gt, comb, e, gi, last=False):
            idx = [0]

            def evac(m, c0, c1, p, t):
                i = 2 * m + (1 if c0 else 0)
                xv = x3[:, m, c0:c1]
                xt[i] = stt(xv, p, comb[:, m, e:e + 1], xv, ALU.mult, ALU.add, t, xt[i], cbt) if comb is not None \
                    else tt(xv, xv, p, ALU.add, t, xt[i])
                if last:
                    xstat(m, c0, c1, xt[i])
                return xt[i]
            G_ = GH[gi]
            _, t = gemm_N(st, 3, lambda k: (G_[:, 0, k, :], G_[:, 1, k, :]), gt, evac)
            gfree[gi] = (t,)

        for e in range(8):
            gt, _ = gemm_T(st, 3, 6, xs_split, [], gelu_split(e % 2, lambda k, e=e: col("f1bi", e * 3 + k, 1),
                                                              *gfree[e % 2]), ks=ks)
            if e == 0:
                comb, cbt = route1()
            if e == 1:
                biases(comb, 8, "f1bo")
            if pend:
                down(*pend.pop())
            pend.append((gt, comb, e, e % 2))
        down(*pend.pop(), last=True)
        xt0 = xt

        lt = ln(x3, xn3, D, xt0)
        warm(WARM[4])
        ks = to_XS(lt)
        xl = wk(0, m=2, f=1024)
        xlt, _ = gemm_N(st, 6, xs_split, [], lambda m, c0, c1, p, t: copy(xl[:, m, c0:c1], p, t, *xt0[:4]), nn=1024,
                        ks=ks)
        rs, rd, rb = load_row("g2as1", 1024), load_row("g2ad1", 1024), load_row("g2b1", 1024)
        o1 = wk(2048, m=2, f=1024)
        ot, t = gat(8, 128, xl, xlt, rs, rd, Cn3, NM3, [nmt], 6144,
                    scale_add(o1, lambda m, c: rb.ap[:, c], 128, rb.tok),
                    ready=lambda m, h: [xlt[2 * (h // 4) + m]])
        rb.free = tuple(ot)
        h1t = []

        def hidden2(k, p, t):
            a = act(HSv[:, 0, k:k + 2, :], p, ACT.Relu, t)
            a = stt(HSv[:, 1, k:k + 2, :], p, 0.0, HSv[:, 0, k:k + 2, :], ALU.max, ALU.subtract, a)
            h1t.extend([[a], [a]])
            return a

        to_T(o1, 8, None, ot, evac2=hidden2)
        xl = wk(0, m=2, f=768)
        xlt = lin8(st, h1t, lambda m, c0, c1, p, t: copy(xl[:, m, c0:c1], p, t, *ot))
        rs, rd, rb = load_row("g2as2", 768), load_row("g2ad2", 768), load_row("g2b2", 768)
        tx = tt(x3, x3, bcast2(rb, 768), ALU.add, rb.tok, *lt)
        rb.free = (tx,)
        x_add = scale_add(x3, lambda m, c: x3[:, m, c], 768, tx)
        xt0, t = gat(1, 768, xl, xlt, rs, rd, Cn3, NM3, [nmt], 6144,
                     lambda m, h0, h1, c0, c1, *a: xstat(m, c0, c1, x_add(m, h0, h1, c0, c1, *a)),
                     ready=lambda m, h: [xlt[2 * h + m]])

        lt = ln(x3, xn3, D, xt0)
        warm(WARM[4])
        ks, xtt = to_XS(lt, keep=True)

        def route2():
            b, z, t = gate_logits("f2gw", XT, xtt)
            sc = small(16).rearrange("p (m e) -> p m e", m=2)
            t = V.do(lambda e, z=z: e.tensor_copy(sc, z), t)
            b.free = (t,)
            sm, t = softmax8(sc, t)
            t = norm8(sc, sc, sm, t)
            sg = small(16).rearrange("p (m e) -> p m e", m=2)
            t = tt(sg, sc, col("f2gb").unsqueeze(1).broadcast_to((P, 2, 8)), ALU.add, t)
            gs = small(8).rearrange("p (m g) -> p m g", m=2)
            t = red(gs, sg.rearrange("p m (g a) -> p m g a", a=2), ALU.add, t)
            keep, t = top2(gs, 4, t)
            t = ts(keep, keep, 1.0, -BIG, ALU.subtract, ALU.mult, t)
            for m in range(2):
                t = tt(sg[:, m, :].rearrange("p (g a) -> p g a", a=2), sg[:, m, :].rearrange("p (g a) -> p g a", a=2),
                       keep[:, m, :].unsqueeze(2).broadcast_to((P, 4, 2)), ALU.add, t)
            sel, t = top2(sg, 8, t)
            comb9 = small(18).rearrange("p (m e) -> p m e", m=2)
            t = V.do(lambda e: e.memset(comb9[:, :, 8:9], 1.0), t)
            cbt = tt(comb9[:, :, 0:8], sc, sel, ALU.mult, t)
            return comb9, cbt

        xt[:] = [None] * 4
        hb = [wk(2304 * i, k=6, n=256) for i in range(2)]
        sb2 = [wk(2304 * i + 1536, k=3, n=256) for i in range(2)]
        gfree[:] = [(), ()]
        hfree = [(), ()]
        pend = []
        for e in range(9):
            i = e % 2
            b1 = (lambda f: col("f2Bs1", f, 1)) if e == 8 else (lambda f, e=e: col("f2B1", e * 6 + f, 1))
            b3 = (lambda f: col("f2Bs3", f, 1)) if e == 8 else (lambda f, e=e: col("f2B3", e * 6 + f, 1))
            H = hb[i]
            r1, _ = gemm_T(st, 6, 6, xs_split, [], lambda f, p, t: act(
                H[:, f, :], p, ACT.Identity, t, *hfree[i], bias=b1(f)), ks=ks)
            if e == 0:
                comb9, cbt = route2()
            if pend:
                down(*pend.pop())
            r3, _ = gemm_T(st, 6, 6, xs_split, [], lambda f, p, t: stt(
                H[:, f, :], p, b3(f), H[:, f, :], ALU.add, ALU.mult, t, r1[f]))
            hg, hl, sg_ = H[:, 0:3, :], H[:, 3:6, :], sb2[i]
            t = ts(hg, hg, 7.0, None, ALU.min, None, *r3)
            t1 = act(sg_, hg, ACT.Sigmoid, t, *hfree[i], scale=1.702)
            t = ts(hl, hl, 7.0, -7.0, ALU.min, ALU.max, *r3)
            t = V.do(lambda e_, hl=hl, hg=hg: e_.scalar_tensor_tensor(
                out=hl, in0=hl, scalar=1.0, in1=hg, op0=ALU.add, op1=ALU.mult), t, t1)
            t = tt(hl, hl, sg_, ALU.mult, t, t1)
            t = split(GH[i][:, 0, :, :], GH[i][:, 1, :, :], hl, t, *gfree[i])
            hfree[i] = (t,)
            if e == 0:
                biases(comb9, 9, "f2B2")
            pend.append(([t], comb9 if e < 8 else None, e, i))
        down(*pend.pop(), last=True)

        LA, LB = wk(14336, a=768), wk(15104, a=2304)
        L.dma(lambda e: e.dma_start(LA, dr["f3A"]), s_f, *xt)
        L.dma(lambda e: e.dma_start(LB, dr["f3B"]), s_f)
        ltok = (s_f, 32)
        lt = ln(x3, xn3, D, xt)
        warm(WARM[4])
        xtt = to_T(xn3, KT, XT, pair(lt))
        ft = wk(0, m=2, f=768)
        res = wk(1536, m=2, f=768)
        BD = col("g3BD")
        ftt = []
        rtt = []
        for m in range(2):
            for k in range(6):
                if k % 2 == 0:
                    b = bank()
                h = (k % 2) * 256
                t = mm(b, b.t[:, h:h + 256], [(XT[:, k, m * P:(m + 1) * P], BD)], [*xtt, ctok])
                if k % 2:
                    pv = b.t[:, :].rearrange("p (k a n) -> p k a n", k=2, a=2)
                    c0 = (k - 1) * P
                    fo = ft[:, m, c0:c0 + 256].rearrange("p (k n) -> p k n", k=2)
                    ro = res[:, m, c0:c0 + 256].rearrange("p (k n) -> p k n", k=2)
                    t1 = act(fo, pv[:, :, 0, :], ACT.Copy, t, *xt[:4])
                    t2 = V.do(lambda e, ro=ro, pv=pv: e.tensor_copy(ro, pv[:, :, 1, :]), t, t1, *xt[:4])
                    b.free = (t1, t2)
                    ftt.append(t1)
                    rtt.append(t2)
        rs, rd = load_row("g3al", 768), load_row("g3ar", 768)
        o1 = wk(3072, m=2, f=768)
        ot, t = gat(12, 64, ft, ftt, rs, rd, Cn3, NM3, [nmt], 4608, scale_evac(o1, 64))
        t = tt(o1, o1, res, ALU.add, *ot, *rtt)
        xt = [xstat(m, 0, 768, stt(x3[:, m, :], o1[:, m, :], 0.0, x3[:, m, :], ALU.max, ALU.add, t))
              for m in range(2)]

        st = Stream([("f3Wqkv", 0), ("f3Wqkv", 1), ("f3Wqkv", 2), ("f3Wp", None)], after=xt)
        st.prime()
        lt = ln(x3, xn3, D, xt)
        warm(WARM[4])
        ks, xtt = to_XS(lt, keep=True)
        bs = [bank() for _ in range(3)]
        def q_base(f):
            (w,) = st.get()
            b, h = bs[f // 2], (f % 2) * 256
            pr_ = [x for k in range(6) for x in parts(True, w.h[:, k * P:(k + 1) * P], w.l[:, k * P:(k + 1) * P],
                                                      xs_split(k))]
            for q, pp in enumerate(pr_):
                fn = lambda e, pp=pp, b=b, h=h, a=(q == 0 and f % 2 == 0): e.matmul(
                    b.t[:, h:h + 256], pp[0], pp[1], start=a, stop=False, skip_group_check=True)
                if q == 0:
                    T.quiet(fn, w.tok, *b.free, *(x for k in ks for x in k))
                elif q == len(pr_) - 1:
                    t3 = T.do(fn)
                else:
                    T.quiet(fn)
            st.done([w], t3)
        q_base(0)
        q_base(1)
        b, z, t = gate_logits("f3gw", XT, xtt)
        pr = small(16).rearrange("p (m e) -> p m e", m=2)
        t = tt(pr, z, col("f3gb").unsqueeze(1).broadcast_to((P, 2, 8)), ALU.add, t)
        b.free = (t,)
        sm, t = softmax8(pr, t)
        t = norm8(pr, pr, sm, t)
        sel, t = top2(pr, 8, t)
        t = tt(pr, pr, sel, ALU.mult, t)
        t = ts(pr, pr, 2.0, None, ALU.mult, None, t)
        A6 = [LA[:, k * P:(k + 1) * P] for k in range(6)]
        ad = wk(0, m=2, f=128)
        adt = []
        for m in range(2):
            b = bank()
            t2 = mm(b, b.t[:, 0:P], [(XT[:, k, m * P:(m + 1) * P], A6[k]) for k in range(6)], [*xtt, ltok])
            r = tt(ad[:, m, :].rearrange("p (n r) -> p n r", n=8),
                   b.t[:, 0:P].rearrange("p (n r) -> p n r", n=8),
                   pr[:, m, :].unsqueeze(2).broadcast_to((P, 8, 16)), ALU.mult, t2, t)
            b.free = (r,)
            adt.append(r)
        adT = wk(256, n=256)
        qA, kA = wk(512, k=6, n=256), wk(2048, k=6, n=256)
        vA = wk(3584, m=2, f=768)
        for f in range(2, 6):
            q_base(f)
        b = bank()
        for m in range(2):
            t2 = tr(b, b.t[:, m * P:(m + 1) * P], ad[:, m, :], (adt[m],))
        adTt = V.do(lambda e, b=b: e.tensor_copy(adT, b.t[:, 0:256]), t2)
        b.free = (adTt,)
        qk = []
        for f in range(6):
            b, h = bs[f // 2], (f % 2) * 256
            t3 = T.do(lambda e, b=b, h=h, f=f: e.matmul(b.t[:, h:h + 256], LB[:, f * P:(f + 1) * P], adT,
                                                        start=False, stop=True, skip_group_check=True),
                      adTt, ltok)
        for f in range(6):
            b, h = bs[f // 2], (f % 2) * 256
            r = act(qA[:, f, :], b.t[:, h:h + 256], ACT.Identity, t3, bias=col("f3bq", f, 1))
            b.free = (r,)
            qk.append(r)
        for f in range(6):
            (w,) = st.get()
            b = bank()
            pr_ = [x for k in range(6) for x in parts(True, w.h[:, k * P:(k + 1) * P], w.l[:, k * P:(k + 1) * P],
                                                      xs_split(k))]
            t = mm(b, b.t[:, 0:256], pr_ + [(LB[:, 768 + f * P:768 + (f + 1) * P], adT)], [w.tok])
            st.done([w], t)
            r = act(kA[:, f, :], b.t[:, 0:256], ACT.Identity, t, bias=col("f3bk", f, 1))
            b.free = (r,)
            qk.append(r)
        rb = load_row("f3bv", 768)
        vt, vlast = gemm_N(st, 6, xs_split, [],
                           lambda m, c0, c1, p, t: tt(vA[:, m, c0:c1], p, rb.ap[:, c0:c1], ALU.add, t, rb.tok),
                           more=lambda m, c0, c1: [(adT[:, m * P:(m + 1) * P], LB[:, 1536 + c0:1536 + c1])])
        rb.free = tuple(vt)
        ctt = attention(qA, kA, vA, [*qk, *vt], 5120, lambda k, p, t: to_split(k, p, t, vlast))
        rb = load_row("f3bp", 768)
        t = tt(x3, x3, bcast2(rb, 768), ALU.add, rb.tok, *lt)
        xt, t = gemm_N(st, 6, xs_split, ctt, lambda m, c0, c1, p, tk, t=t: tt(
            x3[:, m, c0:c1], x3[:, m, c0:c1], p, ALU.add, tk, t))
        L.dma(lambda e: e.dma_start(out.rearrange("(m p) f -> p m f", p=P), x3), s_out, *xt)
        L.quiet(lambda e: e.wait_ge(s_out, 16))

        block = ctx.enter_context(nc.Block())

        @block.sync
        def _(e):
            L.emit(e)

        @block.scalar
        def _(e):
            S.emit(e)

        @block.vector
        def _(e):
            V.emit(e)

        @block.gpsimd
        def _(e):
            G.emit(e)

        @block.tensor
        def _(e):
            T.emit(e)


def _lay(i):
    import numpy as np

    def W(w):
        k, n = w.shape
        return w.reshape(k // P, P, n).transpose(1, 0, 2).reshape(P, -1)

    def T6(w):
        k, n = w.shape
        return w.reshape(k // P, P, n // P, P).transpose(1, 2, 0, 3).reshape(P, -1)

    def T3(w):
        k, n = w.shape
        return w.reshape(k // P, P, n // 256, 256).transpose(1, 2, 0, 3).reshape(P, -1)

    def T8(w):
        return w.reshape(8, P, 3, 256).transpose(1, 2, 0, 3).reshape(P, -1)

    def two(a, b, n):
        a, b = (v.reshape(P, -1, n * TILE) for v in (a, b))
        return np.stack([a, b], 2).reshape(P, -1)

    def C(v):
        return np.asarray(v).reshape(-1, P).T

    def wide(v):
        v = np.asarray(v).reshape(-1)
        return np.broadcast_to(v, (P, v.size))

    a = {}
    i = {k: np.asarray(v) for k, v in i.items()}
    a["x"] = i["x"]
    a["edges"] = np.concatenate([i[k].reshape(P, NEDGE_T) for k in ("src", "dst", "edge_type_3")], 1)
    a["iota16"] = np.broadcast_to(np.arange(768, dtype=np.int16), (P, 768))
    a["queries"] = W(i["L0_gnn_query_embs"].reshape(512, D).T)
    for n in ("1", "2"):
        a["Wrel" + n] = np.stack([T6(w) for w in i["L0_gnn_W_rel" + n]])
        a["Wroot" + n] = T6(i["L0_gnn_W_root" + n])
    a["Wgh"], a["Wgq"] = T6(i["L0_gnn_Wg"][:, :D].T), T6(i["L0_gnn_Wg"][:, D:].T)
    a["Wqh"], a["Wqq"] = T6(i["L0_gnn_Wq"][:, :D].T), T6(i["L0_gnn_Wq"][:, D:].T)
    for n in "qkv":
        a["f0W" + n] = T6(i["L0_ffn_W" + n])
    a["f0Wom"] = two(T6(i["L0_ffn_Wo"]), T6(i["L0_ffn_Wm"]), 2)
    a["f0W12"] = np.concatenate([T6(i["L0_ffn_W1"]), T3(i["L0_ffn_W2"])], 1)
    a["f0bv"], a["f0bf2"] = i["L0_ffn_bv"], i["L0_ffn_bf2"]
    a["f0bom"] = np.stack([i["L0_ffn_bo"], i["L0_ffn_bm"]])
    for n in ("W1", "Wr1"):
        a["g1" + n] = T6(i["L1_gnn_" + n])
    for n in ("W2", "Wr2"):
        a["g1" + n] = T8(i["L1_gnn_" + n])
    for n, m in (("as1", "a_src1"), ("ad1", "a_dst1"), ("as2", "a_src2"), ("ad2", "a_dst2"), ("b1", "b1"),
                 ("b2", "b2"), ("g2", "g2"), ("be2", "be2"), ("br2", "br2")):
        a["g1" + n] = i["L1_gnn_" + m].reshape(-1)
    a["f1Wi"] = np.stack([T6(w.T) for w in i["L1_ffn_Wi"]])
    a["f1Wo"] = np.stack([T3(w.T) for w in i["L1_ffn_Wo"]])
    a["f1bo"] = i["L1_ffn_bo"]
    a["g2W1"] = T6(i["L2_gnn_W1"].T)
    a["g2W2"] = T8(i["L2_gnn_W2"].T)
    for n, m in (("as1", "att_src1"), ("ad1", "att_dst1"), ("as2", "att_src2"), ("ad2", "att_dst2"),
                 ("b1", "b1"), ("b2", "b2")):
        a["g2" + n] = i["L2_gnn_" + m].reshape(-1)

    def eo(w):
        return np.concatenate([w[..., ::2], w[..., 1::2]], -1)

    a["f2W1"] = np.stack([T6(eo(w)) for w in i["L2_ffn_W1"]])
    a["f2W3"] = np.stack([T6(eo(w)) for w in i["L2_ffn_W3"]])
    a["f2W2"] = np.stack([T3(w) for w in i["L2_ffn_W2"]])
    a["f2Ws1"], a["f2Ws3"] = T6(eo(i["L2_ffn_Ws1"])), T6(eo(i["L2_ffn_Ws3"]))
    a["f2Ws2"] = T3(i["L2_ffn_Ws2"])
    a["f2B2"] = np.concatenate([i["L2_ffn_B2"], i["L2_ffn_Bs2"][None]])
    a["g3al"], a["g3ar"] = i["L3_gnn_attn_l"].reshape(-1), i["L3_gnn_attn_r"].reshape(-1)
    a["f3A"] = W(i["L3_ffn_A"].reshape(128, D).T)
    a["f3B"] = i["L3_ffn_B_lora"].transpose(0, 2, 1).reshape(128, 3 * D)
    a["f3Wqkv"] = np.stack([T6(i["L3_ffn_W_qkv"][c * D:(c + 1) * D].T) for c in range(3)])
    a["f3bv"], a["f3bp"] = i["L3_ffn_b_qkv"][2 * D:], i["L3_ffn_b_proj"]
    a["f3Wp"] = T6(i["L3_ffn_W_proj"].T)
    BD = np.zeros((P, 256), np.float32)
    for s in range(2):
        BD[s * 64:(s + 1) * 64, s * 64:(s + 1) * 64] = i["L3_gnn_W"].T
        BD[s * 64:(s + 1) * 64, 128 + s * 64:128 + (s + 1) * 64] = i["L3_gnn_W_res"].T
    c = {
        "g0b1": C(i["L0_gnn_b1"]), "g0b2": C(i["L0_gnn_b2"]), "g0bg": C(i["L0_gnn_bg"]), "g0bq": C(i["L0_gnn_bq"]),
        "f0g1": C(i["L0_ffn_g1"]), "f0b1": C(i["L0_ffn_b1"]), "f0g2": C(i["L0_ffn_g2"]), "f0b2": C(i["L0_ffn_b2"]),
        "f0Wr": C(i["L0_ffn_Wr"]), "f0bq": C(i["L0_ffn_bq"]), "f0bk": C(i["L0_ffn_bk"]),
        "f0bf1": C(i["L0_ffn_bf1"]), "f0br": wide(i["L0_ffn_br"]),
        "g1g1": C(i["L1_gnn_g1"]), "g1be1": C(i["L1_gnn_be1"]), "g1br1": C(i["L1_gnn_br1"]),
        "f1bi": C(i["L1_ffn_bi"]), "f1Wr": W(i["L1_ffn_Wr"].T),
        "f2gw": W(i["L2_ffn_gate_w"].T), "f2gb": wide(i["L2_ffn_gate_b"]),
        "f2B1": C(eo(i["L2_ffn_B1"])), "f2B3": C(eo(i["L2_ffn_B3"])),
        "f2Bs1": C(eo(i["L2_ffn_Bs1"])), "f2Bs3": C(eo(i["L2_ffn_Bs3"])),
        "g3BD": BD, "f3bq": C(i["L3_ffn_b_qkv"][:D]), "f3bk": C(i["L3_ffn_b_qkv"][D:2 * D]),
        "f3gw": W(i["L3_ffn_W_gate"].T), "f3gb": wide(i["L3_ffn_b_gate"]),
        "ident": np.eye(P, dtype=np.float32), "iota": wide(np.arange(768, dtype=np.float32)),
        "pidx": np.arange(256, dtype=np.float32).reshape(2, P).T,
        "eps": np.full((P, 1), 1e-5, np.float32),
        "lt8": wide(np.tril(np.ones((8, 8), np.float32), -1)),
    }
    a["cols"] = np.concatenate([c[n] for n in COLS], 1).astype(np.float32)
    assert a["cols"].shape == (P, NCOL)
    return {k: np.ascontiguousarray(v) for k, v in a.items()}


def kernel(**inputs):
    import concourse.bacc as _bacc
    from concourse.bass_utils import run_bass_kernel_spmd as _run

    nc = _bacc.Bacc("TRN2", target_bir_lowering=False, num_devices=1)
    arrays = _lay(inputs)
    dr = {k: nc.dram_tensor(k + "_in", v.shape, mybir.dt.from_np(v.dtype), kind="ExternalInput").ap()
          for k, v in arrays.items()}
    out = nc.dram_tensor("out", (N, D), F32, kind="ExternalOutput").ap()
    build(nc, dr, out)
    r = _run(nc, [{k + "_in": v for k, v in arrays.items()}], core_ids=[0])
    return r.results[0]["out"]
```
